# Optimizing a Trainium2 kernel written in Bass

```python
import numpy as np
import jax
import jax.numpy as jnp

def _softmax(x, axis=-1):
    return jax.nn.softmax(x, axis=axis)

def _gelu(x):
    return jax.nn.gelu(x, approximate=True)

def _silu(x):
    return jax.nn.silu(x)

def _sigmoid(x):
    return jax.nn.sigmoid(x)

def _layernorm(x, axis=-1, eps=1e-05):
    m = jnp.mean(x, axis=axis, keepdims=True)
    v = jnp.var(x, axis=axis, keepdims=True)
    return (x - m) / jnp.sqrt(v + eps)

def _scatter_add(tgt, idx, src, axis=0):
    return tgt.at[idx].add(src)

def _segment_sum(src, seg, n):
    return jax.ops.segment_sum(src, seg, n)
kernel_name = 'mk_seq_postln_d2_jaxref_r8_eef2ee'

def setup_inputs(seed: int=0):
    np.random.seed(seed)
    _w = jnp.asarray

    def _L0_attn_setup():
        import jax, jax.numpy as jnp
        import numpy as np
        DIM = 128
        HEADS = 16
        HEAD_DIM = 64
        WINDOW = 64
        key = jax.random.key(seed)
        ks = jax.random.split(key, 9)
        s = lambda fan_in: 1.0 / np.sqrt(fan_in)
        x = jax.random.normal(ks[0], (2, 256, DIM), dtype=jnp.float32)
        W1 = jax.random.uniform(ks[1], (DIM, DIM), jnp.float32, -s(DIM), s(DIM))
        b1 = jax.random.uniform(ks[2], (DIM,), jnp.float32, -s(DIM), s(DIM))
        W2 = jax.random.uniform(ks[3], (DIM, DIM), jnp.float32, -s(DIM), s(DIM))
        b2 = jax.random.uniform(ks[4], (DIM,), jnp.float32, -s(DIM), s(DIM))
        Wg = jax.random.uniform(ks[5], (3 * HEADS * HEAD_DIM, DIM), jnp.float32, -s(DIM), s(DIM))
        bg = jax.random.uniform(ks[6], (3 * HEADS * HEAD_DIM,), jnp.float32, -s(DIM), s(DIM))
        Wo = jax.random.uniform(ks[7], (DIM, HEADS * HEAD_DIM), jnp.float32, -s(HEADS * HEAD_DIM), s(HEADS * HEAD_DIM))
        bo = jax.random.uniform(ks[8], (DIM,), jnp.float32, -s(HEADS * HEAD_DIM), s(HEADS * HEAD_DIM))
        return {'x': x, 'W1': W1, 'b1': b1, 'W2': W2, 'b2': b2, 'Wg': Wg, 'bg': bg, 'Wo': Wo, 'bo': bo}
    _L0_attn_in = _L0_attn_setup()

    def _L0_ffn_setup():
        import jax, jax.numpy as jnp
        import numpy as np
        B, L, D = (4, 64, 128)
        E, TOP_K = (16, 4)
        F = 4 * D
        key = jax.random.key(seed)
        ks = jax.random.split(key, 6)
        scale = 0.02
        return {'x': jax.random.normal(ks[0], (B, L, D), jnp.float32), 'keys': jax.random.normal(ks[1], (E, D), jnp.float32), 'w1': jax.random.normal(ks[2], (E, F, D), jnp.float32) * scale, 'b1': jnp.zeros((E, F), jnp.float32), 'w2': jax.random.normal(ks[3], (E, D, F), jnp.float32) * scale, 'b2': jnp.zeros((E, D), jnp.float32), 'rw': jax.random.normal(ks[4], (E, D), jnp.float32) * scale, 'rb': jnp.zeros((E,), jnp.float32)}
    _L0_ffn_in = _L0_ffn_setup()

    def _L1_attn_setup():
        import jax, jax.numpy as jnp
        import numpy as np
        DIM = 128
        HEADS = 16
        HEAD_DIM = DIM // HEADS
        RANK = 16
        LORA_ALPHA = 1
        SCALING = LORA_ALPHA / RANK
        SCALE = HEAD_DIM ** (-0.5)
        B, N = (8, 128)

        def _lora_linear(x, W, A, Blo, bias=None):
            y = x @ W.T + x @ A.T @ Blo.T * SCALING
            if bias is not None:
                y = y + bias
            return y

        def _split_heads(t, b, n):
            return t.reshape(b, n, HEADS, HEAD_DIM).transpose(0, 2, 1, 3)
        key = jax.random.key(seed)
        ks = jax.random.split(key, 15)
        s = 1.0 / np.sqrt(DIM)
        inp = {'x': jax.random.normal(ks[0], (B, N, DIM), jnp.float32), 'Wq': jax.random.normal(ks[1], (DIM, DIM), jnp.float32) * s, 'Wk': jax.random.normal(ks[2], (DIM, DIM), jnp.float32) * s, 'Wv': jax.random.normal(ks[3], (DIM, DIM), jnp.float32) * s, 'Wo': jax.random.normal(ks[4], (DIM, DIM), jnp.float32) * s, 'bo': jnp.zeros((DIM,), jnp.float32), 'Aq': jax.random.normal(ks[5], (RANK, DIM), jnp.float32) * s, 'Bq': jax.random.normal(ks[6], (DIM, RANK), jnp.float32) * s, 'Ak': jax.random.normal(ks[7], (RANK, DIM), jnp.float32) * s, 'Bk': jax.random.normal(ks[8], (DIM, RANK), jnp.float32) * s, 'Av': jax.random.normal(ks[9], (RANK, DIM), jnp.float32) * s, 'Bv': jax.random.normal(ks[10], (DIM, RANK), jnp.float32) * s, 'Ao': jax.random.normal(ks[11], (RANK, DIM), jnp.float32) * s, 'Bo': jax.random.normal(ks[12], (DIM, RANK), jnp.float32) * s}
        return inp
    _L1_attn_in = _L1_attn_setup()

    def _L1_ffn_setup():
        import jax, jax.numpy as jnp
        import numpy as np
        from jax import lax
        T, B, I, M, O = (32, 64, 128, 128, 128)

        def _xavier(key, shape):
            fan_out, fan_in = shape
            limit = float(np.sqrt(6.0 / (fan_in + fan_out)))
            return jax.random.uniform(key, shape, jnp.float32, -limit, limit)
        key = jax.random.key(seed)
        ks = jax.random.split(key, 9)
        x = jax.random.normal(ks[0], (T, B, I), jnp.float32)
        return {'x': x, 'wf': _xavier(ks[1], (M, I)), 'uf': _xavier(ks[2], (M, M)), 'bf': jnp.zeros((M,), jnp.float32), 'wi': _xavier(ks[3], (M, I)), 'ui': _xavier(ks[4], (M, M)), 'bi': jnp.zeros((M,), jnp.float32), 'wc': _xavier(ks[5], (M, I)), 'uc': _xavier(ks[6], (M, M)), 'bc': jnp.zeros((M,), jnp.float32), 'wo': _xavier(ks[7], (O, I)), 'uo': _xavier(ks[8], (O, M)), 'bo': jnp.zeros((O,), jnp.float32), 'in_c': jnp.zeros((M,), jnp.float32)}
    _L1_ffn_in = _L1_ffn_setup()
    _d = {'L0_attn_x': _L0_attn_in['x'], 'L0_attn_W1': _L0_attn_in['W1'], 'L0_attn_b1': _L0_attn_in['b1'], 'L0_attn_W2': _L0_attn_in['W2'], 'L0_attn_b2': _L0_attn_in['b2'], 'L0_attn_Wg': _L0_attn_in['Wg'], 'L0_attn_bg': _L0_attn_in['bg'], 'L0_attn_Wo': _L0_attn_in['Wo'], 'L0_attn_bo': _L0_attn_in['bo'], 'L0_ffn_keys': _L0_ffn_in['keys'], 'L0_ffn_w1': _L0_ffn_in['w1'], 'L0_ffn_b1': _L0_ffn_in['b1'], 'L0_ffn_w2': _L0_ffn_in['w2'], 'L0_ffn_b2': _L0_ffn_in['b2'], 'L0_ffn_rw': _L0_ffn_in['rw'], 'L0_ffn_rb': _L0_ffn_in['rb'], 'L1_attn_Wq': _L1_attn_in['Wq'], 'L1_attn_Wk': _L1_attn_in['Wk'], 'L1_attn_Wv': _L1_attn_in['Wv'], 'L1_attn_Wo': _L1_attn_in['Wo'], 'L1_attn_bo': _L1_attn_in['bo'], 'L1_attn_Aq': _L1_attn_in['Aq'], 'L1_attn_Bq': _L1_attn_in['Bq'], 'L1_attn_Ak': _L1_attn_in['Ak'], 'L1_attn_Bk': _L1_attn_in['Bk'], 'L1_attn_Av': _L1_attn_in['Av'], 'L1_attn_Bv': _L1_attn_in['Bv'], 'L1_attn_Ao': _L1_attn_in['Ao'], 'L1_attn_Bo': _L1_attn_in['Bo'], 'L1_ffn_wf': _L1_ffn_in['wf'], 'L1_ffn_uf': _L1_ffn_in['uf'], 'L1_ffn_bf': _L1_ffn_in['bf'], 'L1_ffn_wi': _L1_ffn_in['wi'], 'L1_ffn_ui': _L1_ffn_in['ui'], 'L1_ffn_bi': _L1_ffn_in['bi'], 'L1_ffn_wc': _L1_ffn_in['wc'], 'L1_ffn_uc': _L1_ffn_in['uc'], 'L1_ffn_bc': _L1_ffn_in['bc'], 'L1_ffn_wo': _L1_ffn_in['wo'], 'L1_ffn_uo': _L1_ffn_in['uo'], 'L1_ffn_bo': _L1_ffn_in['bo'], 'L1_ffn_in_c': _L1_ffn_in['in_c']}
    _x0 = _d['L0_attn_x']
    _d['L0_attn_x'] = jax.random.normal(jax.random.fold_in(jax.random.key(seed), 1), (16, 256, 128), dtype=_x0.dtype)
    del _x0
    return _d

def reference(L0_attn_x, L0_attn_W1, L0_attn_b1, L0_attn_W2, L0_attn_b2, L0_attn_Wg, L0_attn_bg, L0_attn_Wo, L0_attn_bo, L0_ffn_keys, L0_ffn_w1, L0_ffn_b1, L0_ffn_w2, L0_ffn_b2, L0_ffn_rw, L0_ffn_rb, L1_attn_Wq, L1_attn_Wk, L1_attn_Wv, L1_attn_Wo, L1_attn_bo, L1_attn_Aq, L1_attn_Bq, L1_attn_Ak, L1_attn_Bk, L1_attn_Av, L1_attn_Bv, L1_attn_Ao, L1_attn_Bo, L1_ffn_wf, L1_ffn_uf, L1_ffn_bf, L1_ffn_wi, L1_ffn_ui, L1_ffn_bi, L1_ffn_wc, L1_ffn_uc, L1_ffn_bc, L1_ffn_wo, L1_ffn_uo, L1_ffn_bo, L1_ffn_in_c):

    def _L0_attn_ref(x, W1, b1, W2, b2, Wg, bg, Wo, bo):
        import jax, jax.numpy as jnp
        import numpy as np
        DIM = 128
        HEADS = 16
        HEAD_DIM = 64
        WINDOW = 64
        b, n, _ = x.shape
        h = jax.nn.silu(x @ W1.T + b1) @ W2.T + b2
        qkv = h @ Wg.T + bg
        q, k, v = jnp.split(qkv, 3, axis=-1)
        reshape = lambda t: t.reshape(b, n, HEADS, HEAD_DIM).transpose(0, 2, 1, 3)
        q, k, v = (reshape(q), reshape(k), reshape(v))
        dots = jnp.einsum('bhid,bhjd->bhij', q, k) * HEAD_DIM ** (-0.5)
        i = jnp.arange(n)[:, None]
        j = jnp.arange(n)[None, :]
        mask = j >= i + WINDOW
        dots = jnp.where(mask, -jnp.inf, dots)
        attn = jax.nn.softmax(dots, axis=-1)
        out = jnp.einsum('bhij,bhjd->bhid', attn, v)
        out = out.transpose(0, 2, 1, 3).reshape(b, n, HEADS * HEAD_DIM)
        return out @ Wo.T + bo

    def _L0_ffn_ref(x, keys, w1, b1, w2, b2, rw, rb):
        import jax, jax.numpy as jnp
        import numpy as np
        B, L, D = (4, 64, 128)
        E, TOP_K = (16, 4)
        F = 4 * D
        diff = x[:, :, None, :] - keys
        dist2 = jnp.sum(diff * diff, axis=-1)
        logits = -dist2 + jnp.einsum('bld,ed->ble', x, rw) + rb
        topv, topi = jax.lax.top_k(logits, TOP_K)
        w = jax.nn.softmax(topv, axis=-1)
        hidden = jax.nn.gelu(jnp.einsum('bld,efd->blef', x, w1) + b1, approximate=False)
        exp_out = jnp.einsum('blef,edf->bled', hidden, w2) + b2
        sel = jnp.take_along_axis(exp_out, topi[..., None], axis=2)
        fused = jnp.sum(w[..., None] * sel, axis=2)
        return fused

    def _L1_attn_ref(x, Wq, Wk, Wv, Wo, bo, Aq, Bq, Ak, Bk, Av, Bv, Ao, Bo):
        import jax, jax.numpy as jnp
        import numpy as np
        DIM = 128
        HEADS = 16
        HEAD_DIM = DIM // HEADS
        RANK = 16
        LORA_ALPHA = 1
        SCALING = LORA_ALPHA / RANK
        SCALE = HEAD_DIM ** (-0.5)
        B, N = (8, 128)

        def _lora_linear(x, W, A, Blo, bias=None):
            y = x @ W.T + x @ A.T @ Blo.T * SCALING
            if bias is not None:
                y = y + bias
            return y

        def _split_heads(t, b, n):
            return t.reshape(b, n, HEADS, HEAD_DIM).transpose(0, 2, 1, 3)
        b, n, c = x.shape
        q = _split_heads(_lora_linear(x, Wq, Aq, Bq), b, n)
        k = _split_heads(_lora_linear(x, Wk, Ak, Bk), b, n)
        v = _split_heads(_lora_linear(x, Wv, Av, Bv), b, n)
        attn = jnp.einsum('bhnd,bhmd->bhnm', q, k) * SCALE
        attn = jax.nn.softmax(attn, axis=-1)
        out = jnp.einsum('bhnm,bhmd->bhnd', attn, v)
        out = out.transpose(0, 2, 1, 3).reshape(b, n, c)
        return _lora_linear(out, Wo, Ao, Bo, bias=bo)

    def _L1_ffn_ref(x, wf, uf, bf, wi, ui, bi, wc, uc, bc, wo, uo, bo, in_c):
        import jax, jax.numpy as jnp
        import numpy as np
        from jax import lax
        T, B, I, M, O = (32, 64, 128, 128, 128)

        def _xavier(key, shape):
            fan_out, fan_in = shape
            limit = float(np.sqrt(6.0 / (fan_in + fan_out)))
            return jax.random.uniform(key, shape, jnp.float32, -limit, limit)
        batch = x.shape[1]
        c0 = jnp.broadcast_to(in_c, (batch, in_c.shape[0]))

        def step(c, xt):
            ft = jax.nn.sigmoid(xt @ wf.T + c @ uf.T + bf)
            it = jax.nn.sigmoid(xt @ wi.T + c @ ui.T + bi)
            gt = jnp.tanh(xt @ wc.T + c @ uc.T + bc)
            c = ft * c + it * gt
            return (c, None)
        c_final, _ = lax.scan(step, c0, x)
        h = jnp.tanh(jnp.einsum('tbi,oi->tbo', x, wo) + c_final @ uo.T + bo)
        return h
    x = L0_attn_x
    x = _layernorm(x + _L0_attn_ref(x, L0_attn_W1, L0_attn_b1, L0_attn_W2, L0_attn_b2, L0_attn_Wg, L0_attn_bg, L0_attn_Wo, L0_attn_bo), axis=-1)
    x = _layernorm(x + _L0_ffn_ref(x, L0_ffn_keys, L0_ffn_w1, L0_ffn_b1, L0_ffn_w2, L0_ffn_b2, L0_ffn_rw, L0_ffn_rb), axis=-1)
    x = _layernorm(x + _L1_attn_ref(x, L1_attn_Wq, L1_attn_Wk, L1_attn_Wv, L1_attn_Wo, L1_attn_bo, L1_attn_Aq, L1_attn_Bq, L1_attn_Ak, L1_attn_Bk, L1_attn_Av, L1_attn_Bv, L1_attn_Ao, L1_attn_Bo), axis=-1)
    x = _layernorm(x + _L1_ffn_ref(x, L1_ffn_wf, L1_ffn_uf, L1_ffn_bf, L1_ffn_wi, L1_ffn_ui, L1_ffn_bi, L1_ffn_wc, L1_ffn_uc, L1_ffn_bc, L1_ffn_wo, L1_ffn_uo, L1_ffn_bo, L1_ffn_in_c), axis=-1)
    return x

_drawn_inputs = setup_inputs


def setup_inputs(seed=0):
    import zlib

    import numpy as np

    out = dict(_drawn_inputs(seed))
    spreads = {'L0_ffn_b1': (0.0, 0.304),
     'L0_ffn_b2': (0.0, 0.1),
     'L0_ffn_rb': (0.0, 0.8),
     'L1_attn_bo': (0.0, 0.1),
     'L1_ffn_bf': (0.0, 0.756),
     'L1_ffn_bi': (0.0, 0.672),
     'L1_ffn_bc': (0.0, 0.1),
     'L1_ffn_bo': (0.0, 0.1),
     'L1_ffn_in_c': (0.0, 0.8)}
    factors = {'L0_attn_W1': 8.0,
     'L0_attn_b1': 7.587,
     'L0_ffn_rw': 8.0,
     'L1_attn_Aq': 8.0,
     'L1_attn_Bq': 8.0,
     'L1_attn_Ak': 8.0,
     'L1_attn_Bk': 8.0,
     'L1_attn_Av': 8.0,
     'L1_attn_Bv': 8.0,
     'L1_attn_Ao': 8.0,
     'L1_attn_Bo': 8.0}
    for name, (base, spread) in spreads.items():
        noise = np.random.default_rng([zlib.crc32(name.encode()), seed]).standard_normal(out[name].shape)
        drawn = base * np.exp(spread * noise) if base else spread * noise
        out[name] = jnp.asarray(drawn.astype(out[name].dtype))
    for name, factor in factors.items():
        out[name] = (out[name] * factor).astype(out[name].dtype)
    return out
```

```python
import concourse.bass as bass
from concourse import mybir
from contextlib import ExitStack

DT = mybir.dt
fp32, bf16, i32, u32 = DT.float32, DT.bfloat16, DT.int32, DT.uint32
ACT = mybir.ActivationFunctionType
ALU = mybir.AluOpType

B, N, D = 16, 256, 128
TOK = B * N
TT = N // 128
H, DH = 16, 64
PAIRS = H // 2
WINDOW = 64
SCALE0 = DH ** -0.5
E, TOPK, F = 16, 4, 512
FC = F // 128
H1, DH1 = 16, 8
SCALE1 = DH1 ** -0.5
RANK, LORA = 16, 1.0 / 16
NPART = 3
MROW = 64
BIG = 1.0e30
EPS = 1e-5
GT = 256
CAP = TOK + GT
DUMMY = E * CAP
NT = (TOK * TOPK + E * (GT - 1)) // GT
NT += NT % 2
ROWS = DUMMY + GT
WA = F + FC
WB = FC * D + 1
WCOLS = WA + WB


def batch_loop(eng, front, end, back, body):
    for b in range(front):
        body(b)
    with eng.Fori(front, end) as b:
        body(b)
    for b in range(end, end + back):
        body(b)


class Tally:

    FULL = 1

    def __init__(self, offsets):
        self.offsets = offsets

    def before(self, b, k=0):
        if not isinstance(b, int):
            n = len(self.offsets)
            return n * b + (self.before(self.FULL) - n * self.FULL + k)
        done = [0 <= c + o < B for c in range(-3, b) for o in self.offsets]
        return sum(done) + sum(0 <= b + o < B for o in self.offsets[:k])


def attention_loop(eng, body):
    for b in range(-3, 1):
        body(b, b % 2)
    with eng.Fori(0, 6) as i:
        body(2 * i + 1, 1)
        body(2 * i + 2, 0)
    for b in range(13, B + 1):
        body(b, b % 2)


def layernorm(v, x, out, n, stat, mv, rstd, nhalf, t2, ready):
    for k in range(n):
        v.bn_stats(stat[:, k, :], x[:, k, :])
    v.drain()
    for k in range(n):
        v.bn_aggr(mv[:, k, :], stat[:, k, :])
    v.drain()
    inv_sqrt(v, rstd[:, 0:n], mv[:, 0:n, 1], nhalf[:, 0:n], t2[:, 0:n])
    ready()
    for k in range(n):
        last = v.tensor_scalar(out[:, k, :], x[:, k, :], mv[:, k, 0:1], rstd[:, k:k + 1], ALU.subtract, ALU.mult)
    return last


def inv_sqrt(v, y, var, nhalf, t2):
    v.tensor_scalar(nhalf, var, EPS, None, ALU.add)
    v.drain()
    v.tensor_scalar(t2.bitcast(i32), nhalf.bitcast(i32), 1, None, ALU.logical_shift_right)
    v.drain()
    v.tensor_scalar(y.bitcast(i32), t2.bitcast(i32), -1.0, float(0x5F3759DF), ALU.mult, ALU.add)
    v.tensor_scalar(nhalf, nhalf, -0.5, None, ALU.mult)
    v.drain()
    for _ in range(3):
        v.tensor_tensor(t2, y, y, ALU.mult)
        v.drain()
        v.tensor_tensor(t2, t2, nhalf, ALU.mult)
        v.drain()
        v.scalar_tensor_tensor(y, t2, 1.5, y, ALU.add, ALU.mult)
        v.drain()


def build(nc, t, out):
    ctx = ExitStack()
    with ctx:
        def sb(name, shape, dt=fp32, c=ctx):
            return c.enter_context(nc.sbuf_tensor(name, shape, dt))

        def sem(name):
            return ctx.enter_context(nc.semaphore(name))

        psum = ctx.enter_context(nc.psum_tensor("psum", [128, 8 * 512], fp32))
        bank = [psum[:, i * 512:(i + 1) * 512] for i in range(8)]

        ident = sb("ident", [128, 128])
        x_all = sb("x_all", [128, B * TT, D])
        wall = sb("wall", [128, E, WCOLS])
        posf_all = sb("posf_all", [128, B * TT * TOPK])
        pos_all = sb("pos_all", [128, B * TT * TOPK], u32)
        gate_all = sb("gate_all", [128, B, TT * TOPK])
        count = sb("count", [128, E])

        first_row = sb("first_row", [128, E])

        a = ExitStack()
        wg = sb("wg", [128, 3 * H * DH], c=a)
        wo = sb("wo", [128, PAIRS, D], c=a)
        w1 = sb("w1", [128, D], c=a)
        w2 = sb("w2", [128, D], c=a)
        cols = sb("cols", [128, 3 + 2 * PAIRS], c=a)
        bv = sb("bv", [128, H * DH], c=a)
        hT = sb("hT", [128, TOK], c=a)
        xT = sb("xT", [128, 2, 512], c=a)
        h1 = sb("h1", [128, 2, 512], c=a)
        hV = sb("hV", [128, N], c=a)
        qT = sb("qT", [128, PAIRS, N], c=a)
        kT = sb("kT", [128, PAIRS, 2, N], c=a)
        V = sb("V", [128, TT, H * DH], c=a)
        band = sb("band", [128, TT, N], c=a)
        shifted = sb("shifted", [128, 2, TT, 2, N], c=a)
        least = sb("least", [128, 2, 4], c=a)
        P = sb("P", [128, 2, TT, 2, N], c=a)
        rowsum = sb("rowsum", [128, 2, 4], c=a)
        rinv = sb("rinv", [128, 2, 4], c=a)
        PT = sb("PT", [128, 2, 2, 2 * N], c=a)
        OT = sb("OT", [128, 2, N], c=a)
        yT = sb("yT", [128, N], c=a)
        x1T = sb("x1T", [128, N], c=a)
        x1c = sb("x1c", [128, TT, D], c=a)
        res = sb("res", [128, TT, D], c=a)
        sqj = sb("sqj", [128, D], c=a)
        xsq = sb("xsq", [128, TT], c=a)
        st = sb("st", [128, TT, 6], c=a)
        mv = sb("mv", [128, TT, 2], c=a)
        rstd = sb("rstd", [128, TT], c=a)
        nhalf = sb("nhalf", [128, TT], c=a)
        t2 = sb("t2", [128, TT], c=a)
        keysT = sb("keysT", [128, E], c=a)
        rwT = sb("rwT", [128, E], c=a)
        rmat = sb("rmat", [128, E], c=a)
        ksq = sb("ksq", [128, E], c=a)
        rconst = sb("rconst", [128, E], c=a)
        ones = sb("ones", [128, 128], c=a)
        onesb = sb("onesb", [128, 128], bf16, c=a)
        tri = sb("tri", [128, 128], bf16, c=a)
        iota_e = sb("iota_e", [128, E], c=a)
        lg = sb("lg", [128, TT, E], c=a)
        top = sb("top", [128, TT, 8], c=a)
        topi = sb("topi", [128, TT, 8], u32, c=a)
        topif = sb("topif", [128, TT, 8], c=a)
        ntop = sb("ntop", [128, TT], c=a)
        wexp = sb("wexp", [128, TT, TOPK], c=a)
        wsum = sb("wsum", [128, TT], c=a)
        hot = sb("hot", [128, TT, TOPK, E], c=a)
        mask = sb("mask", [128, TT, E], bf16, c=a)
        chosen = sb("chosen", [128, TT, E], c=a)
        rank = sb("rank", [128, TT, E], c=a)
        junk = sb("junk", [128, TT * TOPK, E], c=a)
        posf = sb("posf", [128, TT * TOPK], c=a)
        pos = sb("pos", [128, TT * TOPK], u32, c=a)
        a.close()

        cnt_i = sb("cnt_i", [128, E], i32)
        ntile = sb("ntile", [128, E])
        ncum = sb("ncum", [128, E])
        tile_no = sb("tile_no", [128, 1])
        past = sb("past", [128, E])
        skip = sb("skip", [128, E])
        tile_e = sb("tile_e", [128, 1])
        tile_s = sb("tile_s", [128, 1])
        used = sb("used", [128, 1])
        plan2 = sb("plan2", [128, 2], i32)
        pad_at = sb("pad_at", [128, E], i32)
        plan = sb("plan", [1, 256], i32)
        xg = sb("xg", [128, 2, 2, D])
        xgT = sb("xgT", [128, 2, GT])
        wA = sb("wA", [128, 2, WA])
        wB = sb("wB", [128, 2, WB])
        hid = sb("hid", [128, 2, FC, GT])
        yTe = sb("yTe", [128, 2, GT])
        yrow = sb("yrow", [128, 2, 2, D])
        zrow = sb("zrow", [128, 2, D])

        shift_sum = sb("shift_sum", [128, B * TT * TOPK])
        cw = sb("cw", [128, 4, D])
        lora_a = sb("lora_a", [RANK, 4, D])
        lora_b = sb("lora_b", [RANK, 4, D])
        gw = sb("gw", [128, 4, D])
        gu = sb("gu", [128, 4, D])
        gcol = sb("gcol", [128, 4])
        bo1 = sb("bo1", [128, D])
        bo2 = sb("bo2", [128, D])
        identb = sb("identb", [128, 128], bf16)
        qst = sb("qst", [128, 2, H, N], bf16)
        kst = sb("kst", [128, 2, H, N], bf16)
        shift = qst[:, 0, :, :].rearrange("q h n -> q (h n)").bitcast(fp32).rearrange("q (n e) -> q n e", e=E)
        zst = sb("zst", [NPART, H // 2, N], bf16)
        v32 = sb("v32", [128, 2, TT, H, 32])
        spare = wall[:, :, :].rearrange("q e c -> q (e c)")
        xo_all = spare[:, 0:B * N].rearrange("q (t d) -> q t d", d=D)
        pc = spare[:, B * N:2 * B * N].rearrange("q (s h j n) -> q s h j n", s=4, h=2, j=TT)
        yk = sb("yk", [128, TT * TOPK, D])
        posc = sb("posc", [128, TT * TOPK], u32)
        gcur = sb("gcur", [128, TT * TOPK])
        res2 = sb("res2", [128, TT, D])
        acc = sb("acc", [128, TT, D])
        x2c = sb("x2c", [128, TT, D])
        x2T = sb("x2T", [128, 2, N])
        parts = sb("parts", [128, NPART, 2 * N], bf16)
        rest = sb("rest", [128, 2 * N])
        mx = sb("mx", [128, TT, H])
        mrest = sb("mrest", [128, TT, H])
        nmx = sb("nmx", [128, TT, NPART, H], bf16)
        mrow = sb("mrow", [NPART * H, N], bf16)
        oTc = sb("oTc", [128, N])
        dinv = sb("dinv", [128, TT, 4])
        otok = sb("otok", [128, TT, D])
        oT = sb("oT", [128, N])
        x3c = sb("x3c", [128, TT, D])
        x3T = sb("x3T", [128, N])
        c2 = sb("c2", [128, N])
        tf = sb("tf", [128, N])
        ti = sb("ti", [128, N])
        tg = sb("tg", [128, N])
        state = sb("state", [128, TT, D])
        st2 = sb("st2", [128, 8, 6])
        mv2 = sb("mv2", [128, 8, 2])
        rstd2 = sb("rstd2", [128, 8])
        nh2 = sb("nh2", [128, 8])
        u2 = sb("u2", [128, 8])

        UP = [psum[:, 0:1024], psum[:, 1024:2048]]
        TI, DN, TO = bank[4], bank[5], bank[6]
        S0, S1, PTA, PTB, OTB, J, Y, M = bank

        xs = nc.dram_tensor("xs", (ROWS, D), fp32, kind="Internal").ap()
        ys = nc.dram_tensor("ys", (NT * GT, D), fp32, kind="Internal").ap()
        qkd = nc.dram_tensor("qkd", (NPART, 128, 2 * N), bf16, kind="Internal").ap()
        md = nc.dram_tensor("md", (NPART, H1, N), bf16, kind="Internal").ap()
        plan_d = nc.dram_tensor("plan_d", (128, 2), i32, kind="Internal").ap()

        names = """w_in xT_in x_in cst cst2 went_on hA_mm hA_act hB_mm h_ready
            qk_mm q_ev k_ev v_mm v_ev hv_ready
            scores shifted_ready exps pn_ready pt_mm ptA_ev ptB_ev pv_mm ot_ev wo_mm yT_ev
            m_y x1c_ready m_x x1T_ready m_l mask_ready m_r pos_ready xsq_ready x1_kept scat exp_w top_ready
            ksq_ready rmat_ready a_done plan_ready zrow_ready plan_out plan_in pad_in
            xg_in0 xg_in1 tin_mm xgT_ready wA_ready wB_ready up_mm hid_ready dn_mm yTe_ready tout_mm yrow_ready ys_out
            cw_in lora_mm c_set st_full exps1 s_full max_done pv_full o_free misc_full misc_free a1_ready parts_ready
            qkd_out stk0 stk1 md_out m_in nm_ready x2_ready x2_kept x3_ready x3_kept gates_full gate_act scan_done
            yk_in comb_done posc_ready pos_all_ready state_mm state_ready h_pre h_act fin_ready out_done""".split()
        s = {n: sem(n) for n in names}

        def pair(b, p, off=0):
            return 8 * b + (p + off)

        def is_pair(b, p, off):
            return 0 <= 8 * b + p + off < 8 * B if isinstance(b, int) else True

        def is_batch(b, off):
            return 0 <= b + off < B if isinstance(b, int) else True

        def need(eng, name, n):
            if not isinstance(n, int) or n > 0:
                eng.wait_ge(s[name], n)

        def need_alone(eng, name, n):
            if not isinstance(n, int) or n > 0:
                eng.wait_ge(s[name], n)
                eng.sem_inc(s["went_on"], 1)

        def has(b, off):
            return 0 <= b + off < B if isinstance(b, int) else True

        PRODUCTS = [(0, 0), (0, 1), (0, 2), (1, 0), (1, 1), (2, 0)]
        NSTK = 2 * len(PRODUCTS) + 1
        QK, TO3, VP, TOT, TO0, WO, TM, TO1, TX3, TX2, TO2 = range(11)
        misc = Tally([2, -1, 1, -1, 0, -1, 1, 0, -1, 3, 0])
        TOS = [TO3, TO0, TO1, TO2]
        SB = [bank[0], bank[1]]
        ST = [psum[:, 1024:2048], psum[:, 2048:3072]]
        OB, MI = bank[6], bank[7]
        MIB = MI.bitcast(bf16)

        def quad(b, p):
            return (-1, 3) if p < 2 else (0, p // 2 - 1)

        def is_tile(i, p, off):
            return 0 <= 2 * i + p + off < NT if isinstance(i, int) else True

        block = ctx.enter_context(nc.Block())
        NCH = TOK // 512

        @block.sync
        def _(sp):
            for dst, src in ((w1, "w1T"), (w2, "w2T"), (cols, "colsA"), (wg, "wgT"), (wo, "woT"),
                             (keysT, "keysT"), (rwT, "rwT"), (ident, "ident"), (bv, "bvB"), (rconst, "rbB")):
                dst = dst[:, :, :] if len(dst.shape) == 3 else dst[:, :]
                sp.dma_start(dst, t[src]).then_inc(s["w_in"], 16)
            sp.dma_start(x_all[:, :, :], t["x"].rearrange("(n p) d -> p n d", p=128)).then_inc(s["x_in"], 16)
            sp.dma_start(wall[:, :, :], t["wall"]).then_inc(s["x_in"], 16)
            for c in range(NCH):
                if c >= 2:
                    sp.wait_ge(s["hA_mm"], c - 1)
                sp.dma_start(xT[:, c % 2, :], t["xT"][:, c * 512:(c + 1) * 512]).then_inc(s["xT_in"], 16)
                if c == 0:
                    sp.wait_ge(s["xT_in"], 16)
                else:
                    sp.wait_ge(s["xT_in"], 16 * c + 16)
            sp.wait_ge(s["a_done"], 4)
            for dst, src in ((cw, "cw"), (lora_a, "lora_a"), (lora_b, "lora_b"), (gw, "gw"), (gu, "gu"), (gcol, "gcol"),
                             (bo1, "bo1"), (bo2, "bo2")):
                dst = dst[:, :, :] if len(dst.shape) == 3 else dst[:, :]
                sp.dma_start(dst, t[src]).then_inc(s["cw_in"], 16)
            sp.wait_ge(s["plan_ready"], 1)
            sp.dma_start(plan_d, plan2[:, :]).then_inc(s["plan_out"], 16)
            sp.wait_ge(s["zrow_ready"], 1)
            for e in range(E + 1):
                at = sp.value_load(pad_at[0:1, e:e + 1], min_val=0, max_val=DUMMY) if e < E else DUMMY
                sp.dma_start(xs[bass.ds(at, GT), :].rearrange("(p a) d -> p a d", a=2), zrow[:, :, :]).then_inc(s["pad_in"], 16)
            sp.wait_ge(s["plan_out"], 16)
            sp.dma_start(plan[:, :], plan_d.rearrange("(o t) c -> o (t c)", o=1)).then_inc(s["plan_in"], 16)
            sp.wait_ge(s["plan_in"], 16)
            sp.wait_ge(s["pad_in"], 16 * (E + 1))

            def row_of(n):
                at = 2 * n + 1
                src = plan[0:1, at:at + 1] if isinstance(n, int) else plan[0:1, bass.ds(at, 1)]
                return sp.value_load(src, min_val=0, max_val=DUMMY)

            def load_rows(n, par):
                need_alone(sp, "tin_mm", n - 1)
                sp.dma_start(xg[:, par, :, :], xs[bass.ds(row_of(n), GT), :].rearrange("(p a) d -> p a d", a=2)).then_inc(s[f"xg_in{par}"], 16)

            load_rows(0, 0)
            load_rows(1, 1)

            def body(i):
                for p in range(2):
                    n = 2 * i + p
                    if is_tile(i, p, 2):
                        load_rows(n + 2, p)
                    if is_tile(i, p, -2):
                        need_alone(sp, "yrow_ready", n - 1)
                        need_alone(sp, "ys_out", 16 * n - 32)
                        sp.dma_start(ys[bass.ds((n - 2) * GT, GT), :].rearrange("(p a) d -> p a d", a=2), yrow[:, p, :, :]).then_inc(s["ys_out"], 16)

            batch_loop(sp, 1, NT // 2 - 1, 2, body)
            sp.wait_ge(s["ys_out"], 16 * NT)

            def attention(b, par):
                if has(b, 2):
                    need_alone(sp, "parts_ready", b + 3)
                    need_alone(sp, "stk1", 16 * NSTK * (b + 2))
                    sp.dma_start(qkd.rearrange("a r c -> r a c"), parts[:, :, :]).then_inc(s["qkd_out"], 16)
                    need_alone(sp, "qkd_out", 16 * (b + 3))
                    stack(b, par, 0)
                if has(b, 1):
                    need_alone(sp, "misc_free", misc.before(b, TM + 1))
                    need_alone(sp, "m_in", 16 * (b + 1))
                    sp.dma_start(md.rearrange("a h n -> (a h) n"), mrow[:, :]).then_inc(s["md_out"], 16)
                    need_alone(sp, "md_out", 16 * (b + 2))
                    need_alone(sp, "s_full", H1 * (b + 2))
                    sp.dma_start(qst[MROW:MROW + NPART, 1 - par, :, :], md).then_inc(s["m_in"], 16)
                if has(b, 2):
                    stack(b, par, 1)

            def stack(b, par, half):
                if has(b, 0):
                    need_alone(sp, "st_full", 8 * b + 4 * (half + 1))
                hs = slice(8 * half, 8 * half + 8)
                for n, (qa, ka) in enumerate(PRODUCTS):
                    for dst, part, c0 in ((qst, qa, 0), (kst, ka, N)):
                        sp.dma_start(dst[DH1 * n:DH1 * n + DH1, par, hs, :],
                                     qkd[part].rearrange("(h d) c -> d h c", d=DH1)[:, hs, c0:c0 + N]).then_inc(s[f"stk{half}"], 16)
                sp.dma_start(qst[MROW:MROW + NPART, par, hs, :], zst[:, :, :]).then_inc(s[f"stk{half}"], 16)

            sp.wait_ge(s["c_set"], 1)
            attention_loop(sp, attention)
            for c in range(B // 4):
                sp.wait_ge(s["fin_ready"], c + 1)
                sp.dma_start(out[c * 4 * N:(c + 1) * 4 * N, :].rearrange("(n p) d -> p n d", p=128), x_all[:, 8 * c:8 * c + 8, :]).then_inc(s["out_done"], 16)
            sp.wait_ge(s["out_done"], 16 * B // 4)

        @block.gpsimd
        def _(pool):
            g = nc.gpsimd
            g.memset(kT[:, :, :, :], 0.0).then_inc(s["cst2"], 1)
            g.memset(P[:, :, :, :, :], 0.0).then_inc(s["cst2"], 1)
            g.memset(band[:, :, :], 0.0).then_inc(s["cst"], 1)
            pool.wait_ge(s["cst"], 1)
            for it in range(TT):
                g.affine_select(out=band[:, it, :], in_=band[:, it, :], compare_op=ALU.is_ge, fill=-BIG,
                                base=WINDOW - 1 + 128 * it, pattern=[[-1, N]], channel_multiplier=1).then_inc(s["cst"], 1)
            g.memset(ones[:, :], 1.0).then_inc(s["cst"], 1)
            g.memset(onesb[:, :], 1.0).then_inc(s["cst"], 1)
            pool.wait_ge(s["cst"], 5)
            g.affine_select(out=tri[:, :], in_=onesb[:, :], compare_op=ALU.is_gt, fill=0.0, base=0,
                            pattern=[[1, 128]], channel_multiplier=-1).then_inc(s["cst"], 1)
            g.iota(iota_e[:, :], pattern=[[1, E]], base=0, channel_multiplier=0,
                   allow_small_or_imprecise_dtypes=True).then_inc(s["cst"], 1)
            g.iota(first_row[:, :], pattern=[[CAP // 16, E]], base=0, channel_multiplier=0,
                   allow_small_or_imprecise_dtypes=True).then_inc(s["cst"], 1)
            g.memset(count[:, :], 0.0).then_inc(s["cst"], 1)
            pool.wait_ge(s["h_ready"], NCH)
            g.tensor_copy(hV[:, :], hT[:, 0:N]).then_inc(s["hv_ready"], 1)

            def body(b):
                for p in range(8):
                    if p == 3 and is_batch(b, 1):
                        need(pool, "v_mm", 4 * b + 4)
                        g.tensor_copy(hV[:, :], hT[:, bass.ds((b + 1) * N, N)]).then_inc(s["hv_ready"], 1)
                    if p == 5 and is_batch(b, -1):
                        need(pool, "x1c_ready", b)
                        g.tensor_copy(x_all[:, bass.ds((b - 1) * TT, TT), :], x1c[:, :, :]).then_inc(s["x1_kept"], 1)
                    if p < 4 and is_batch(b, -2):
                        if p == 0:
                            need_alone(pool, "pos_ready", b - 1)
                        for k in (2 * p, 2 * p + 1):
                            nc.gpsimd.indirect_dma_start(
                                out=xs, out_offset=bass.IndirectOffsetOnAxis(pos[:, k:k + 1], 0),
                                in_=x1c[:, k // TOPK, :], in_offset=None).then_inc(s["scat"], 16)

            batch_loop(pool, 2, B - 1, 3, body)
            pool.wait_ge(s["scat"], 16 * B * TT * TOPK)
            g.drain().then_inc(s["a_done"], 1)
            pool.wait_ge(s["a_done"], 4)
            g.memset(zrow[:, :, :], 0.0).then_inc(s["zrow_ready"], 1)
            g.iota(tile_no[:, :], pattern=[[0, 1]], base=0, channel_multiplier=1,
                   allow_small_or_imprecise_dtypes=True).then_inc(s["zrow_ready"], 1)
            pool.wait_ge(s["ys_out"], 16 * NT)
            pool.wait_ge(s["pos_all_ready"], 1)

            def attention(b, par):
                for p in range(8):
                    if p < 4 and has(b, 3):
                        if p == 0:
                            g.tensor_copy(posc[:, :], pos_all[:, bass.ds((b + 3) * TT * TOPK, TT * TOPK)]).then_inc(s["posc_ready"], 1)
                            need_alone(pool, "posc_ready", b + 4)
                            need_alone(pool, "comb_done", b + 3)
                        for n in (2 * p, 2 * p + 1):
                            g.indirect_dma_start(out=yk[:, n, :], out_offset=None, in_=ys,
                                                 in_offset=bass.IndirectOffsetOnAxis(posc[:, n:n + 1], 0)).then_inc(s["yk_in"], 16)
                    if p == 5 and has(b, -1):
                        need(pool, "x3_ready", b)
                        g.tensor_copy(x_all[:, bass.ds((b - 1) * TT, TT), :], x3c[:, :, :]).then_inc(s["x3_kept"], 1)
                    if p == 6 and has(b, 3):
                        need(pool, "x2_ready", b + 4)
                        g.tensor_copy(x_all[:, bass.ds((b + 3) * TT, TT), :], x2c[:, :, :]).then_inc(s["x2_kept"], 1)

            attention_loop(pool, attention)

        @block.tensor
        def _(pe):
            mm = nc.tensor.matmul
            pe.wait_ge(s["w_in"], 160)
            pe.wait_ge(s["cst"], 5)
            pe.wait_ge(s["rmat_ready"], 1)
            mm(M[:, 0:E], ones[:, :], ksq[:, :], start=True, stop=True).then_inc(s["ksq_ready"], 1)
            for c in range(NCH + 1):
                if c < NCH:
                    pe.wait_ge(s["xT_in"], 16 * c + 16)
                    if c >= 2:
                        pe.wait_ge(s["hA_act"], c - 1)
                    mm(bank[c % 2][:, :], w1[:, :], xT[:, c % 2, :], start=True, stop=True).then_inc(s["hA_mm"], 1)
                if c >= 1:
                    pe.wait_ge(s["hA_act"], c)
                    if c >= 3:
                        pe.wait_ge(s["h_ready"], c - 2)
                    mm(bank[2 + c % 2][:, :], w2[:, :], h1[:, (c - 1) % 2, :], start=True, stop=True).then_inc(s["hB_mm"], 1)

            def qk(b, p, n, j):
                need(pe, "q_ev", n)
                need(pe, "k_ev", 2 * n)
                need(pe, "v_ev", j)
                c = n // 8 if isinstance(n, int) else (b if p == 0 else b + 1)
                r = (p + 7) % 8
                tok = hT[:, bass.ds(c * N, N)] if not isinstance(c, int) else hT[:, c * N:(c + 1) * N]
                mm(J[:, 0:N], wg[:, r * 128:(r + 1) * 128], tok, start=True, stop=True)
                mm(J[:, N:2 * N], wg[:, H * DH + r * 128:H * DH + (r + 1) * 128], tok, start=True, stop=True).then_inc(s["qk_mm"], 1)

            def vproj(nqk, nv, half, jt):
                need(pe, "q_ev", nqk)
                need(pe, "k_ev", 2 * nqk)
                need(pe, "v_ev", nv)
                c0 = 2 * H * DH + half * 512
                mm(J[:, :], hV[:, jt * 128:(jt + 1) * 128], wg[:, c0:c0 + 512], start=True, stop=True).then_inc(s["v_mm"], 1)

            pe.wait_ge(s["h_ready"], NCH)
            for n in range(7):
                qk(0, n + 1, n, 0)
            pe.wait_ge(s["hv_ready"], 1)
            for jt in range(TT):
                vproj(7, jt, 0, jt)

            def body(b):
                for p in range(8):
                    par, par1 = p % 2, (p - 1) % 2
                    if is_pair(b, p, 0):
                        need(pe, "q_ev", pair(b, p, 1))
                        need(pe, "k_ev", 2 * pair(b, p, 1))
                        for it, bk in ((0, S0), (1, S1)):
                            w = N - WINDOW if it == 0 else N
                            need(pe, "shifted_ready", 4 * pair(b, p) - 2 * (1 - it) if not isinstance(b, int) or 8 * b + p > 0 else 0)
                            mm(bk[:, 0:2 * w].rearrange("q (h j) -> q h j", h=2), qT[:, p, it * 128:(it + 1) * 128],
                               kT[:, p, :, 0:w], start=True, stop=True).then_inc(s["scores"], 1)
                    if is_pair(b, p, 7):
                        nv = 2 + 4 * b + (0, 0, 1, 2, 2, 2, 3, 4)[p]
                        qk(b, p, pair(b, p, 7), nv)
                    if is_pair(b, p, -1):
                        for h, bk, ev in ((0, PTA, "ptA_ev"), (1, PTB, "ptB_ev")):
                            need(pe, "pn_ready", 4 * pair(b, p) - 2 * (1 - h))
                            need(pe, ev, pair(b, p, -1))
                            for jt in range(TT):
                                for it in range(TT):
                                    c0 = (N if jt == 0 else 0) + it * 128
                                    last = nc.tensor.transpose(bk[:, c0:c0 + 128], P[:, par1, it, h, jt * 128:(jt + 1) * 128], ident[:, :])
                            last.then_inc(s["pt_mm"], 1)
                    if is_pair(b, p, -2):
                        r = (p - 2) % 8
                        need(pe, "ptA_ev", pair(b, p, -1))
                        need(pe, "ptB_ev", pair(b, p, -1))
                        need(pe, "ot_ev", pair(b, p, -2))
                        bb = b - 1 if p < 2 else b
                        need(pe, "v_ev", 4 * bb + (2 if r < 4 else 4))
                        for h in range(2):
                            mm(OTB[64 * h:64 * h + 64, 0:N], V[:, 0, r * 128 + 64 * h:r * 128 + 64 * h + 64], PT[:, par, h, N:2 * N], start=True, stop=False)
                        for h in range(2):
                            last = mm(OTB[64 * h:64 * h + 64, WINDOW:N], V[:, 1, r * 128 + 64 * h:r * 128 + 64 * h + 64], PT[:, par, h, WINDOW:N], start=False, stop=True)
                        last.then_inc(s["pv_mm"], 1)
                    if p in (1, 2) and is_batch(b, 0):
                        vproj(pair(b, p, 8) if is_pair(b, p, 7) else 8 * B, 4 * b + 2 + (p - 1), 1, p - 1)
                    if p in (5, 6) and is_batch(b, 1):
                        if p == 5:
                            need(pe, "hv_ready", b + 2)
                        vproj(pair(b, p, 8) if is_pair(b, p, 7) else 8 * B, 4 * b + 4 + (p - 5), 0, p - 5)
                    if is_pair(b, p, -3):
                        r = (p - 3) % 8
                        need(pe, "ot_ev", pair(b, p, -2))
                        if r == 0:
                            need(pe, "yT_ev", b)
                        mm(Y[:, 0:N], wo[:, r, :], OT[:, par1, :], start=(r == 0), stop=(r == 7)).then_inc(s["wo_mm"], 1)
                    if is_batch(b, -1):
                        if p == 3:
                            need(pe, "yT_ev", b)
                            need(pe, "pos_ready", b - 1)
                            for it in range(TT):
                                last = nc.tensor.transpose(M[:, it * D:(it + 1) * D], yT[:, it * 128:(it + 1) * 128], ident[:, :])
                            last.then_inc(s["m_y"], 1)
                        if p == 4:
                            need(pe, "x1c_ready", b)
                            for it in range(TT):
                                last = nc.tensor.transpose(M[:, it * 128:(it + 1) * 128], x1c[:, it, :], ident[:, :])
                            last.then_inc(s["m_x"], 1)
                        if p == 5:
                            need(pe, "x1T_ready", b)
                            for it in range(TT):
                                last = mm(M[:, it * E:(it + 1) * E], x1T[:, it * 128:(it + 1) * 128], rmat[:, :], start=True, stop=True)
                            last.then_inc(s["m_l"], 1)
                        if p == 6:
                            need(pe, "mask_ready", b)
                            mm(M[:, 0:E], tri[:, :], mask[:, 0, :], start=True, stop=True)
                            mm(M[:, E:2 * E], tri[:, :], mask[:, 1, :], start=True, stop=False)
                            mm(M[:, E:2 * E], onesb[:, :], mask[:, 0, :], start=False, stop=True)
                            mm(M[:, 2 * E:3 * E], onesb[:, :], mask[:, 0, :], start=True, stop=False)
                            mm(M[:, 2 * E:3 * E], onesb[:, :], mask[:, 1, :], start=False, stop=True).then_inc(s["m_r"], 1)

            batch_loop(pe, 1, B - 1, 2, body)
            pe.drain().then_inc(s["a_done"], 1)
            pe.wait_ge(s["a_done"], 4)

            def rows_in(n, par, loads):
                need(pe, f"xg_in{par}", loads)
                need(pe, "xgT_ready", n)
                for k in range(2):
                    last = nc.tensor.transpose(TI[:, k * 128:(k + 1) * 128], xg[:, par, k, :], ident[:, :])
                last.then_inc(s["tin_mm"], 1)

            rows_in(0, 0, 16)

            def tiles(i):
                for p in range(2):
                    n, q = 2 * i + p, 1 - p
                    if is_tile(i, p, 0):
                        need(pe, "xgT_ready", n + 1)
                        need(pe, "wA_ready", n + 1)
                        need(pe, "hid_ready", 4 * n - 4)
                        for f in range(FC):
                            mm(UP[p][:, f * GT:(f + 1) * GT], wA[:, p, f * 128:(f + 1) * 128], xgT[:, p, :], start=True, stop=True).then_inc(s["up_mm"], 1)
                    if is_tile(i, p, 1):
                        rows_in(n + 1, q, 16 * i + 16 * (p + 1))
                    if is_tile(i, p, -1):
                        need(pe, "hid_ready", 4 * n)
                        need(pe, "wB_ready", n)
                        need(pe, "yTe_ready", n - 1)
                        for f in range(FC):
                            last = mm(DN[:, 0:GT], wB[:, q, f * D:(f + 1) * D], hid[:, q, f, :], start=(f == 0), stop=(f == FC - 1))
                        last.then_inc(s["dn_mm"], 1)
                    if is_tile(i, p, -2):
                        need(pe, "yTe_ready", n - 1)
                        need(pe, "yrow_ready", n - 2)
                        for k in range(2):
                            last = nc.tensor.transpose(TO[:, k * D:(k + 1) * D], yTe[:, p, k * 128:(k + 1) * 128], ident[:, :])
                        last.then_inc(s["tout_mm"], 1)

            batch_loop(pe, 1, NT // 2 - 1, 2, tiles)

            pe.wait_ge(s["cw_in"], 128)
            for k in range(4):
                last = mm(MI[:, k * D:(k + 1) * D], lora_a[:, k, :], lora_b[:, k, :], start=True, stop=True)
            last.then_inc(s["lora_mm"], 1)
            pe.wait_ge(s["c_set"], 1)

            def use_misc(b, k):
                need(pe, "misc_free", misc.before(b, k))

            def attention(b, par):
                for p in range(8):
                    if has(b, 0):
                        if p == 0:
                            need(pe, "m_in", 16 * b + 16)
                        need(pe, "exps1", 8 * b + (p - 1))
                        for k in range(2):
                            for jt in range(TT):
                                last = mm(ST[p % 2][:, (2 * k + jt) * N:(2 * k + jt + 1) * N], kst[:, par, 2 * p + k, jt * 128:(jt + 1) * 128],
                                          qst[:, par, 2 * p + k, :], start=True, stop=True)
                        last.then_inc(s["st_full"], 1)
                    if has(b, 1) and p < 4:
                        if p == 0:
                            need(pe, "stk0", 16 * NSTK * (b + 2))
                            need(pe, "gate_act", b - 1)
                        if p == 2:
                            need(pe, "stk1", 16 * NSTK * (b + 2))
                        for k in range(4):
                            need(pe, "max_done", H1 * (b + 1) + (4 * p + k - 1))
                            for it in range(TT):
                                last = mm(SB[k % 2][:, it * N:(it + 1) * N], qst[:, 1 - par, 4 * p + k, it * 128:(it + 1) * 128],
                                          kst[:, 1 - par, 4 * p + k, :], start=True, stop=True)
                            last.then_inc(s["s_full"], 1)
                    off, j = quad(b, p)
                    if p % 2 == 0 and has(b, off):
                        need(pe, "exps1", 8 * b + p)
                        need(pe, "o_free", 4 * b + (p // 2 - 1))
                        vpar = par if off == 0 else 1 - par
                        for jt in range(TT):
                            for r in range(4):
                                hd = 4 * j + r
                                last = mm(OB[32 * r:32 * r + 32, 0:N], v32[:, vpar, jt, hd, :], pc[:, hd // 2 % 4, r % 2, jt, :],
                                          start=(jt == 0), stop=(jt == TT - 1))
                        last.then_inc(s["pv_full"], 1)
                    if p % 2 == 1 and has(b, off):
                        use_misc(b, TOS[(p - 1) // 2])
                        need(pe, "o_free", 4 * b + (p - 1) // 2)
                        for it in range(TT):
                            last = nc.tensor.transpose(MI[:, it * 128:(it + 1) * 128], oTc[:, it * 128:(it + 1) * 128], ident[:, :])
                        last.then_inc(s["misc_full"], 1)
                    if p == 0 and has(b, 2):
                        use_misc(b, QK)
                        mm(MI[:, 0:N], cw[:, 0, :], x2T[:, par, :], start=True, stop=True)
                        mm(MI[:, N:2 * N], cw[:, 1, :], x2T[:, par, :], start=True, stop=True).then_inc(s["misc_full"], 1)
                    if p == 1 and has(b, 1):
                        use_misc(b, VP)
                        for jt in range(TT):
                            last = mm(MI[:, jt * D:(jt + 1) * D], x2T[:, 1 - par, jt * 128:(jt + 1) * 128], cw[:, 2, :], start=True, stop=True)
                        last.then_inc(s["misc_full"], 1)
                    if p == 2 and has(b, -1):
                        use_misc(b, TOT)
                        for it in range(TT):
                            last = nc.tensor.transpose(MI[:, it * 128:(it + 1) * 128], otok[:, it, :], ident[:, :])
                        last.then_inc(s["misc_full"], 1)
                    if p == 3 and has(b, -1):
                        use_misc(b, WO)
                        for it in range(TT):
                            last = mm(MI[:, it * D:(it + 1) * D], oT[:, it * 128:(it + 1) * 128], cw[:, 3, :], start=True, stop=True)
                        last.then_inc(s["misc_full"], 1)
                    if p == 4 and has(b, 1):
                        use_misc(b, TM)
                        need_alone(pe, "nm_ready", b + 2)
                        for it in range(TT):
                            last = nc.tensor.transpose(MIB[0:NPART * H1, it * 128:(it + 1) * 128], nmx[:, it, :, :].rearrange("q a h -> q (a h)"), identb[:, :])
                        last.then_inc(s["misc_full"], 1)
                    if p == 5 and has(b, -1):
                        use_misc(b, TX3)
                        need(pe, "x3_ready", b)
                        for it in range(TT):
                            last = nc.tensor.transpose(MI[:, it * 128:(it + 1) * 128], x3c[:, it, :], ident[:, :])
                        last.then_inc(s["misc_full"], 1)
                    if p == 6 and has(b, -1):
                        need(pe, "misc_free", misc.before(b, TX3 + 1))
                        need(pe, "scan_done", b)
                        if has(b, 1):
                            need(pe, "max_done", H1 * (b + 2))
                        for k, dst in enumerate((SB[0][:, 0:N], SB[0][:, N:2 * N], SB[1][:, 0:N])):
                            mm(dst, gw[:, k, :], x3T[:, :], start=True, stop=False)
                            mm(dst, gu[:, k, :], c2[:, :], start=False, stop=True)
                        for it in range(TT):
                            last = mm(SB[1][:, N + it * D:N + (it + 1) * D], x3T[:, it * 128:(it + 1) * 128], gw[:, 3, :], start=True, stop=True)
                        last.then_inc(s["gates_full"], 1)
                    if p == 6 and has(b, 3):
                        use_misc(b, TX2)
                        need(pe, "x2_ready", b + 4)
                        for it in range(TT):
                            last = nc.tensor.transpose(MI[:, it * 128:(it + 1) * 128], x2c[:, it, :], ident[:, :])
                        last.then_inc(s["misc_full"], 1)

            attention_loop(pe, attention)
            pe.wait_ge(s["scan_done"], B + 1)
            for it in range(TT):
                last = mm(SB[0][:, it * D:(it + 1) * D], c2[:, it * 128:(it + 1) * 128], gu[:, 3, :], start=True, stop=True)
            last.then_inc(s["state_mm"], 1)

        @block.scalar
        def _(act):
            sc = nc.scalar
            act.wait_ge(s["w_in"], 160)
            for c in range(NCH + 1):
                if c < NCH:
                    act.wait_ge(s["hA_mm"], c + 1)
                    if c >= 2:
                        act.wait_ge(s["hB_mm"], c - 1)
                    sc.activation(h1[:, c % 2, :], bank[c % 2][:, :], ACT.Silu, bias=cols[:, 0:1]).then_inc(s["hA_act"], 1)
                if c >= 1:
                    act.wait_ge(s["hB_mm"], c)
                    sc.activation(hT[:, (c - 1) * 512:c * 512], bank[2 + c % 2][:, :], ACT.Identity, bias=cols[:, 1:2]).then_inc(s["h_ready"], 1)

            act.wait_ge(s["cst2"], 2)

            def qk_evac(b, p, n):
                r = (p + 7) % 8
                need(act, "qk_mm", n + 1)
                sc.activation(qT[:, r, :], J[:, 0:N], ACT.Identity, bias=cols[:, 3 + r:4 + r]).then_inc(s["q_ev"], 1)
                for h in range(2):
                    sc.activation(kT[64 * h:64 * h + 64, r, h, :], J[64 * h:64 * h + 64, N:2 * N], ACT.Identity,
                                  bias=cols[64 * h:64 * h + 64, 3 + PAIRS + r:4 + PAIRS + r]).then_inc(s["k_ev"], 1)

            for n in range(7):
                qk_evac(0, n + 1, n)

            def body(b):
                for p in range(8):
                    par, par1 = p % 2, (p - 1) % 2
                    if p == 3 and is_batch(b, -1):
                        need(act, "wo_mm", 8 * b)
                        need(act, "m_y", b - 1)
                        sc.activation(yT[:, :], Y[:, 0:N], ACT.Identity, bias=cols[:, 2:3]).then_inc(s["yT_ev"], 1)
                    if p == 5 and is_batch(b, -1):
                        need(act, "m_x", b)
                        sc.activation(x1T[:, :], M[:, 0:N], ACT.Copy).then_inc(s["x1T_ready"], 1)
                        for it in range(TT):
                            sc.activation(sqj[:, :], x1c[:, it, :], ACT.Square, accum_out=xsq[:, it:it + 1]).then_inc(s["xsq_ready"], 1)
                            need(act, "xsq_ready", 2 * b - 1 + it)
                    if is_pair(b, p, 0):
                        need(act, "pt_mm", 2 * pair(b, p) - 2 if not isinstance(b, int) or 8 * b + p > 1 else 0)
                        for it in range(TT):
                            for h in range(2):
                                n = 2 * h + it
                                w = N - WINDOW if it == 0 else N
                                need(act, "shifted_ready", 4 * pair(b, p) + (2 * it + h + 1))
                                last = sc.activation(P[:, par, it, h, 0:w], shifted[:, par, it, h, 0:w], ACT.Exp, scale=-1.0,
                                                     bias=least[:, par, n:n + 1], accum_out=rowsum[:, par, n:n + 1])
                        last.then_inc(s["exps"], 1)
                    if is_pair(b, p, 7):
                        qk_evac(b, p, pair(b, p, 7))
                    if is_pair(b, p, -1):
                        need(act, "pt_mm", 2 * pair(b, p))
                        need(act, "pv_mm", pair(b, p, -2))
                        sc.activation(PT[:, par1, 1, WINDOW:2 * N], PTB[:, WINDOW:2 * N], ACT.Copy).then_inc(s["ptB_ev"], 1)
                    if is_pair(b, p, -2):
                        need(act, "pv_mm", pair(b, p, -1))
                        need(act, "wo_mm", pair(b, p, -3))
                        sc.activation(OT[:, par, :], OTB[:, 0:N], ACT.Copy).then_inc(s["ot_ev"], 1)
                    if p == 7 and is_batch(b, -1):
                        need(act, "top_ready", b)
                        for it in range(TT):
                            last = sc.activation(wexp[:, it, :], top[:, it, 0:TOPK], ACT.Exp, bias=ntop[:, it:it + 1], accum_out=wsum[:, it:it + 1])
                        last.then_inc(s["exp_w"], 1)

            batch_loop(act, 1, B - 1, 2, body)
            act.drain().then_inc(s["a_done"], 1)
            act.wait_ge(s["a_done"], 4)

            def tiles(i):
                for p in range(2):
                    n, q = 2 * i + p, 1 - p
                    if is_tile(i, p, 0):
                        need(act, "dn_mm", n - 1)
                        for f in range(FC):
                            need(act, "up_mm", 4 * n + (2 * (f // 2) + 2))
                            sc.activation(hid[:, p, f, :], UP[p][:, f * GT:(f + 1) * GT], ACT.Gelu, bias=wA[:, p, F + f:F + f + 1]).then_inc(s["hid_ready"], 1)
                    if is_tile(i, p, -1):
                        need(act, "dn_mm", n)
                        need(act, "tout_mm", n - 2)
                        sc.activation(yTe[:, q, :], DN[:, 0:GT], ACT.Identity, bias=wB[:, q, FC * D:FC * D + 1]).then_inc(s["yTe_ready"], 1)

            batch_loop(act, 1, NT // 2 - 1, 2, tiles)

            def attention(b, par):
                for p in range(8):
                    off, j = quad(b, p)
                    if has(b, 0):
                        need(act, "st_full", 8 * b + p + 1)
                        need(act, "pv_full", 4 * b + (p // 2 - 1))
                        sc.activation(pc[:, p % 4, :, :, :].rearrange("q h j n -> q (h j n)"), ST[p % 2], ACT.Exp, scale=SCALE1).then_inc(s["exps1"], 1)
                    if p % 2 == 0 and has(b, off):
                        need(act, "pv_full", 4 * b + p // 2)
                        if p > 0 and (p > 2 or has(b, -1)):
                            need(act, "misc_full", misc.before(b, TOS[p // 2 - 1] + 1))
                        if p == 0:
                            need(act, "misc_full", misc.before(b))
                        sc.activation(oTc[:, :], OB[:, 0:N], ACT.Copy).then_inc(s["o_free"], 1)
                    if p == 0 and has(b, 2):
                        need(act, "misc_full", misc.before(b, QK + 1))
                        need(act, "qkd_out", 16 * (b + 2))
                        sc.activation(parts[:, 0, :], MI[:, :], ACT.Copy).then_inc(s["a1_ready"], 1)
                    if p == 2 and has(b, -1):
                        need(act, "misc_full", misc.before(b, TOT + 1))
                        sc.activation(oT[:, :], MI[:, 0:N], ACT.Copy).then_inc(s["misc_free"], 1)
                    if p == 4 and has(b, 1):
                        need(act, "misc_full", misc.before(b, TM + 1))
                        need(act, "md_out", 16 * (b + 1))
                        sc.activation(mrow[:, :], MIB[0:NPART * H1, 0:N], ACT.Copy).then_inc(s["misc_free"], 1)
                    if p == 5 and has(b, -1):
                        need(act, "misc_full", misc.before(b, TX3 + 1))
                        sc.activation(x3T[:, :], MI[:, 0:N], ACT.Copy).then_inc(s["misc_free"], 1)
                    if p == 6 and has(b, -1):
                        need(act, "gates_full", b)
                        sc.activation(tf[:, :], SB[0][:, 0:N], ACT.Tanh, bias=gcol[:, 0:1], scale=0.5)
                        sc.activation(ti[:, :], SB[0][:, N:2 * N], ACT.Tanh, bias=gcol[:, 1:2], scale=0.5)
                        sc.activation(tg[:, :], SB[1][:, 0:N], ACT.Tanh, bias=gcol[:, 2:3])
                        sc.activation(xo_all[:, bass.ds((b - 1) * TT, TT), :].rearrange("q i d -> q (i d)"), SB[1][:, N:2 * N], ACT.Copy).then_inc(s["gate_act"], 1)
                    if p == 7 and has(b, 3):
                        need(act, "misc_full", misc.before(b, TX2 + 1))
                        sc.activation(x2T[:, 1 - par, :], MI[:, 0:N], ACT.Copy).then_inc(s["misc_free"], 1)

            attention_loop(act, attention)
            for c in range(B // 4):
                act.wait_ge(s["h_pre"], c + 1)
                sc.activation(xo_all[:, 8 * c:8 * c + 8, :], xo_all[:, 8 * c:8 * c + 8, :], ACT.Tanh).then_inc(s["h_act"], 1)

        @block.vector
        def _(dve):
            v = nc.vector
            dve.wait_ge(s["w_in"], 160)
            v.tensor_tensor(ksq[:, :], keysT[:, :], keysT[:, :], ALU.mult)
            v.scalar_tensor_tensor(rmat[:, :], keysT[:, :], 2.0, rwT[:, :], ALU.mult, ALU.add)
            v.drain()
            dve.wait_ge(s["cst"], 9)
            v.tensor_scalar(first_row[:, :], first_row[:, :], 16.0, None, ALU.mult).then_inc(s["rmat_ready"], 1)
            dve.wait_ge(s["ksq_ready"], 1)
            v.tensor_tensor(rconst[:, :], rconst[:, :], M[:, 0:E], ALU.subtract)
            v.drain()

            for jt in range(TT):
                dve.wait_ge(s["v_mm"], jt + 1)
                v.tensor_tensor(V[:, jt, 0:512], J[:, :], bv[:, 0:512], ALU.add).then_inc(s["v_ev"], 1)

            def body(b):
                for p in range(8):
                    par, par1 = p % 2, (p - 1) % 2
                    if is_pair(b, p, -1):
                        need(dve, "exps", pair(b, p))
                        v.reciprocal(rinv[:, par1, :], rowsum[:, par1, :])
                        v.drain()
                        for h in range(2):
                            for it in range(TT):
                                n = 2 * h + it
                                w = N - WINDOW if it == 0 else N
                                x = P[:, par1, it, h, 0:w]
                                v.tensor_scalar(x, x, rinv[:, par1, n:n + 1], None, ALU.mult).then_inc(s["pn_ready"], 1)
                    if is_pair(b, p, 0):
                        for it, bk in ((0, S0), (1, S1)):
                            w = N - WINDOW if it == 0 else N
                            need_alone(dve, "scores", 2 * pair(b, p) + (it + 1))
                            for h in range(2):
                                n = 2 * h + it
                                v.tensor_tensor_reduce(out=shifted[:, par, it, h, 0:w], in0=bk[:, h * w:(h + 1) * w],
                                                       in1=band[:, it, 0:w], scale=-SCALE0, scalar=3.0e38, op0=ALU.add, op1=ALU.min,
                                                       accum_out=least[:, par, n:n + 1]).then_inc(s["shifted_ready"], 1)
                    if is_pair(b, p, -1):
                        need(dve, "pt_mm", 2 * pair(b, p) - 1)
                        need(dve, "pv_mm", pair(b, p, -2))
                        v.tensor_copy(PT[:, par1, 0, WINDOW:2 * N], PTA[:, WINDOW:2 * N]).then_inc(s["ptA_ev"], 1)
                    if p in (1, 2) and is_batch(b, 0):
                        need(dve, "v_mm", 4 * b + 2 + p)
                        v.tensor_tensor(V[:, p - 1, 512:1024], J[:, :], bv[:, 512:1024], ALU.add).then_inc(s["v_ev"], 1)
                    if p in (5, 6) and is_batch(b, 1):
                        need(dve, "v_mm", 4 * b + p)
                        v.tensor_tensor(V[:, p - 5, 0:512], J[:, :], bv[:, 0:512], ALU.add).then_inc(s["v_ev"], 1)
                    if not is_batch(b, -1):
                        continue
                    if p == 4:
                        need(dve, "m_y", b)
                        need(dve, "xsq_ready", 2 * b - 2)
                        v.tensor_tensor(res[:, :, :], M[:, 0:N].rearrange("q (i d) -> q i d", i=TT), x_all[:, bass.ds((b - 1) * TT, TT), :], ALU.add)
                        v.drain()
                        for it in range(TT):
                            v.bn_stats(st[:, it, :], res[:, it, :])
                        v.drain()
                        for it in range(TT):
                            v.bn_aggr(mv[:, it, :], st[:, it, :])
                        v.drain()
                        inv_sqrt(v, rstd[:, :], mv[:, :, 1], nhalf[:, :], t2[:, :])
                        need(dve, "scat", 16 * TT * TOPK * (b - 1) if not isinstance(b, int) or b > 1 else 0)
                        need(dve, "x1_kept", b - 1)
                        for it in range(TT):
                            last = v.tensor_scalar(x1c[:, it, :], res[:, it, :], mv[:, it, 0:1], rstd[:, it:it + 1], ALU.subtract, ALU.mult)
                        last.then_inc(s["x1c_ready"], 1)
                    if p == 6:
                        need(dve, "m_l", b)
                        need(dve, "xsq_ready", 2 * b)
                        need(dve, "exp_w", b - 1)
                        for it in range(TT):
                            v.scalar_tensor_tensor(lg[:, it, :], M[:, it * E:(it + 1) * E], xsq[:, it:it + 1], rconst[:, :], ALU.subtract, ALU.add)
                        v.drain()
                        for it in range(TT):
                            v.max(top[:, it, :], lg[:, it, :])
                        v.drain()
                        for it in range(TT):
                            v.max_index(topi[:, it, :], top[:, it, :], lg[:, it, :])
                        v.tensor_scalar(ntop[:, :], top[:, :, 0], -1.0, None, ALU.mult).then_inc(s["top_ready"], 1)
                        v.drain()
                        v.tensor_copy(topif[:, :, :], topi[:, :, :])
                        v.drain()
                        for it in range(TT):
                            for k in range(TOPK):
                                v.tensor_scalar(hot[:, it, k, :], iota_e[:, :], topif[:, it, k:k + 1], None, ALU.is_equal)
                        v.drain()
                        v.tensor_reduce(out=chosen[:, :, :], in_=hot[:, :, :, :].rearrange("q i k e -> q i e k"), axis=mybir.AxisListType.X, op=ALU.add)
                        v.drain()
                        v.tensor_copy(mask[:, :, :], chosen[:, :, :]).then_inc(s["mask_ready"], 1)
                    if p == 7:
                        need(dve, "m_r", b)
                        v.tensor_tensor(rank[:, :, :], M[:, 0:2 * E].rearrange("q (i e) -> q i e", i=TT), count[:, :].rearrange("q (o e) -> q o e", o=1).to_broadcast([128, TT, E]), ALU.add)
                        v.drain()
                        v.tensor_tensor(rank[:, :, :], rank[:, :, :], first_row[:, :].rearrange("q (o e) -> q o e", o=1).to_broadcast([128, TT, E]), ALU.add)
                        v.tensor_tensor(count[:, :], count[:, :], M[:, 2 * E:3 * E], ALU.add)
                        v.drain()
                        need(dve, "exp_w", b)
                        v.reciprocal(wsum[:, :], wsum[:, :])
                        for it in range(TT):
                            v.tensor_tensor(junk[:, it * TOPK:(it + 1) * TOPK, :], hot[:, it, :, :],
                                            rank[:, it:it + 1, :].to_broadcast([128, TOPK, E]), ALU.mult)
                        v.drain()
                        v.tensor_reduce(out=posf[:, :], in_=junk[:, :, :], axis=mybir.AxisListType.X, op=ALU.add)
                        for it in range(TT):
                            v.tensor_scalar(gate_all[:, bass.ds(b - 1, 1), it * TOPK:(it + 1) * TOPK].rearrange("q o k -> q (o k)"), wexp[:, it, :], wsum[:, it:it + 1], None, ALU.mult)
                        v.drain()
                        v.tensor_copy(posf_all[:, bass.ds((b - 1) * TT * TOPK, TT * TOPK)], posf[:, :])
                        v.tensor_copy(pos[:, :], posf[:, :]).then_inc(s["pos_ready"], 1)

            batch_loop(dve, 1, B - 1, 2, body)
            v.drain().then_inc(s["a_done"], 1)
            dve.wait_ge(s["a_done"], 4)

            dve.wait_ge(s["zrow_ready"], 2)
            v.tensor_scalar(past[:, :], count[:, :], float(GT - 1), None, ALU.add)
            v.drain()
            v.tensor_copy(cnt_i[:, :], past[:, :])
            v.drain()
            v.tensor_scalar(cnt_i[:, :], cnt_i[:, :], GT.bit_length() - 1, None, ALU.logical_shift_right)
            v.drain()
            v.tensor_copy(ntile[:, :], cnt_i[:, :])
            v.memset(past[:, :], 1.0)
            v.drain()
            v.tensor_tensor_scan(ncum[:, :], past[:, :], ntile[:, :], 0.0, ALU.mult, ALU.add)
            v.drain()
            v.tensor_scalar(past[:, :], ncum[:, :], tile_no[:, :], None, ALU.is_le)
            v.drain()
            v.tensor_reduce(out=tile_e[:, :], in_=past[:, :], axis=mybir.AxisListType.X, op=ALU.add)
            v.tensor_tensor(skip[:, :], past[:, :], ntile[:, :], ALU.mult)
            v.drain()
            v.tensor_reduce(out=tile_s[:, :], in_=skip[:, :], axis=mybir.AxisListType.X, op=ALU.add)
            v.tensor_scalar(used[:, :], tile_e[:, :], float(E), None, ALU.is_lt)
            v.drain()
            v.tensor_tensor(tile_s[:, :], tile_no[:, :], tile_s[:, :], ALU.subtract)
            v.drain()
            v.tensor_scalar(tile_s[:, :], tile_s[:, :], float(GT), float(-DUMMY), ALU.mult, ALU.add)
            v.drain()
            v.scalar_tensor_tensor(tile_s[:, :], tile_e[:, :], float(CAP), tile_s[:, :], ALU.mult, ALU.add)
            v.tensor_scalar(plan2[:, 0:1], tile_e[:, :], float(E - 1), None, ALU.min)
            v.drain()
            v.tensor_tensor(tile_s[:, :], tile_s[:, :], used[:, :], ALU.mult)
            v.drain()
            v.tensor_scalar(plan2[:, 1:2], tile_s[:, :], float(DUMMY), None, ALU.add)
            v.tensor_tensor(skip[:, :], count[:, :], first_row[:, :], ALU.add)
            v.drain()
            v.tensor_copy(pad_at[:, :], skip[:, :])
            v.drain().then_inc(s["plan_ready"], 1)

            v.tensor_tensor(past[:, :], ncum[:, :], ntile[:, :], ALU.subtract)
            v.drain()
            v.scalar_tensor_tensor(past[:, :], past[:, :], float(GT), first_row[:, :], ALU.mult, ALU.subtract)
            v.drain()
            v.tensor_copy(skip[:, 0:1], past[:, 0:1])
            v.tensor_tensor(skip[:, 1:E], past[:, 1:E], past[:, 0:E - 1], ALU.subtract)
            v.drain()
            npos = B * TT * TOPK
            at = posf_all[:, :].rearrange("q (n o) -> q n o", o=1).to_broadcast([128, npos, E])
            v.tensor_tensor(shift[:, :, :], at, first_row[:, :].rearrange("q (o e) -> q o e", o=1).to_broadcast([128, npos, E]), ALU.is_ge)
            v.drain()
            v.tensor_tensor(shift[:, :, :], shift[:, :, :], skip[:, :].rearrange("q (o e) -> q o e", o=1).to_broadcast([128, npos, E]), ALU.mult)
            v.drain()
            v.tensor_reduce(out=shift_sum[:, :], in_=shift[:, :, :], axis=mybir.AxisListType.X, op=ALU.add)
            v.drain()
            v.tensor_tensor(posf_all[:, :], posf_all[:, :], shift_sum[:, :], ALU.add)
            v.drain()
            v.tensor_copy(pos_all[:, :], posf_all[:, :]).then_inc(s["pos_all_ready"], 1)

            dve.wait_ge(s["plan_in"], 16)

            def expert_of(n):
                src = plan[0:1, 2 * n:2 * n + 1] if isinstance(n, int) else plan[0:1, bass.ds(2 * n, 1)]
                return dve.value_load(src, min_val=0, max_val=E - 1)

            def weights_A(e, par):
                v.tensor_copy(wA[:, par, :], wall[:, bass.ds(e, 1), 0:WA].rearrange("q o c -> q (o c)")).then_inc(s["wA_ready"], 1)

            def weights_B(e, par):
                v.tensor_copy(wB[:, par, :], wall[:, bass.ds(e, 1), WA:WCOLS].rearrange("q o c -> q (o c)")).then_inc(s["wB_ready"], 1)

            def rows_T(n, par):
                need(dve, "tin_mm", n + 1)
                v.tensor_copy(xgT[:, par, :], TI[:, 0:GT]).then_inc(s["xgT_ready"], 1)

            first = expert_of(0)
            weights_A(first, 0)
            rows_T(0, 0)
            weights_B(first, 0)

            def tiles(i):
                for p in range(2):
                    n, q = 2 * i + p, 1 - p
                    if is_tile(i, p, 1):
                        e = expert_of(n + 1)
                        need(dve, "up_mm", 4 * n)
                        need(dve, "hid_ready", 4 * n)
                        weights_A(e, q)
                        rows_T(n + 1, q)
                    if is_tile(i, p, -1):
                        need(dve, "dn_mm", n)
                        need(dve, "yTe_ready", n)
                    if is_tile(i, p, 1):
                        weights_B(e, q)
                    if is_tile(i, p, -2):
                        need(dve, "tout_mm", n - 1)
                        need(dve, "ys_out", 16 * n - 48)
                        v.tensor_copy(yrow[:, p, :, :], TO[:, 0:GT].rearrange("q (a d) -> q a d", a=2)).then_inc(s["yrow_ready"], 1)

            batch_loop(dve, 2, NT // 2 - 1, 2, tiles)

            v.tensor_copy(identb[:, :], ident[:, :])
            v.memset(qst[:, :, :, :].rearrange("q a h n -> q (a h n)").bitcast(u32), 0)
            v.memset(kst[:, :, :, :].rearrange("q a h n -> q (a h n)").bitcast(u32), 0)
            v.memset(zst[:, :, :], 0.0)
            v.memset(v32[:, :, :, :, :], 0.0)
            v.drain()
            v.memset(kst[MROW:MROW + NPART, :, :, :], 1.0)
            v.memset(v32[:, :, :, :, DH1:DH1 + 1], 1.0)
            dve.wait_ge(s["cw_in"], 128)
            v.tensor_scalar(gu[:, :, :], gu[:, :, :], 0.5, None, ALU.mult)
            v.tensor_scalar(gcol[:, 0:2], gcol[:, 0:2], 0.5, None, ALU.mult)
            v.memset(c2[:, :], 0.0)
            v.drain()
            v.tensor_scalar(c2[:, :], c2[:, :], gcol[:, 3:4], 2.0, ALU.add, ALU.mult).then_inc(s["scan_done"], 1)
            dve.wait_ge(s["lora_mm"], 1)
            v.scalar_tensor_tensor(cw[:, :, :], MI.rearrange("q (k d) -> q k d", k=4), LORA, cw[:, :, :], ALU.mult, ALU.add)
            v.drain().then_inc(s["c_set"], 1)

            def attention(b, par):
                for p in range(8):
                    if has(b, 1) and p < 4:
                        for k in range(4):
                            need(dve, "s_full", H1 * (b + 1) + (4 * p + k + 1))
                            v.tensor_reduce(out=mx[:, :, 4 * p + k], in_=SB[k % 2].rearrange("q (i n) -> q i n", i=TT),
                                            axis=mybir.AxisListType.X, op=ALU.max).then_inc(s["max_done"], 1)
                    off, j = quad(b, p)
                    if p == 0 and has(b, 2):
                        need(dve, "a1_ready", b + 3)
                        v.tensor_tensor(rest[:, :], MI[:, :], parts[:, 0, :], ALU.subtract).then_inc(s["misc_free"], 1)
                        v.drain()
                        v.tensor_copy(parts[:, 1, :], rest[:, :])
                        v.drain()
                        v.tensor_tensor(parts[:, 2, :], rest[:, :], parts[:, 1, :], ALU.subtract).then_inc(s["parts_ready"], 1)
                    if p % 2 == 1 and has(b, off):
                        need(dve, "misc_full", misc.before(b, TOS[(p - 1) // 2] + 1))
                        o = MI[:, 0:N].rearrange("q (i r c) -> q i r c", i=TT, r=4)
                        v.reciprocal(dinv[:, :, :], o[:, :, :, DH1])
                        v.drain()
                        for it in range(TT):
                            last = v.tensor_tensor(otok[:, it, 32 * j:32 * j + 32].rearrange("q (r c) -> q r c", r=4), o[:, it, :, 0:DH1],
                                                   dinv[:, it, :].rearrange("q (r o) -> q r o", o=1).to_broadcast([128, 4, DH1]), ALU.mult)
                        v.drain().then_inc(s["misc_free"], 1)
                    if p == 1 and has(b, 1):
                        need(dve, "misc_full", misc.before(b, VP + 1))
                        for jt in range(TT):
                            v.tensor_copy(v32[:, 1 - par, jt, :, 0:DH1], MI[:, jt * D:(jt + 1) * D].rearrange("q (h d) -> q h d", h=H1))
                        v.drain().then_inc(s["misc_free"], 1)
                    if p == 3 and has(b, -1):
                        need(dve, "misc_full", misc.before(b, WO + 1))
                        need(dve, "x2_kept", b)
                        v.tensor_tensor(res2[:, :, :], MI[:, 0:N].rearrange("q (i d) -> q i d", i=TT), x_all[:, bass.ds((b - 1) * TT, TT), :], ALU.add).then_inc(s["misc_free"], 1)
                        v.drain()
                        v.tensor_tensor(res2[:, :, :], res2[:, :, :], bo1[:, :].rearrange("q (o d) -> q o d", o=1).to_broadcast([128, TT, D]), ALU.add)
                        v.drain()
                        layernorm(v, res2, x3c, TT, st2, mv2, rstd2, nh2, u2, lambda: need(dve, "x3_kept", b - 1)).then_inc(s["x3_ready"], 1)
                    if p == 4 and has(b, 1):
                        v.drain()
                        v.tensor_scalar(nmx[:, :, 0, :], mx[:, :, :], -1.0, None, ALU.mult)
                        v.drain()
                        v.scalar_tensor_tensor(mrest[:, :, :], mx[:, :, :], -1.0, nmx[:, :, 0, :], ALU.mult, ALU.subtract)
                        v.drain()
                        v.tensor_copy(nmx[:, :, 1, :], mrest[:, :, :])
                        v.drain()
                        v.tensor_tensor(nmx[:, :, 2, :], mrest[:, :, :], nmx[:, :, 1, :], ALU.subtract).then_inc(s["nm_ready"], 1)
                    if p == 5 and has(b, 3):
                        need(dve, "yk_in", 16 * TT * TOPK * (b + 4))
                        v.tensor_copy(gcur[:, :], gate_all[:, bass.ds(b + 3, 1), :].rearrange("q o k -> q (o k)"))
                        v.tensor_copy(acc[:, :, :], x_all[:, bass.ds((b + 3) * TT, TT), :])
                        v.drain()
                        for k in range(TOPK):
                            for it in range(TT):
                                n = it * TOPK + k
                                last = v.scalar_tensor_tensor(acc[:, it, :], yk[:, n, :], gcur[:, n:n + 1], acc[:, it, :], ALU.mult, ALU.add)
                            if k == TOPK - 1:
                                last.then_inc(s["comb_done"], 1)
                            v.drain()
                        layernorm(v, acc, x2c, TT, st2, mv2, rstd2, nh2, u2, lambda: need(dve, "x2_kept", b + 3)).then_inc(s["x2_ready"], 1)
                    if p == 7 and has(b, -1):
                        need(dve, "gate_act", b)
                        v.scalar_tensor_tensor(c2[:, :], tf[:, :], 1.0, c2[:, :], ALU.add, ALU.mult)
                        v.scalar_tensor_tensor(tg[:, :], ti[:, :], 1.0, tg[:, :], ALU.add, ALU.mult)
                        v.drain()
                        v.scalar_tensor_tensor(c2[:, :], c2[:, :], 0.5, tg[:, :], ALU.mult, ALU.add).then_inc(s["scan_done"], 1)

            attention_loop(dve, attention)
            dve.wait_ge(s["state_mm"], 1)
            v.tensor_tensor(state[:, :, :], SB[0][:, 0:N].rearrange("q (i d) -> q i d", i=TT), bo2[:, :].rearrange("q (o d) -> q o d", o=1).to_broadcast([128, TT, D]), ALU.add)
            v.drain()
            for c in range(B // 4):
                xo = xo_all[:, 8 * c:8 * c + 8, :].rearrange("q (k i) d -> q k i d", i=TT)
                v.tensor_tensor(xo, xo, state[:, :, :].rearrange("q (o i) d -> q o i d", o=1).to_broadcast([128, 4, TT, D]), ALU.add).then_inc(s["h_pre"], 1)
            dve.wait_ge(s["x3_kept"], B)
            for c in range(B // 4):
                dve.wait_ge(s["h_act"], c + 1)
                xs_ = x_all[:, 8 * c:8 * c + 8, :]
                v.tensor_tensor(xs_, xs_, xo_all[:, 8 * c:8 * c + 8, :], ALU.add)
                v.drain()
                layernorm(v, xs_, xs_, 8, st2, mv2, rstd2, nh2, u2, lambda: None)
                v.drain().then_inc(s["fin_ready"], 1)


def laid_out(inputs):
    import numpy as np

    def c(v):
        return np.ascontiguousarray(v)

    def g(name):
        return np.asarray(inputs[name])

    def stack_T(layer, names):
        return c(np.stack([g(f"{layer}_{n}").T for n in names], 1))

    r = {}
    r["x"] = c(g("L0_attn_x").reshape(TOK, D))
    r["xT"] = c(r["x"].T)
    for dst, src in (("w1T", "attn_W1"), ("w2T", "attn_W2"), ("wgT", "attn_Wg"), ("keysT", "ffn_keys"), ("rwT", "ffn_rw")):
        r[dst] = c(g("L0_" + src).T)
    bg = g("L0_attn_bg")
    hd = H * DH
    r["colsA"] = c(np.concatenate([g("L0_attn_b1")[:, None], g("L0_attn_b2")[:, None], g("L0_attn_bo")[:, None],
                                   bg[:hd].reshape(PAIRS, 128).T, bg[hd:2 * hd].reshape(PAIRS, 128).T], 1))
    r["bvB"] = c(np.broadcast_to(bg[2 * hd:], (128, hd)))
    r["woT"] = c(g("L0_attn_Wo").T.reshape(PAIRS, 128, D).transpose(1, 0, 2))
    r["rbB"] = c(np.broadcast_to(g("L0_ffn_rb"), (128, E)))
    r["ident"] = np.eye(128, dtype=np.float32)
    w1 = g("L0_ffn_w1").transpose(2, 0, 1)
    b1 = g("L0_ffn_b1").reshape(E, FC, 128).transpose(2, 0, 1)
    w2 = g("L0_ffn_w2").transpose(0, 2, 1).reshape(E, FC, 128, D).transpose(2, 0, 1, 3).reshape(128, E, FC * D)
    b2 = g("L0_ffn_b2").T[:, :, None]
    r["wall"] = c(np.concatenate([w1, b1, w2, b2], 2))
    r["cw"] = stack_T("L1_attn", ("Wq", "Wk", "Wv", "Wo"))
    r["lora_a"] = c(np.stack([g("L1_attn_" + n) for n in ("Aq", "Ak", "Av", "Ao")], 1))
    r["lora_b"] = stack_T("L1_attn", ("Bq", "Bk", "Bv", "Bo"))
    r["gw"] = stack_T("L1_ffn", ("wf", "wi", "wc", "wo"))
    r["gu"] = stack_T("L1_ffn", ("uf", "ui", "uc", "uo"))
    r["gcol"] = c(np.stack([g("L1_ffn_" + n) for n in ("bf", "bi", "bc", "in_c")], 1))
    r["bo1"] = c(np.broadcast_to(g("L1_attn_bo"), (128, D)))
    r["bo2"] = c(np.broadcast_to(g("L1_ffn_bo"), (128, D)))
    return r


def kernel(**inputs):
    import concourse.bacc as bacc
    from concourse import mybir as my
    from concourse.bass_utils import run_bass_kernel_spmd

    arrays = {"in_" + k: v for k, v in laid_out(inputs).items()}
    nc = bacc.Bacc("TRN2", target_bir_lowering=False, num_devices=1)
    t = {k[3:]: nc.dram_tensor(k, v.shape, my.dt.float32, kind="ExternalInput").ap() for k, v in arrays.items()}
    out = nc.dram_tensor("out", (TOK, D), my.dt.float32, kind="ExternalOutput").ap()
    build(nc, t, out)
    r = run_bass_kernel_spmd(nc, [arrays], core_ids=[0])
    return r.results[0]["out"].reshape(B, N, D)
```

```python
import concourse.bass as bass
from concourse import mybir
from contextlib import ExitStack

DT = mybir.dt
fp32, bf16, i32, u32 = DT.float32, DT.bfloat16, DT.int32, DT.uint32
ACT = mybir.ActivationFunctionType
ALU = mybir.AluOpType

B, N, D = 16, 256, 128
TOK = B * N
TT = N // 128
H, DH = 16, 64
PAIRS = H // 2
WINDOW = 64
SCALE0 = DH ** -0.5
E, TOPK, F = 16, 4, 512
FC = F // 128
H1, DH1 = 16, 8
SCALE1 = DH1 ** -0.5
RANK, LORA = 16, 1.0 / 16
NPART = 3
MROW = 64
BIG = 1.0e30
EPS = 1e-5
GT = 256
CAP = TOK + GT
DUMMY = E * CAP
NT = (TOK * TOPK + E * (GT - 1)) // GT
NT += NT % 2
ROWS = DUMMY + GT
WA = F + FC
WB = FC * D + 1
WCOLS = WA + WB


def batch_loop(eng, front, end, back, body):
    for b in range(front):
        body(b)
    with eng.Fori(front, end) as b:
        body(b)
    for b in range(end, end + back):
        body(b)


class Tally:

    FULL = 1

    def __init__(self, offsets):
        self.offsets = offsets

    def before(self, b, k=0):
        if not isinstance(b, int):
            n = len(self.offsets)
            return n * b + (self.before(self.FULL) - n * self.FULL + k)
        takes_place = [(c, n, any(0 <= c + o < B for o in offs)) for c in range(-3, b + 1) for n, offs in enumerate(self.offsets)]
        return sum(t for c, n, t in takes_place if (c, n) < (b, k))


def attention_loop(eng, body):
    for b in range(-3, 1):
        body(b, b % 3)
    with eng.Fori(0, (B - 4) // 3) as i:
        for k in range(1, 4):
            body(3 * i + k, k % 3)
    for b in range(B - 3, B + 1):
        body(b, b % 3)


def moments(v, x, n, stat, mv):
    for k in range(n):
        v.bn_stats(stat[:, k, :], x[:, k, :])
    v.drain()
    for k in range(n):
        v.bn_aggr(mv[:, k, :], stat[:, k, :])
    v.drain()


def normalise(v, x, outs, mv, rstd, nhalf, t2, ready=None):
    n = len(outs)
    inv_sqrt(v, rstd[:, 0:n], mv[:, 0:n, 1], nhalf[:, 0:n], t2[:, 0:n])
    if ready:
        ready()
    return [v.tensor_scalar(outs[k], x[:, k, :], mv[:, k, 0:1], rstd[:, k:k + 1], ALU.subtract, ALU.mult) for k in range(n)]


def inv_sqrt(v, y, var, nhalf, t2):
    v.tensor_scalar(nhalf, var, EPS, None, ALU.add)
    v.drain()
    v.tensor_scalar(t2.bitcast(i32), nhalf.bitcast(i32), 1, None, ALU.logical_shift_right)
    v.drain()
    v.tensor_scalar(y.bitcast(i32), t2.bitcast(i32), -1.0, float(0x5F3759DF), ALU.mult, ALU.add)
    v.tensor_scalar(nhalf, nhalf, -0.5, None, ALU.mult)
    v.drain()
    for _ in range(3):
        v.tensor_tensor(t2, y, y, ALU.mult)
        v.drain()
        v.tensor_tensor(t2, t2, nhalf, ALU.mult)
        v.drain()
        v.scalar_tensor_tensor(y, t2, 1.5, y, ALU.add, ALU.mult)
        v.drain()


def build(nc, t, out):
    ctx = ExitStack()
    with ctx:
        def sb(name, shape, dt=fp32, c=ctx):
            return c.enter_context(nc.sbuf_tensor(name, shape, dt))

        def sem(name):
            return ctx.enter_context(nc.semaphore(name))

        psum = ctx.enter_context(nc.psum_tensor("psum", [128, 8 * 512], fp32))
        bank = [psum[:, i * 512:(i + 1) * 512] for i in range(8)]

        ident = sb("ident", [128, 128])
        x_all = sb("x_all", [128, B * TT, D])
        wall = sb("wall", [128, E, WCOLS])
        posf_all = sb("posf_all", [128, B * TT * TOPK])
        pos_all = sb("pos_all", [128, B * TT * TOPK], u32)
        gate_all = sb("gate_all", [128, B, TT * TOPK])
        count = sb("count", [128, E])

        first_row = sb("first_row", [128, E])

        cnt_i = sb("cnt_i", [128, E], i32)
        ntile = sb("ntile", [128, E])
        ncum = sb("ncum", [128, E])
        delta = sb("delta", [128, E])
        tile_no = sb("tile_no", [128, 1])
        past = sb("past", [128, E])
        skip = sb("skip", [128, E])
        tile_e = sb("tile_e", [128, 1])
        tile_s = sb("tile_s", [128, 1])
        used = sb("used", [128, 1])
        plan2 = sb("plan2", [128, 2], i32)
        pad_at = sb("pad_at", [128, E], i32)
        plan = sb("plan", [1, 256], i32)
        zrow = sb("zrow", [128, 2, D])

        a = ExitStack()
        wg = sb("wg", [128, 3 * H * DH], c=a)
        wo = sb("wo", [128, PAIRS, D], c=a)
        w1 = sb("w1", [128, D], c=a)
        w2 = sb("w2", [128, D], c=a)
        cols = sb("cols", [128, 3 + 2 * PAIRS], c=a)
        bv = sb("bv", [128, H * DH], c=a)
        hT = sb("hT", [128, TOK], c=a)
        h1 = sb("h1", [128, 2, 512], c=a)
        hV = sb("hV", [128, N], c=a)
        qT = sb("qT", [128, PAIRS, N], c=a)
        kT = sb("kT", [128, PAIRS, 2, N], c=a)
        V = sb("V", [128, TT, H * DH], c=a)
        band = sb("band", [128, TT, N], c=a)
        shifted = sb("shifted", [128, 2, TT, 2, N], c=a)
        least = sb("least", [128, 2, 4], c=a)
        P = sb("P", [128, 2, TT, 2, N], c=a)
        rowsum = sb("rowsum", [128, 2, 4], c=a)
        rinv = sb("rinv", [128, 2, 4], c=a)
        PT = sb("PT", [128, 2, 2, 2 * N], c=a)
        OT = sb("OT", [128, 2, N], c=a)
        yT = sb("yT", [128, N], c=a)
        x1T = sb("x1T", [128, N], c=a)
        x1c = sb("x1c", [128, TT, D], c=a)
        res = sb("res", [128, TT, D], c=a)
        sqj = sb("sqj", [128, D], c=a)
        xsq = sb("xsq", [128, TT], c=a)
        st = sb("st", [128, TT, 6], c=a)
        mv = sb("mv", [128, TT, 2], c=a)
        rstd = sb("rstd", [128, TT], c=a)
        nhalf = sb("nhalf", [128, TT], c=a)
        t2 = sb("t2", [128, TT], c=a)
        minus_half = sb("minus_half", [128, TT], c=a)
        keysT = sb("keysT", [128, E], c=a)
        rwT = sb("rwT", [128, E], c=a)
        rmat = sb("rmat", [128, E], c=a)
        ksq = sb("ksq", [128, E], c=a)
        rconst = sb("rconst", [128, E], c=a)
        ones = sb("ones", [128, 128], c=a)
        onesb = sb("onesb", [128, 128], bf16, c=a)
        tri = sb("tri", [128, 128], bf16, c=a)
        iota_e = sb("iota_e", [128, E], c=a)
        lg = sb("lg", [128, TT, E], c=a)
        top = sb("top", [128, TT, 8], c=a)
        topi = sb("topi", [128, TT, 8], u32, c=a)
        topif = sb("topif", [128, TT, 8], c=a)
        ntop = sb("ntop", [128, TT], c=a)
        wexp = sb("wexp", [128, TT, TOPK], c=a)
        wsum = sb("wsum", [128, TT], c=a)
        hot = sb("hot", [128, TT, TOPK, E], c=a)
        mask = sb("mask", [128, TT, E], bf16, c=a)
        chosen = sb("chosen", [128, TT, E], c=a)
        rank = sb("rank", [128, TT, E], c=a)
        junk = sb("junk", [128, TT * TOPK, E], c=a)
        posf = sb("posf", [128, TT * TOPK], c=a)
        pos = sb("pos", [128, TT * TOPK], u32, c=a)
        a.close()

        xg = sb("xg", [128, 2, 2, D])
        xgT = sb("xgT", [128, 2, GT])
        wA = sb("wA", [128, 2, WA])
        wB = sb("wB", [128, 2, WB])
        hid = sb("hid", [128, 2, FC, GT])
        yTe = sb("yTe", [128, 2, GT])
        yrow = sb("yrow", [128, 2, 2, D])

        cw = sb("cw", [128, 4, D])
        lora_a = sb("lora_a", [RANK, 4, D])
        lora_b = sb("lora_b", [RANK, 4, D])
        gw = sb("gw", [128, 4, D])
        gu = sb("gu", [128, 4, D])
        gcol = sb("gcol", [128, 4])
        bo1 = sb("bo1", [128, D])
        bo2 = sb("bo2", [128, D])
        identb = sb("identb", [128, 128], bf16)
        spare = wall[:, :, :].rearrange("q e c -> q (e c)")
        qst = [sb("qst0", [128, H, N], bf16), sb("qst1", [128, H, N], bf16),
               spare[:, 2 * B * N:2 * B * N + H * N // 2].bitcast(bf16).rearrange("q (h n) -> q h n", h=H)]
        kst = [sb("kst0", [128, H, N], bf16), sb("kst1", [128, H, N], bf16),
               spare[:, 2 * B * N + H * N // 2:2 * B * N + H * N].bitcast(bf16).rearrange("q (h n) -> q h n", h=H)]
        shift = qst[0][:, :, :].rearrange("q h n -> q (h n)").bitcast(fp32).rearrange("q (n e) -> q n e", e=E)
        zst = sb("zst", [NPART, H, N], bf16)
        v32 = sb("v32", [128, 3, TT, H, 32])
        xo_all = spare[:, 0:B * N].rearrange("q (t d) -> q t d", d=D)
        pc = spare[:, B * N:2 * B * N].rearrange("q (s h j n) -> q s h j n", s=4, h=2, j=TT)
        yk = sb("yk", [128, TT * TOPK, D])
        posc = sb("posc", [128, TT * TOPK], u32)
        gcur = sb("gcur", [128, TT * TOPK])
        sums = sb("sums", [128, 2 * TT, D])
        acc, res2 = sums[:, 0:TT, :], sums[:, TT:2 * TT, :]
        x2c = sb("x2c", [128, TT, D])
        x2T = sb("x2T", [128, 3, N])
        parts = sb("parts", [128, NPART, 2 * N], bf16)
        rest = sb("rest", [128, 2 * N])
        mx = sb("mx", [128, TT, H])
        mrest = sb("mrest", [128, TT, H // 2])
        nmx = sb("nmx", [128, TT, 2, NPART, H // 2], bf16)
        mrow = sb("mrow", [NPART * H // 2, N], bf16)
        oTc = sb("oTc", [128, N])
        dinv = sb("dinv", [128, TT, 4])
        otok = sb("otok", [128, TT, D])
        oT = sb("oT", [128, N])
        x3c = sb("x3c", [128, TT, D])
        x3T = sb("x3T", [128, N])
        c2 = sb("c2", [128, N])
        tf = sb("tf", [128, N])
        ti = sb("ti", [128, N])
        tg = sb("tg", [128, N])
        state = sb("state", [128, TT, D])
        st2 = sb("st2", [128, 8, 6])
        mv2 = sb("mv2", [128, 8, 2])
        rstd2 = sb("rstd2", [128, 8])
        nh2 = sb("nh2", [128, 8])
        u2 = sb("u2", [128, 8])

        UP = [psum[:, 0:1024], psum[:, 1024:2048]]
        TI, DN, TO = bank[4], bank[5], bank[6]
        S0, S1, PTA, PTB, OTB, J, Y, M = bank

        xs = nc.dram_tensor("xs", (ROWS, D), fp32, kind="Internal").ap()
        ys = nc.dram_tensor("ys", (NT * GT, D), fp32, kind="Internal").ap()
        qkd = nc.dram_tensor("qkd", (NPART, 128, 2 * N), bf16, kind="Internal").ap()
        plan_d = nc.dram_tensor("plan_d", (128, 2), i32, kind="Internal").ap()

        names = """w_in xT_in0 xT_in1 xT_in2 xT_in3 wg_in rest_in x_in wall_in cst cst2 went_on hA_mm hA_act hB_mm h_ready
            qk_mm q_ev k_ev v_mm v_ev hv_ready
            scores shifted_ready exps pn_ready pt_mm ptA_ev ptB_ev pv_mm ot_ev wo_mm yT_ev
            m_y var_ready pow_ready x1c_ready m_x x1T_ready m_l mask_ready m_r pos_ready xsq_ready x1_kept scat exp_w top_ready
            ksq_ready rmat_ready a_done plan_ready zrow_ready plan_out plan_in pad_in
            xg_in0 xg_in1 tin_mm xgT_ready wA_ready wB_ready up_mm hid_ready dn_mm yTe_ready tout_mm yrow_ready ys_out
            cw_in lora_mm c_set cleared st_full exps1 s_full max_done pv_full o_free full0 full1 free0 free1 a1_ready parts_ready
            qkd_out stk m_in nm_ready x2_ready x2_kept x3_ready x3_kept gates_full gate_act scan_done
            yk_in comb_done posc_ready state_mm state_ready h_pre h_act fin_ready out_done""".split()
        s = {n: sem(n) for n in names}

        def pair(b, p, off=0):
            return 8 * b + (p + off)

        def is_pair(b, p, off):
            return 0 <= 8 * b + p + off < 8 * B if isinstance(b, int) else True

        def is_batch(b, off):
            return 0 <= b + off < B if isinstance(b, int) else True

        def need(eng, name, n):
            if not isinstance(n, int) or n > 0:
                eng.wait_ge(s[name], n)

        def need_alone(eng, name, n):
            if not isinstance(n, int) or n > 0:
                eng.wait_ge(s[name], n)
                eng.sem_inc(s["went_on"], 1)

        def has(b, off):
            return 0 <= b + off < B if isinstance(b, int) else True

        PRODUCTS = [(0, 0), (0, 1), (0, 2), (1, 0), (1, 1), (2, 0)]
        NSTK = 2 * len(PRODUCTS) + 1
        QK, TO3, TMB, TOT, VP, TO0, WO = (0, 0), (1, 0), (0, 1), (1, 1), (0, 2), (1, 2), (0, 3)
        TMA, TO1, TX, GA, GB, TO2 = (1, 3), (0, 4), (1, 4), (0, 5), (1, 5), (0, 6)
        tally = [Tally([(2,), (0,), (1,), (-1,), (0,), (-1,), (0,)]), Tally([(-1,), (-1,), (0,), (1,), (3, -1), (-1,)])]
        TOS = [TO3, TO0, TO1, TO2]
        ST = psum[:, 0:1024]
        SB = [bank[2], bank[3], bank[4]]
        OB, MIS = bank[5], [bank[6], bank[7]]

        def shared(use):
            return MIS[use[0]]

        def need_full(eng, b, use):
            need(eng, f"full{use[0]}", tally[use[0]].before(b, use[1] + 1))

        def need_free(eng, b, use, done=0):
            need(eng, f"free{use[0]}", tally[use[0]].before(b, use[1] + done))

        def quad(b, p):
            return (-1, 3) if p < 2 else (0, p // 2 - 1)

        def is_tile(i, p, off):
            return 0 <= 2 * i + p + off < NT if isinstance(i, int) else True

        block = ctx.enter_context(nc.Block())
        NCH = TOK // 512

        @block.sync
        def _(sp):
            def load(dst, src, signal):
                dst = dst[:, :, :] if len(dst.shape) == 3 else dst[:, :]
                sp.dma_start(dst, t[src]).then_inc(s[signal], 16)

            for dst, src in ((w1, "w1T"), (w2, "w2T"), (cols, "colsA")):
                load(dst, src, "w_in")
            for c in range(4):
                sp.dma_start(hT[:, c * (TOK // 4):(c + 1) * (TOK // 4)], t["xT"][:, c * (TOK // 4):(c + 1) * (TOK // 4)]).then_inc(s[f"xT_in{c}"], 16)
            load(wg, "wgT", "wg_in")
            for dst, src in ((ident, "ident"), (bv, "bvB"), (keysT, "keysT"), (rwT, "rwT"), (rconst, "rbB"), (wo, "woT")):
                load(dst, src, "rest_in")
            sp.dma_start(x_all[:, :, :], t["x"].rearrange("(n p) d -> p n d", p=128)).then_inc(s["x_in"], 16)
            load(wall, "wall", "wall_in")
            sp.wait_ge(s["plan_ready"], 1)
            sp.dma_start(plan_d, plan2[:, :]).then_inc(s["plan_out"], 16)
            sp.wait_ge(s["zrow_ready"], 1)

            def pad(e):
                at = sp.value_load(pad_at[0:1, e:e + 1], min_val=0, max_val=DUMMY) if e < E else DUMMY
                sp.dma_start(xs[bass.ds(at, GT), :].rearrange("(p a) d -> p a d", a=2), zrow[:, :, :]).then_inc(s["pad_in"], 16)

            for e in range(4):
                pad(e)
            sp.wait_ge(s["plan_out"], 16)
            sp.dma_start(plan[:, :], plan_d.rearrange("(o t) c -> o (t c)", o=1)).then_inc(s["plan_in"], 16)
            for e in range(4, E + 1):
                pad(e)
            sp.wait_ge(s["plan_in"], 16)
            sp.wait_ge(s["pad_in"], 16 * (E + 1))
            sp.wait_ge(s["a_done"], 4)

            def row_of(n):
                at = 2 * n + 1
                src = plan[0:1, at:at + 1] if isinstance(n, int) else plan[0:1, bass.ds(at, 1)]
                return sp.value_load(src, min_val=0, max_val=DUMMY)

            def load_rows(n, par):
                need_alone(sp, "tin_mm", n - 1)
                sp.dma_start(xg[:, par, :, :], xs[bass.ds(row_of(n), GT), :].rearrange("(p a) d -> p a d", a=2)).then_inc(s[f"xg_in{par}"], 16)

            load_rows(0, 0)
            load_rows(1, 1)
            for dst, src in ((cw, "cw"), (lora_a, "lora_a"), (lora_b, "lora_b"), (gw, "gw"), (gu, "gu"), (gcol, "gcol"),
                             (bo1, "bo1"), (bo2, "bo2")):
                load(dst, src, "cw_in")

            def body(i):
                for p in range(2):
                    n = 2 * i + p
                    if is_tile(i, p, 2):
                        load_rows(n + 2, p)
                    if is_tile(i, p, -2):
                        need_alone(sp, "yrow_ready", n - 1)
                        need_alone(sp, "ys_out", 16 * n - 32)
                        sp.dma_start(ys[bass.ds((n - 2) * GT, GT), :].rearrange("(p a) d -> p a d", a=2), yrow[:, p, :, :]).then_inc(s["ys_out"], 16)

            batch_loop(sp, 2, NT // 2 - 1, 2, body)
            sp.wait_ge(s["ys_out"], 16 * NT)

            def attention(b, par):
                if has(b, 2):
                    load = (par + 2) % 3
                    need_alone(sp, "parts_ready", b + 3)
                    sp.dma_start(qkd.rearrange("a r c -> r a c"), parts[:, :, :]).then_inc(s["qkd_out"], 16)
                if has(b, 0):
                    maxima(b, TMB, par, 1, 2 * b + 1, H1 * (b + 1))
                if has(b, 2):
                    need_alone(sp, "qkd_out", 16 * (b + 3))
                    need_alone(sp, "st_full", 8 * b)
                    need_alone(sp, "stk", 16 * NSTK * (b + 2))
                    for n, (qa, ka) in enumerate(PRODUCTS):
                        for dst, part, c0 in ((qst[load], qa, 0), (kst[load], ka, N)):
                            sp.dma_start(dst[DH1 * n:DH1 * n + DH1, :, :],
                                         qkd[part].rearrange("(h d) c -> d h c", d=DH1)[:, :, c0:c0 + N]).then_inc(s["stk"], 16)
                    sp.dma_start(qst[load][MROW:MROW + NPART, :, :], zst[:, :, :]).then_inc(s["stk"], 16)
                if has(b, 1):
                    maxima(b, TMA, (par + 1) % 3, 0, 2 * b + 2, H1 * (b + 1) + H1 // 2)

            def maxima(b, use, slot, half, before, scored):
                need_alone(sp, f"free{use[0]}", tally[use[0]].before(b, use[1] + 1))
                need_alone(sp, "s_full", scored)
                need_alone(sp, "m_in", 16 * NPART * before)
                hh = H1 // 2
                for k in range(NPART):
                    sp.dma_start(qst[slot][MROW + k:MROW + k + 1, half * hh:half * hh + hh, :], mrow[k * hh:(k + 1) * hh, :]).then_inc(s["m_in"], 16)

            sp.wait_ge(s["cleared"], 2)
            attention_loop(sp, attention)
            for c in range(B // 4):
                sp.wait_ge(s["fin_ready"], c + 1)
                sp.dma_start(out[c * 4 * N:(c + 1) * 4 * N, :].rearrange("(n p) d -> p n d", p=128), x_all[:, 8 * c:8 * c + 8, :]).then_inc(s["out_done"], 16)
            sp.wait_ge(s["out_done"], 16 * B // 4)

        @block.gpsimd
        def _(pool):
            g = nc.gpsimd
            g.memset(kT[:, :, :, :], 0.0).then_inc(s["cst2"], 1)
            g.memset(P[:, :, :, :, :], 0.0).then_inc(s["cst2"], 1)
            g.memset(band[:, :, :], 0.0).then_inc(s["cst"], 1)
            pool.wait_ge(s["cst"], 1)
            for it in range(TT):
                g.affine_select(out=band[:, it, :], in_=band[:, it, :], compare_op=ALU.is_ge, fill=-BIG,
                                base=WINDOW - 1 + 128 * it, pattern=[[-1, N]], channel_multiplier=1).then_inc(s["cst"], 1)
            g.memset(ones[:, :], 1.0).then_inc(s["cst"], 1)
            g.memset(onesb[:, :], 1.0).then_inc(s["cst"], 1)
            pool.wait_ge(s["cst"], 5)
            g.affine_select(out=tri[:, :], in_=onesb[:, :], compare_op=ALU.is_gt, fill=0.0, base=0,
                            pattern=[[1, 128]], channel_multiplier=-1).then_inc(s["cst"], 1)
            g.iota(iota_e[:, :], pattern=[[1, E]], base=0, channel_multiplier=0,
                   allow_small_or_imprecise_dtypes=True).then_inc(s["cst"], 1)
            g.iota(first_row[:, :], pattern=[[CAP // 16, E]], base=0, channel_multiplier=0,
                   allow_small_or_imprecise_dtypes=True).then_inc(s["cst"], 1)
            g.memset(count[:, :], 0.0).then_inc(s["cst"], 1)
            g.memset(minus_half[:, :], -0.5)
            g.drain()
            g.memset(zrow[:, :, :], 0.0).then_inc(s["zrow_ready"], 1)
            g.iota(tile_no[:, :], pattern=[[0, 1]], base=0, channel_multiplier=1,
                   allow_small_or_imprecise_dtypes=True).then_inc(s["zrow_ready"], 1)
            pool.wait_ge(s["h_ready"], 1)
            g.tensor_copy(hV[:, :], hT[:, 0:N]).then_inc(s["hv_ready"], 1)

            def body(b):
                for p in range(8):
                    if p == 3 and is_batch(b, 1):
                        need(pool, "v_mm", 4 * b + 4)
                        g.tensor_copy(hV[:, :], hT[:, bass.ds((b + 1) * N, N)]).then_inc(s["hv_ready"], 1)
                    if p == 4 and is_batch(b, -1):
                        need_alone(pool, "var_ready", b)
                        g.tensor_tensor(rstd[:, :], t2[:, :], minus_half[:, :], ALU.pow).then_inc(s["pow_ready"], 1)
                    if p == 5 and is_batch(b, -1):
                        need(pool, "x1c_ready", b)
                        g.tensor_copy(x_all[:, bass.ds((b - 1) * TT, TT), :], x1c[:, :, :]).then_inc(s["x1_kept"], 1)
                    if p < 4 and is_batch(b, -2):
                        if p == 0:
                            need_alone(pool, "pos_ready", b - 1)
                        for k in (2 * p, 2 * p + 1):
                            nc.gpsimd.indirect_dma_start(
                                out=xs, out_offset=bass.IndirectOffsetOnAxis(pos[:, k:k + 1], 0),
                                in_=x1c[:, k // TOPK, :], in_offset=None).then_inc(s["scat"], 16)

            batch_loop(pool, 2, B - 1, 3, body)
            pool.wait_ge(s["scat"], 16 * B * TT * TOPK)
            g.drain().then_inc(s["a_done"], 1)
            pool.wait_ge(s["a_done"], 4)
            def clear(k):
                g.memset(qst[k][:, :, :].rearrange("q h n -> q (h n)").bitcast(fp32), 0.0)
                g.memset(kst[k][:, :, :].rearrange("q h n -> q (h n)").bitcast(fp32), 0.0)
                g.drain()
                g.memset(kst[k][MROW:MROW + NPART, :, :], 1.0)
                g.drain()

            npos = B * TT * TOPK
            pool.wait_ge(s["plan_ready"], 3)

            at = posf_all[:, :].rearrange("q (n o) -> q n o", o=1)
            g.tensor_tensor(shift[:, :, :], shift[:, :, :], delta[:, :].rearrange("q (o e) -> q o e", o=1).to_broadcast([128, npos, E]), ALU.mult)
            g.drain()
            w = E // 2
            while w:
                g.tensor_tensor(shift[:, :, 0:w], shift[:, :, 0:w], shift[:, :, w:2 * w], ALU.add)
                g.drain()
                w //= 2
            g.tensor_tensor(at, at, shift[:, :, 0:1], ALU.add)
            g.drain()
            g.tensor_copy(pos_all[:, :], posf_all[:, :])
            g.drain()
            for k in range(2):
                clear(k)
            g.memset(zst[:, :, :], 0.0)
            g.drain()
            g.memset(v32[:, :, :, :, :], 0.0)
            g.drain()
            g.memset(v32[:, :, :, :, DH1:DH1 + 1], 1.0).then_inc(s["cleared"], 1)
            pool.wait_ge(s["wB_ready"], NT)
            clear(2)
            g.drain().then_inc(s["cleared"], 1)
            pool.wait_ge(s["ys_out"], 16 * NT)

            def outputs(b):
                if has(b, 4):
                    g.tensor_copy(posc[:, :], pos_all[:, bass.ds((b + 4) * TT * TOPK, TT * TOPK)]).then_inc(s["posc_ready"], 1)
                    need_alone(pool, "posc_ready", b + 5)
                    need_alone(pool, "comb_done", b + 4)
                    for n in range(TT * TOPK):
                        g.indirect_dma_start(out=yk[:, n, :], out_offset=None, in_=ys,
                                             in_offset=bass.IndirectOffsetOnAxis(posc[:, n:n + 1], 0)).then_inc(s["yk_in"], 16)
                if has(b, -1):
                    need(pool, "x3_ready", b)
                    g.tensor_copy(x_all[:, bass.ds((b - 1) * TT, TT), :], x3c[:, :, :]).then_inc(s["x3_kept"], 1)
                if has(b, 3):
                    need(pool, "x2_ready", b + 4)
                    g.tensor_tensor(x_all[:, bass.ds((b + 3) * TT, TT), :], x2c[:, :, :],
                                    bo1[:, :].rearrange("q (o d) -> q o d", o=1).to_broadcast([128, TT, D]), ALU.add).then_inc(s["x2_kept"], 1)
                if has(b, 4):
                    need(pool, "yk_in", 16 * TT * TOPK * (b + 5))
                    g.tensor_copy(gcur[:, :], gate_all[:, bass.ds(b + 4, 1), :].rearrange("q o k -> q (o k)"))
                    g.drain()
                    g.tensor_tensor(yk[:, :, :], yk[:, :, :], gcur[:, :].rearrange("q (n o) -> q n o", o=1).to_broadcast([128, TT * TOPK, D]), ALU.mult)
                    g.drain()
                    y4 = yk[:, :, :].rearrange("q (i k) d -> q i k d", i=TT)
                    g.tensor_tensor(y4[:, :, 0:2, :], y4[:, :, 0:2, :], y4[:, :, 2:4, :], ALU.add)
                    g.drain()
                    g.tensor_tensor(acc, y4[:, :, 0, :], y4[:, :, 1, :], ALU.add)
                    g.drain()
                    g.tensor_tensor(acc, acc, x_all[:, bass.ds((b + 4) * TT, TT), :], ALU.add).then_inc(s["comb_done"], 1)

            pool.sem_inc(s["x3_kept"], 1)
            for b in range(-4, 1):
                outputs(b)
            with pool.Fori(1, B - 4) as b:
                outputs(b)
            for b in range(B - 4, B + 1):
                outputs(b)

        @block.tensor
        def _(pe):
            mm = nc.tensor.matmul
            pe.wait_ge(s["w_in"], 48)

            def qk(b, p, n, j):
                need(pe, "q_ev", n)
                need(pe, "k_ev", 2 * n)
                need(pe, "v_ev", j)
                c = n // 8 if isinstance(n, int) else (b if p == 0 else b + 1)
                r = (p + 7) % 8
                tok = hT[:, bass.ds(c * N, N)] if not isinstance(c, int) else hT[:, c * N:(c + 1) * N]
                mm(J[:, 0:N], wg[:, r * 128:(r + 1) * 128], tok, start=True, stop=True)
                mm(J[:, N:2 * N], wg[:, H * DH + r * 128:H * DH + (r + 1) * 128], tok, start=True, stop=True).then_inc(s["qk_mm"], 1)

            def vproj(nqk, nv, half, jt):
                need(pe, "q_ev", nqk)
                need(pe, "k_ev", 2 * nqk)
                need(pe, "v_ev", nv)
                c0 = 2 * H * DH + half * 512
                mm(J[:, :], hV[:, jt * 128:(jt + 1) * 128], wg[:, c0:c0 + 512], start=True, stop=True).then_inc(s["v_mm"], 1)

            for c in range(NCH + 1):
                if c < NCH:
                    if c % 2 == 0:
                        pe.wait_ge(s[f"xT_in{c // 2}"], 16)
                    if c >= 2:
                        pe.wait_ge(s["hA_act"], c - 1)
                    mm(bank[c % 2][:, :], w1[:, :], hT[:, c * 512:(c + 1) * 512], start=True, stop=True).then_inc(s["hA_mm"], 1)
                if c >= 1:
                    pe.wait_ge(s["hA_act"], c)
                    if c >= 3:
                        pe.wait_ge(s["h_ready"], c - 2)
                    mm(bank[2 + c % 2][:, :], w2[:, :], h1[:, (c - 1) % 2, :], start=True, stop=True).then_inc(s["hB_mm"], 1)
                if c >= 2:
                    if c == 2:
                        pe.wait_ge(s["wg_in"], 16)
                        pe.wait_ge(s["h_ready"], 1)
                    qk(0, c - 1, c - 2, 0)
            pe.wait_ge(s["cst"], 5)
            pe.wait_ge(s["rmat_ready"], 1)
            mm(M[:, 0:E], ones[:, :], ksq[:, :], start=True, stop=True).then_inc(s["ksq_ready"], 1)
            pe.wait_ge(s["rest_in"], 96)
            pe.wait_ge(s["hv_ready"], 1)
            for jt in range(TT):
                vproj(7, jt, 0, jt)

            def body(b):
                for p in range(8):
                    par, par1 = p % 2, (p - 1) % 2
                    if is_pair(b, p, 0):
                        need(pe, "q_ev", pair(b, p, 1))
                        need(pe, "k_ev", 2 * pair(b, p, 1))
                        for it, bk in ((0, S0), (1, S1)):
                            w = N - WINDOW if it == 0 else N
                            need(pe, "shifted_ready", 4 * pair(b, p) - 2 * (1 - it) if not isinstance(b, int) or 8 * b + p > 0 else 0)
                            mm(bk[:, 0:2 * w].rearrange("q (h j) -> q h j", h=2), qT[:, p, it * 128:(it + 1) * 128],
                               kT[:, p, :, 0:w], start=True, stop=True).then_inc(s["scores"], 1)
                    if is_pair(b, p, 7):
                        nv = 2 + 4 * b + (0, 0, 1, 2, 2, 2, 3, 4)[p]
                        qk(b, p, pair(b, p, 7), nv)
                    if is_batch(b, -1):
                        after_attention(b, p)
                    if is_pair(b, p, -1):
                        for h, bk, ev in ((0, PTA, "ptA_ev"), (1, PTB, "ptB_ev")):
                            need(pe, "pn_ready", 4 * pair(b, p) - 2 * (1 - h))
                            need(pe, ev, pair(b, p, -1))
                            for jt in range(TT):
                                for it in range(TT):
                                    c0 = (N if jt == 0 else 0) + it * 128
                                    last = nc.tensor.transpose(bk[:, c0:c0 + 128], P[:, par1, it, h, jt * 128:(jt + 1) * 128], ident[:, :])
                            last.then_inc(s["pt_mm"], 1)
                    if is_pair(b, p, -2):
                        r = (p - 2) % 8
                        need(pe, "ptA_ev", pair(b, p, -1))
                        need(pe, "ptB_ev", pair(b, p, -1))
                        need(pe, "ot_ev", pair(b, p, -2))
                        bb = b - 1 if p < 2 else b
                        need(pe, "v_ev", 4 * bb + (2 if r < 4 else 4))
                        for h in range(2):
                            mm(OTB[64 * h:64 * h + 64, 0:N], V[:, 0, r * 128 + 64 * h:r * 128 + 64 * h + 64], PT[:, par, h, N:2 * N], start=True, stop=False)
                        for h in range(2):
                            last = mm(OTB[64 * h:64 * h + 64, WINDOW:N], V[:, 1, r * 128 + 64 * h:r * 128 + 64 * h + 64], PT[:, par, h, WINDOW:N], start=False, stop=True)
                        last.then_inc(s["pv_mm"], 1)
                    if p in (1, 2) and is_batch(b, 0):
                        vproj(pair(b, p, 8) if is_pair(b, p, 7) else 8 * B, 4 * b + 2 + (p - 1), 1, p - 1)
                    if p in (5, 6) and is_batch(b, 1):
                        if p == 5:
                            need(pe, "hv_ready", b + 2)
                        vproj(pair(b, p, 8) if is_pair(b, p, 7) else 8 * B, 4 * b + 4 + (p - 5), 0, p - 5)
                    if is_pair(b, p, -3):
                        r = (p - 3) % 8
                        need(pe, "ot_ev", pair(b, p, -2))
                        if r == 0:
                            need(pe, "yT_ev", b)
                        mm(Y[:, 0:N], wo[:, r, :], OT[:, par1, :], start=(r == 0), stop=(r == 7)).then_inc(s["wo_mm"], 1)
                    if p == 5 and is_batch(b, -1):
                        need(pe, "x1T_ready", b)
                        for it in range(TT):
                            last = mm(M[:, it * E:(it + 1) * E], x1T[:, it * 128:(it + 1) * 128], rmat[:, :], start=True, stop=True)
                        last.then_inc(s["m_l"], 1)

            def after_attention(b, p):
                if p == 3:
                    need(pe, "yT_ev", b)
                    need(pe, "pos_ready", b - 1)
                    for it in range(TT):
                        last = nc.tensor.transpose(M[:, it * D:(it + 1) * D], yT[:, it * 128:(it + 1) * 128], ident[:, :])
                    last.then_inc(s["m_y"], 1)
                if p == 5:
                    need(pe, "x1c_ready", b)
                    for it in range(TT):
                        last = nc.tensor.transpose(M[:, it * 128:(it + 1) * 128], x1c[:, it, :], ident[:, :])
                    last.then_inc(s["m_x"], 1)
                if p == 7:
                    need(pe, "mask_ready", b)
                    mm(M[:, 0:E], tri[:, :], mask[:, 0, :], start=True, stop=True)
                    mm(M[:, E:2 * E], tri[:, :], mask[:, 1, :], start=True, stop=False)
                    mm(M[:, E:2 * E], onesb[:, :], mask[:, 0, :], start=False, stop=True)
                    mm(M[:, 2 * E:3 * E], onesb[:, :], mask[:, 0, :], start=True, stop=False)
                    mm(M[:, 2 * E:3 * E], onesb[:, :], mask[:, 1, :], start=False, stop=True).then_inc(s["m_r"], 1)

            batch_loop(pe, 2, B - 1, 2, body)
            pe.drain().then_inc(s["a_done"], 1)
            pe.wait_ge(s["a_done"], 4)

            def rows_in(n, par, loads):
                need(pe, f"xg_in{par}", loads)
                need(pe, "xgT_ready", n)
                for k in range(2):
                    last = nc.tensor.transpose(TI[:, k * 128:(k + 1) * 128], xg[:, par, k, :], ident[:, :])
                last.then_inc(s["tin_mm"], 1)

            rows_in(0, 0, 16)
            pe.wait_ge(s["cw_in"], 128)
            for k in range(4):
                last = mm(MIS[1][:, k * D:(k + 1) * D], lora_a[:, k, :], lora_b[:, k, :], start=True, stop=True)
            last.then_inc(s["lora_mm"], 1)

            def tiles(i):
                for p in range(2):
                    n, q = 2 * i + p, 1 - p
                    if is_tile(i, p, 0):
                        need(pe, "xgT_ready", n + 1)
                        need(pe, "wA_ready", n + 1)
                        need(pe, "hid_ready", 4 * n - 4)
                        for f in range(FC):
                            mm(UP[p][:, f * GT:(f + 1) * GT], wA[:, p, f * 128:(f + 1) * 128], xgT[:, p, :], start=True, stop=True).then_inc(s["up_mm"], 1)
                    if is_tile(i, p, 1):
                        rows_in(n + 1, q, 16 * i + 16 * (p + 1))
                    if is_tile(i, p, -1):
                        need(pe, "hid_ready", 4 * n)
                        need(pe, "wB_ready", n)
                        need(pe, "yTe_ready", n - 1)
                        for f in range(FC):
                            last = mm(DN[:, 0:GT], wB[:, q, f * D:(f + 1) * D], hid[:, q, f, :], start=(f == 0), stop=(f == FC - 1))
                        last.then_inc(s["dn_mm"], 1)
                    if is_tile(i, p, -2):
                        need(pe, "yTe_ready", n - 1)
                        need(pe, "yrow_ready", n - 2)
                        for k in range(2):
                            last = nc.tensor.transpose(TO[:, k * D:(k + 1) * D], yTe[:, p, k * 128:(k + 1) * 128], ident[:, :])
                        last.then_inc(s["tout_mm"], 1)

            batch_loop(pe, 2, NT // 2 - 1, 2, tiles)

            pe.wait_ge(s["c_set"], 1)
            pe.wait_ge(s["cleared"], 2)

            def attention(b, par):
                nxt = (par + 1) % 3
                for p in range(8):
                    if has(b, 0):
                        if p % 4 == 0:
                            need(pe, "m_in", 16 * NPART * (2 * b + (p // 4 + 1)))
                        need(pe, "exps1", 8 * b + p)
                        for k in range(2):
                            for jt in range(TT):
                                last = mm(ST[:, (2 * k + jt) * N:(2 * k + jt + 1) * N], kst[par][:, 2 * p + k, jt * 128:(jt + 1) * 128],
                                          qst[par][:, 2 * p + k, :], start=True, stop=True)
                        last.then_inc(s["st_full"], 1)
                    if has(b, 1):
                        if p == 0:
                            need(pe, "stk", 16 * NSTK * (b + 2))
                        for k in range(2):
                            need(pe, "max_done", H1 * (b + 1) + (2 * p + k - 2))
                            for it in range(TT):
                                last = mm(SB[(nxt + 2 * p + k) % 3][:, it * N:(it + 1) * N], qst[nxt][:, 2 * p + k, it * 128:(it + 1) * 128],
                                          kst[nxt][:, 2 * p + k, :], start=True, stop=True)
                            last.then_inc(s["s_full"], 1)
                    off, j = quad(b, p)
                    if p % 2 == 0 and has(b, off):
                        need(pe, "exps1", 8 * b + p)
                        need(pe, "o_free", 4 * b + (p // 2 - 1))
                        vpar = par if off == 0 else (par + 2) % 3
                        for jt in range(TT):
                            for r in range(4):
                                hd = 4 * j + r
                                last = mm(OB[32 * r:32 * r + 32, 0:N], v32[:, vpar, jt, hd, :], pc[:, hd // 2 % 4, r % 2, jt, :],
                                          start=(jt == 0), stop=(jt == TT - 1))
                        last.then_inc(s["pv_full"], 1)
                    if p == 7 and has(b, -1):
                        gates(b, GB)
                    if p % 2 == 1 and has(b, off):
                        use = TOS[(p - 1) // 2]
                        need_free(pe, b, use)
                        need(pe, "o_free", 4 * b + (p - 1) // 2)
                        for it in range(TT):
                            last = nc.tensor.transpose(shared(use)[:, it * 128:(it + 1) * 128], oTc[:, it * 128:(it + 1) * 128], ident[:, :])
                        last.then_inc(s[f"full{use[0]}"], 1)
                    if p == 0 and has(b, 2):
                        need_free(pe, b, QK)
                        need_free(pe, b, TO3)
                        mm(shared(QK)[:, 0:N], cw[:, 0, :], x2T[:, (par + 2) % 3, :], start=True, stop=True)
                        mm(shared(QK)[:, N:2 * N], cw[:, 1, :], x2T[:, (par + 2) % 3, :], start=True, stop=True).then_inc(s["full0"], 1)
                    if p == 1 and has(b, 0):
                        maxima_T(b, TMB, 1, 2 * b + 2)
                    if p == 2 and has(b, -1):
                        need_free(pe, b, TOT)
                        for it in range(TT):
                            last = nc.tensor.transpose(shared(TOT)[:, it * 128:(it + 1) * 128], otok[:, it, :], ident[:, :])
                        last.then_inc(s["full1"], 1)
                    if p == 2 and has(b, 1):
                        need_free(pe, b, VP)
                        for jt in range(TT):
                            last = mm(shared(VP)[:, jt * D:(jt + 1) * D], x2T[:, nxt, jt * 128:(jt + 1) * 128], cw[:, 2, :], start=True, stop=True)
                        last.then_inc(s["full0"], 1)
                    if p == 3 and has(b, -1):
                        need_free(pe, b, WO)
                        need_free(pe, b, TOT, 1)
                        for it in range(TT):
                            last = mm(shared(WO)[:, it * D:(it + 1) * D], oT[:, it * 128:(it + 1) * 128], cw[:, 3, :], start=True, stop=True)
                        last.then_inc(s["full0"], 1)
                    if p == 4 and has(b, 1):
                        maxima_T(b, TMA, 0, 2 * b + 3)
                    if p == 5:
                        need_free(pe, b, TX)
                        if has(b, 3):
                            need(pe, "x2_ready", b + 4)
                            for it in range(TT):
                                last = nc.tensor.transpose(shared(TX)[:, it * 128:(it + 1) * 128], x2c[:, it, :], ident[:, :])
                        if has(b, -1):
                            need(pe, "x3_ready", b)
                            for it in range(TT):
                                last = nc.tensor.transpose(shared(TX)[:, N + it * 128:N + (it + 1) * 128], x3c[:, it, :], ident[:, :])
                        last.then_inc(s["full1"], 1)
                    if p == 6 and has(b, -1):
                        need(pe, "scan_done", b)
                        need_free(pe, b, TX, 1)
                        gates(b, GA)

            def maxima_T(b, use, half, n):
                need_free(pe, b, use)
                need_alone(pe, "nm_ready", n)
                for it in range(TT):
                    last = nc.tensor.transpose(shared(use).bitcast(bf16)[0:NPART * H1 // 2, it * 128:(it + 1) * 128],
                                               nmx[:, it, half, :, :].rearrange("q a h -> q (a h)"), identb[:, :])
                last.then_inc(s[f"full{use[0]}"], 1)

            def gates(b, use):
                need_free(pe, b, use)
                for n, k in enumerate((0, 1) if use == GA else (2,)):
                    mm(shared(use)[:, n * N:(n + 1) * N], gw[:, k, :], x3T[:, :], start=True, stop=False)
                    last = mm(shared(use)[:, n * N:(n + 1) * N], gu[:, k, :], c2[:, :], start=False, stop=True)
                if use == GB:
                    for it in range(TT):
                        last = mm(shared(use)[:, N + it * D:N + (it + 1) * D], x3T[:, it * 128:(it + 1) * 128], gw[:, 3, :], start=True, stop=True)
                last.then_inc(s[f"full{use[0]}"], 1)

            attention_loop(pe, attention)
            pe.wait_ge(s["scan_done"], B + 1)
            for it in range(TT):
                last = mm(SB[0][:, it * D:(it + 1) * D], c2[:, it * 128:(it + 1) * 128], gu[:, 3, :], start=True, stop=True)
            last.then_inc(s["state_mm"], 1)

        @block.scalar
        def _(act):
            sc = nc.scalar
            act.wait_ge(s["w_in"], 48)

            def qk_evac(b, p, n):
                r = (p + 7) % 8
                need(act, "qk_mm", n + 1)
                sc.activation(qT[:, r, :], J[:, 0:N], ACT.Identity, bias=cols[:, 3 + r:4 + r]).then_inc(s["q_ev"], 1)
                for h in range(2):
                    sc.activation(kT[64 * h:64 * h + 64, r, h, :], J[64 * h:64 * h + 64, N:2 * N], ACT.Identity,
                                  bias=cols[64 * h:64 * h + 64, 3 + PAIRS + r:4 + PAIRS + r]).then_inc(s["k_ev"], 1)

            for c in range(NCH + 1):
                if c < NCH:
                    act.wait_ge(s["hA_mm"], c + 1)
                    if c >= 2:
                        act.wait_ge(s["hB_mm"], c - 1)
                    sc.activation(h1[:, c % 2, :], bank[c % 2][:, :], ACT.Silu, bias=cols[:, 0:1]).then_inc(s["hA_act"], 1)
                if c >= 1:
                    act.wait_ge(s["hB_mm"], c)
                    sc.activation(hT[:, (c - 1) * 512:c * 512], bank[2 + c % 2][:, :], ACT.Identity, bias=cols[:, 1:2]).then_inc(s["h_ready"], 1)
                if c == 2:
                    act.wait_ge(s["cst2"], 2)
                if c >= 2:
                    qk_evac(0, c - 1, c - 2)

            def body(b):
                for p in range(8):
                    par, par1 = p % 2, (p - 1) % 2
                    if is_pair(b, p, 0):
                        need(act, "pt_mm", 2 * pair(b, p) - 2 if not isinstance(b, int) or 8 * b + p > 1 else 0)
                        for it in range(TT):
                            for h in range(2):
                                n = 2 * h + it
                                w = N - WINDOW if it == 0 else N
                                need(act, "shifted_ready", 4 * pair(b, p) + (2 * it + h + 1))
                                last = sc.activation(P[:, par, it, h, 0:w], shifted[:, par, it, h, 0:w], ACT.Exp, scale=-1.0,
                                                     bias=least[:, par, n:n + 1], accum_out=rowsum[:, par, n:n + 1])
                        last.then_inc(s["exps"], 1)
                    if is_pair(b, p, 7):
                        qk_evac(b, p, pair(b, p, 7))
                    if p == 5 and is_batch(b, -1):
                        need(act, "m_x", b)
                        sc.activation(x1T[:, :], M[:, 0:N], ACT.Copy).then_inc(s["x1T_ready"], 1)
                        for it in range(TT):
                            sc.activation(sqj[:, :], x1c[:, it, :], ACT.Square, accum_out=xsq[:, it:it + 1]).then_inc(s["xsq_ready"], 1)
                            need(act, "xsq_ready", 2 * b - 1 + it)
                    if is_pair(b, p, -1):
                        need(act, "pt_mm", 2 * pair(b, p))
                        need(act, "pv_mm", pair(b, p, -2))
                        sc.activation(PT[:, par1, 1, WINDOW:2 * N], PTB[:, WINDOW:2 * N], ACT.Copy).then_inc(s["ptB_ev"], 1)
                    if is_pair(b, p, -2):
                        need(act, "pv_mm", pair(b, p, -1))
                        need(act, "wo_mm", pair(b, p, -3))
                        sc.activation(OT[:, par, :], OTB[:, 0:N], ACT.Copy).then_inc(s["ot_ev"], 1)
                    if p == 2 and is_batch(b, -1):
                        need(act, "wo_mm", 8 * b)
                        need(act, "m_y", b - 1)
                        sc.activation(yT[:, :], Y[:, 0:N], ACT.Identity, bias=cols[:, 2:3]).then_inc(s["yT_ev"], 1)
                    if p == 7 and is_batch(b, -1):
                        need(act, "top_ready", b)
                        for it in range(TT):
                            last = sc.activation(wexp[:, it, :], top[:, it, 0:TOPK], ACT.Exp, bias=ntop[:, it:it + 1], accum_out=wsum[:, it:it + 1])
                        last.then_inc(s["exp_w"], 1)

            batch_loop(act, 2, B - 1, 2, body)
            act.drain().then_inc(s["a_done"], 1)
            act.wait_ge(s["a_done"], 4)

            def tiles(i):
                for p in range(2):
                    n, q = 2 * i + p, 1 - p
                    if is_tile(i, p, 0):
                        need(act, "dn_mm", n - 1)
                        for f in range(FC):
                            need(act, "up_mm", 4 * n + (2 * (f // 2) + 2))
                            sc.activation(hid[:, p, f, :], UP[p][:, f * GT:(f + 1) * GT], ACT.Gelu, bias=wA[:, p, F + f:F + f + 1]).then_inc(s["hid_ready"], 1)
                    if is_tile(i, p, -1):
                        need(act, "dn_mm", n)
                        need(act, "tout_mm", n - 2)
                        sc.activation(yTe[:, q, :], DN[:, 0:GT], ACT.Identity, bias=wB[:, q, FC * D:FC * D + 1]).then_inc(s["yTe_ready"], 1)

            batch_loop(act, 2, NT // 2 - 1, 2, tiles)

            def attention(b, par):
                for p in range(8):
                    off, j = quad(b, p)
                    if has(b, 0):
                        need(act, "st_full", 8 * b + p + 1)
                        need(act, "pv_full", 4 * b + (p // 2 - 1))
                        sc.activation(pc[:, p % 4, :, :, :].rearrange("q h j n -> q (h j n)"), ST, ACT.Exp, scale=SCALE1).then_inc(s["exps1"], 1)
                    if p % 2 == 0 and has(b, off):
                        need(act, "pv_full", 4 * b + p // 2)
                        if p > 0 and (p > 2 or has(b, -1)):
                            need_full(act, b, TOS[p // 2 - 1])
                        if p == 0:
                            need(act, "full0", tally[0].before(b))
                        sc.activation(oTc[:, :], OB[:, 0:N], ACT.Copy).then_inc(s["o_free"], 1)
                    if p == 0 and has(b, 2):
                        need_full(act, b, QK)
                        need(act, "qkd_out", 16 * (b + 2))
                        sc.activation(parts[:, 0, :], shared(QK)[:, :], ACT.Copy).then_inc(s["a1_ready"], 1)
                    if p == 2 and has(b, -1):
                        need_full(act, b, TOT)
                        sc.activation(oT[:, :], shared(TOT)[:, 0:N], ACT.Copy).then_inc(s["free1"], 1)
                    if p == 2 and has(b, 1):
                        need_full(act, b, VP)
                        for jt in range(TT):
                            last = sc.activation(v32[:, (par + 1) % 3, jt, :, 0:DH1], shared(VP)[:, jt * D:(jt + 1) * D].rearrange("q (h d) -> q h d", h=H1), ACT.Copy)
                        last.then_inc(s["free0"], 1)
                    if p == 1 and has(b, 0):
                        maxima_row(b, TMB, 2 * b + 1)
                    if p == 4 and has(b, 1):
                        maxima_row(b, TMA, 2 * b + 2)
                    if p == 5:
                        need_full(act, b, TX)
                        if has(b, 3):
                            last = sc.activation(x2T[:, par, :], shared(TX)[:, 0:N], ACT.Copy)
                        if has(b, -1):
                            last = sc.activation(x3T[:, :], shared(TX)[:, N:2 * N], ACT.Copy)
                        last.then_inc(s["free1"], 1)
                    if p == 6 and has(b, -1):
                        need_full(act, b, GA)
                        sc.activation(tf[:, :], shared(GA)[:, 0:N], ACT.Tanh, bias=gcol[:, 0:1], scale=0.5)
                        sc.activation(ti[:, :], shared(GA)[:, N:2 * N], ACT.Tanh, bias=gcol[:, 1:2], scale=0.5).then_inc(s["free0"], 1)
                    if p == 7 and has(b, -1):
                        need_full(act, b, GB)
                        sc.activation(tg[:, :], shared(GB)[:, 0:N], ACT.Tanh, bias=gcol[:, 2:3]).then_inc(s["gate_act"], 1)
                        sc.activation(xo_all[:, bass.ds((b - 1) * TT, TT), :].rearrange("q i d -> q (i d)"), shared(GB)[:, N:2 * N], ACT.Copy).then_inc(s["free1"], 1)

            def maxima_row(b, use, before):
                need_full(act, b, use)
                need(act, "m_in", 16 * NPART * before)
                sc.activation(mrow[:, :], shared(use).bitcast(bf16)[0:NPART * H1 // 2, 0:N], ACT.Copy).then_inc(s[f"free{use[0]}"], 1)

            attention_loop(act, attention)
            for c in range(B // 4):
                act.wait_ge(s["h_pre"], c + 1)
                sc.activation(xo_all[:, 8 * c:8 * c + 8, :], xo_all[:, 8 * c:8 * c + 8, :], ACT.Tanh).then_inc(s["h_act"], 1)

        @block.vector
        def _(dve):
            v = nc.vector
            dve.wait_ge(s["rest_in"], 96)
            v.tensor_tensor(ksq[:, :], keysT[:, :], keysT[:, :], ALU.mult)
            v.scalar_tensor_tensor(rmat[:, :], keysT[:, :], 2.0, rwT[:, :], ALU.mult, ALU.add)
            v.drain()
            dve.wait_ge(s["cst"], 9)
            v.tensor_scalar(first_row[:, :], first_row[:, :], 16.0, None, ALU.mult).then_inc(s["rmat_ready"], 1)
            dve.wait_ge(s["ksq_ready"], 1)
            v.tensor_tensor(rconst[:, :], rconst[:, :], M[:, 0:E], ALU.subtract)
            v.drain()

            for jt in range(TT):
                dve.wait_ge(s["v_mm"], jt + 1)
                v.tensor_tensor(V[:, jt, 0:512], J[:, :], bv[:, 0:512], ALU.add).then_inc(s["v_ev"], 1)

            def body(b):
                for p in range(8):
                    par, par1 = p % 2, (p - 1) % 2
                    if is_pair(b, p, -1):
                        need(dve, "exps", pair(b, p))
                        v.reciprocal(rinv[:, par1, :], rowsum[:, par1, :])
                        v.drain()
                        for h in range(2):
                            for it in range(TT):
                                n = 2 * h + it
                                w = N - WINDOW if it == 0 else N
                                x = P[:, par1, it, h, 0:w]
                                v.tensor_scalar(x, x, rinv[:, par1, n:n + 1], None, ALU.mult).then_inc(s["pn_ready"], 1)
                    if is_pair(b, p, 0):
                        for it, bk in ((0, S0), (1, S1)):
                            w = N - WINDOW if it == 0 else N
                            need_alone(dve, "scores", 2 * pair(b, p) + (it + 1))
                            for h in range(2):
                                n = 2 * h + it
                                v.tensor_tensor_reduce(out=shifted[:, par, it, h, 0:w], in0=bk[:, h * w:(h + 1) * w],
                                                       in1=band[:, it, 0:w], scale=-SCALE0, scalar=3.0e38, op0=ALU.add, op1=ALU.min,
                                                       accum_out=least[:, par, n:n + 1]).then_inc(s["shifted_ready"], 1)
                    if p == 6 and is_batch(b, -1):
                        need(dve, "m_l", b)
                        need(dve, "xsq_ready", 2 * b)
                        need(dve, "exp_w", b - 1)
                        for it in range(TT):
                            v.scalar_tensor_tensor(lg[:, it, :], M[:, it * E:(it + 1) * E], xsq[:, it:it + 1], rconst[:, :], ALU.subtract, ALU.add)
                        v.drain()
                        for it in range(TT):
                            v.max(top[:, it, :], lg[:, it, :])
                        v.drain()
                        for it in range(TT):
                            v.max_index(topi[:, it, :], top[:, it, :], lg[:, it, :])
                        v.tensor_scalar(ntop[:, :], top[:, :, 0], -1.0, None, ALU.mult).then_inc(s["top_ready"], 1)
                    if is_pair(b, p, -1):
                        need(dve, "pt_mm", 2 * pair(b, p) - 1)
                        need(dve, "pv_mm", pair(b, p, -2))
                        v.tensor_copy(PT[:, par1, 0, WINDOW:2 * N], PTA[:, WINDOW:2 * N]).then_inc(s["ptA_ev"], 1)
                    if p in (1, 2) and is_batch(b, 0):
                        need(dve, "v_mm", 4 * b + 2 + p)
                        v.tensor_tensor(V[:, p - 1, 512:1024], J[:, :], bv[:, 512:1024], ALU.add).then_inc(s["v_ev"], 1)
                    if p in (5, 6) and is_batch(b, 1):
                        need(dve, "v_mm", 4 * b + p)
                        v.tensor_tensor(V[:, p - 5, 0:512], J[:, :], bv[:, 0:512], ALU.add).then_inc(s["v_ev"], 1)
                    if not is_batch(b, -1):
                        continue
                    if p == 3:
                        need(dve, "m_y", b)
                        need(dve, "xsq_ready", 2 * b - 2)
                        v.tensor_tensor(res[:, :, :], M[:, 0:N].rearrange("q (i d) -> q i d", i=TT), x_all[:, bass.ds((b - 1) * TT, TT), :], ALU.add)
                        v.drain()
                        moments(v, res, TT, st, mv)
                        v.tensor_scalar(nhalf[:, :], mv[:, :, 1], EPS, -0.5, ALU.add, ALU.mult)
                        v.tensor_scalar(t2[:, :], mv[:, :, 1], EPS, None, ALU.add).then_inc(s["var_ready"], 1)
                    if p == 4:
                        need(dve, "pow_ready", b)
                        for it in range(TT):
                            v.scalar_tensor_tensor(t2[:, it:it + 1], rstd[:, it:it + 1], nhalf[:, it:it + 1], rstd[:, it:it + 1], ALU.mult, ALU.mult)
                        v.drain()
                        v.scalar_tensor_tensor(rstd[:, :], t2[:, :], 1.5, rstd[:, :], ALU.add, ALU.mult)
                        v.drain()
                        need(dve, "scat", 16 * TT * TOPK * (b - 1))
                        need(dve, "x1_kept", b - 1)
                        for it in range(TT):
                            last = v.tensor_scalar(x1c[:, it, :], res[:, it, :], mv[:, it, 0:1], rstd[:, it:it + 1], ALU.subtract, ALU.mult)
                        last.then_inc(s["x1c_ready"], 1)
                    if p == 6:
                        v.drain()
                        v.tensor_copy(topif[:, :, :], topi[:, :, :])
                        v.drain()
                        for it in range(TT):
                            for k in range(TOPK):
                                v.tensor_scalar(hot[:, it, k, :], iota_e[:, :], topif[:, it, k:k + 1], None, ALU.is_equal)
                        v.drain()
                        v.tensor_reduce(out=chosen[:, :, :], in_=hot[:, :, :, :].rearrange("q i k e -> q i e k"), axis=mybir.AxisListType.X, op=ALU.add)
                        v.drain()
                        v.tensor_copy(mask[:, :, :], chosen[:, :, :]).then_inc(s["mask_ready"], 1)
                    if p == 7:
                        need(dve, "m_r", b)
                        v.tensor_tensor(rank[:, :, :], M[:, 0:2 * E].rearrange("q (i e) -> q i e", i=TT), count[:, :].rearrange("q (o e) -> q o e", o=1).to_broadcast([128, TT, E]), ALU.add)
                        v.drain()
                        v.tensor_tensor(rank[:, :, :], rank[:, :, :], first_row[:, :].rearrange("q (o e) -> q o e", o=1).to_broadcast([128, TT, E]), ALU.add)
                        v.tensor_tensor(count[:, :], count[:, :], M[:, 2 * E:3 * E], ALU.add)
                        v.drain()
                        need(dve, "exp_w", b)
                        v.reciprocal(wsum[:, :], wsum[:, :])
                        for it in range(TT):
                            v.tensor_tensor(junk[:, it * TOPK:(it + 1) * TOPK, :], hot[:, it, :, :],
                                            rank[:, it:it + 1, :].to_broadcast([128, TOPK, E]), ALU.mult)
                        v.drain()
                        v.tensor_reduce(out=posf[:, :], in_=junk[:, :, :], axis=mybir.AxisListType.X, op=ALU.add)
                        for it in range(TT):
                            v.tensor_scalar(gate_all[:, bass.ds(b - 1, 1), it * TOPK:(it + 1) * TOPK].rearrange("q o k -> q (o k)"), wexp[:, it, :], wsum[:, it:it + 1], None, ALU.mult)
                        v.drain()
                        v.tensor_copy(posf_all[:, bass.ds((b - 1) * TT * TOPK, TT * TOPK)], posf[:, :])
                        v.tensor_copy(pos[:, :], posf[:, :]).then_inc(s["pos_ready"], 1)

            dve.wait_ge(s["x_in"], 16)
            batch_loop(dve, 2, B - 1, 2, body)
            v.drain().then_inc(s["a_done"], 1)

            dve.wait_ge(s["zrow_ready"], 2)
            v.tensor_scalar(past[:, :], count[:, :], float(GT - 1), None, ALU.add)
            v.drain()
            v.tensor_copy(cnt_i[:, :], past[:, :])
            v.drain()
            v.tensor_scalar(cnt_i[:, :], cnt_i[:, :], GT.bit_length() - 1, None, ALU.logical_shift_right)
            v.drain()
            v.tensor_copy(ntile[:, :], cnt_i[:, :])
            v.memset(past[:, :], 1.0)
            v.drain()
            v.tensor_tensor_scan(ncum[:, :], past[:, :], ntile[:, :], 0.0, ALU.mult, ALU.add)
            v.drain()
            v.tensor_scalar(past[:, :], ncum[:, :], tile_no[:, :], None, ALU.is_le)
            v.drain()
            v.tensor_reduce(out=tile_e[:, :], in_=past[:, :], axis=mybir.AxisListType.X, op=ALU.add)
            v.tensor_tensor(skip[:, :], past[:, :], ntile[:, :], ALU.mult)
            v.drain()
            v.tensor_reduce(out=tile_s[:, :], in_=skip[:, :], axis=mybir.AxisListType.X, op=ALU.add)
            v.tensor_scalar(used[:, :], tile_e[:, :], float(E), None, ALU.is_lt)
            v.drain()
            v.tensor_tensor(tile_s[:, :], tile_no[:, :], tile_s[:, :], ALU.subtract)
            v.drain()
            v.tensor_scalar(tile_s[:, :], tile_s[:, :], float(GT), float(-DUMMY), ALU.mult, ALU.add)
            v.drain()
            v.scalar_tensor_tensor(tile_s[:, :], tile_e[:, :], float(CAP), tile_s[:, :], ALU.mult, ALU.add)
            v.tensor_scalar(plan2[:, 0:1], tile_e[:, :], float(E - 1), None, ALU.min)
            v.drain()
            v.tensor_tensor(tile_s[:, :], tile_s[:, :], used[:, :], ALU.mult)
            v.drain()
            v.tensor_scalar(plan2[:, 1:2], tile_s[:, :], float(DUMMY), None, ALU.add)
            v.tensor_tensor(skip[:, :], count[:, :], first_row[:, :], ALU.add)
            v.drain()
            v.tensor_copy(pad_at[:, :], skip[:, :])
            v.drain().then_inc(s["plan_ready"], 1)

            v.tensor_tensor(past[:, :], ncum[:, :], ntile[:, :], ALU.subtract)
            v.drain()
            v.scalar_tensor_tensor(past[:, :], past[:, :], float(GT), first_row[:, :], ALU.mult, ALU.subtract)
            v.drain()
            v.tensor_copy(delta[:, 0:1], past[:, 0:1])
            v.tensor_tensor(delta[:, 1:E], past[:, 1:E], past[:, 0:E - 1], ALU.subtract).then_inc(s["plan_ready"], 1)

            dve.wait_ge(s["wall_in"], 16)
            dve.wait_ge(s["a_done"], 4)
            dve.wait_ge(s["plan_in"], 16)

            def expert_of(n):
                src = plan[0:1, 2 * n:2 * n + 1] if isinstance(n, int) else plan[0:1, bass.ds(2 * n, 1)]
                return dve.value_load(src, min_val=0, max_val=E - 1)

            def weights_A(e, par):
                v.tensor_copy(wA[:, par, :], wall[:, bass.ds(e, 1), 0:WA].rearrange("q o c -> q (o c)")).then_inc(s["wA_ready"], 1)

            def weights_B(e, par):
                v.tensor_copy(wB[:, par, :], wall[:, bass.ds(e, 1), WA:WCOLS].rearrange("q o c -> q (o c)")).then_inc(s["wB_ready"], 1)

            def rows_T(n, par):
                need(dve, "tin_mm", n + 1)
                v.tensor_copy(xgT[:, par, :], TI[:, 0:GT]).then_inc(s["xgT_ready"], 1)

            first = expert_of(0)
            weights_A(first, 0)
            rows_T(0, 0)
            weights_B(first, 0)

            v.tensor_copy(identb[:, :], ident[:, :])
            dve.wait_ge(s["cw_in"], 128)
            v.tensor_scalar(gu[:, :, :], gu[:, :, :], 0.5, None, ALU.mult)
            v.tensor_scalar(gcol[:, 0:2], gcol[:, 0:2], 0.5, None, ALU.mult)
            v.memset(c2[:, :], 0.0)
            v.drain()
            v.tensor_scalar(c2[:, :], c2[:, :], gcol[:, 3:4], 2.0, ALU.add, ALU.mult).then_inc(s["scan_done"], 1)
            dve.wait_ge(s["lora_mm"], 1)
            v.scalar_tensor_tensor(cw[:, :, :], MIS[1].rearrange("q (k d) -> q k d", k=4), LORA, cw[:, :, :], ALU.mult, ALU.add)
            v.drain().then_inc(s["c_set"], 1)
            npos = B * TT * TOPK
            v.tensor_tensor(shift[:, :, :], posf_all[:, :].rearrange("q (n o) -> q n o", o=1).to_broadcast([128, npos, E]),
                            first_row[:, :].rearrange("q (o e) -> q o e", o=1).to_broadcast([128, npos, E]), ALU.is_ge).then_inc(s["plan_ready"], 1)

            def tiles(i):
                for p in range(2):
                    n, q = 2 * i + p, 1 - p
                    if is_tile(i, p, 1):
                        e = expert_of(n + 1)
                        need(dve, "up_mm", 4 * n)
                        need(dve, "hid_ready", 4 * n)
                        weights_A(e, q)
                        rows_T(n + 1, q)
                    if is_tile(i, p, -1):
                        need(dve, "dn_mm", n)
                        need(dve, "yTe_ready", n)
                    if is_tile(i, p, 1):
                        weights_B(e, q)
                    if is_tile(i, p, -2):
                        need(dve, "tout_mm", n - 1)
                        need(dve, "ys_out", 16 * n - 48)
                        v.tensor_copy(yrow[:, p, :, :], TO[:, 0:GT].rearrange("q (a d) -> q a d", a=2)).then_inc(s["yrow_ready"], 1)

            batch_loop(dve, 2, NT // 2 - 1, 2, tiles)

            def new_state(b):
                need(dve, "gate_act", b)
                v.scalar_tensor_tensor(c2[:, :], tf[:, :], 1.0, c2[:, :], ALU.add, ALU.mult)
                v.scalar_tensor_tensor(tg[:, :], ti[:, :], 1.0, tg[:, :], ALU.add, ALU.mult)
                v.drain()
                v.scalar_tensor_tensor(c2[:, :], c2[:, :], 0.5, tg[:, :], ALU.mult, ALU.add).then_inc(s["scan_done"], 1)

            def minus_maxima(half):
                m = mx[:, :, half * H1 // 2:(half + 1) * H1 // 2]
                n = [nmx[:, :, half, k, :] for k in range(NPART)]
                v.drain()
                v.tensor_scalar(n[0], m, -1.0, None, ALU.mult)
                v.drain()
                v.scalar_tensor_tensor(mrest[:, :, :], m, -1.0, n[0], ALU.mult, ALU.subtract)
                v.drain()
                v.tensor_copy(n[1], mrest[:, :, :])
                v.drain()
                v.tensor_tensor(n[2], mrest[:, :, :], n[1], ALU.subtract).then_inc(s["nm_ready"], 1)

            def norm_tiles(b):
                first = 0 if has(b, 3) else TT
                outs = [x2c[:, it, :] for it in range(TT)] if has(b, 3) else []
                return sums[:, first:, :], outs + ([x3c[:, it, :] for it in range(TT)] if has(b, -1) else [])

            def norms_start(b):
                if has(b, 3):
                    need(dve, "comb_done", b + 4)
                if has(b, -1):
                    need_full(dve, b, WO)
                    need(dve, "x2_kept", b)
                    v.tensor_tensor(res2, shared(WO)[:, 0:N].rearrange("q (i d) -> q i d", i=TT), x_all[:, bass.ds((b - 1) * TT, TT), :], ALU.add).then_inc(s["free0"], 1)
                    v.drain()
                x, outs = norm_tiles(b)
                moments(v, x, len(outs), st2, mv2)

            def norms_end(b):
                def ready():
                    if has(b, 3):
                        need(dve, "x2_kept", b + 3)
                    if has(b, -1):
                        need(dve, "x3_kept", b)
                    else:
                        need(dve, "full1", tally[1].before(b))

                x, outs = norm_tiles(b)
                done = normalise(v, x, outs, mv2, rstd2, nh2, u2, ready)
                if has(b, 3):
                    done[TT - 1].then_inc(s["x2_ready"], 1)
                if has(b, -1):
                    done[-1].then_inc(s["x3_ready"], 1)

            def attention(b, par):
                for p in range(8):
                    if p == 0 and has(b, 0):
                        minus_maxima(1)
                    if has(b, 1):
                        for k in range(2):
                            need(dve, "s_full", H1 * (b + 1) + (2 * p + k + 1))
                            v.tensor_reduce(out=mx[:, :, 2 * p + k], in_=SB[((par + 1) + 2 * p + k) % 3].rearrange("q (i n) -> q i n", i=TT),
                                            axis=mybir.AxisListType.X, op=ALU.max).then_inc(s["max_done"], 1)
                    off, j = quad(b, p)
                    if p == 0 and has(b, 2):
                        need(dve, "a1_ready", b + 3)
                        v.tensor_tensor(rest[:, :], shared(QK)[:, :], parts[:, 0, :], ALU.subtract).then_inc(s["free0"], 1)
                        v.drain()
                        v.tensor_copy(parts[:, 1, :], rest[:, :])
                        v.drain()
                        v.tensor_tensor(parts[:, 2, :], rest[:, :], parts[:, 1, :], ALU.subtract).then_inc(s["parts_ready"], 1)
                    if p % 2 == 1 and has(b, off):
                        use = TOS[(p - 1) // 2]
                        need_full(dve, b, use)
                        o = shared(use)[:, 0:N].rearrange("q (i r c) -> q i r c", i=TT, r=4)
                        v.reciprocal(dinv[:, :, :], o[:, :, :, DH1])
                        v.drain()
                        for it in range(TT):
                            last = v.tensor_tensor(otok[:, it, 32 * j:32 * j + 32].rearrange("q (r c) -> q r c", r=4), o[:, it, :, 0:DH1],
                                                   dinv[:, it, :].rearrange("q (r o) -> q r o", o=1).to_broadcast([128, 4, DH1]), ALU.mult)
                        v.drain().then_inc(s[f"free{use[0]}"], 1)
                    if p == 3 and has(b, 1):
                        minus_maxima(0)
                    if p == 3:
                        norms_start(b)
                    if p == 4:
                        norms_end(b)
                    if p == 7 and has(b, -1):
                        new_state(b)

            attention_loop(dve, attention)
            dve.wait_ge(s["state_mm"], 1)
            need(dve, "free1", tally[1].before(B + 1))
            v.tensor_tensor(state[:, :, :], SB[0][:, 0:N].rearrange("q (i d) -> q i d", i=TT), bo2[:, :].rearrange("q (o d) -> q o d", o=1).to_broadcast([128, TT, D]), ALU.add)
            v.drain()
            for c in range(B // 4):
                xo = xo_all[:, 8 * c:8 * c + 8, :].rearrange("q (k i) d -> q k i d", i=TT)
                v.tensor_tensor(xo, xo, state[:, :, :].rearrange("q (o i) d -> q o i d", o=1).to_broadcast([128, 4, TT, D]), ALU.add).then_inc(s["h_pre"], 1)
            dve.wait_ge(s["x3_kept"], B + 1)
            for c in range(B // 4):
                dve.wait_ge(s["h_act"], c + 1)
                xs_ = x_all[:, 8 * c:8 * c + 8, :]
                v.tensor_tensor(xs_, xs_, xo_all[:, 8 * c:8 * c + 8, :], ALU.add)
                v.drain()
                moments(v, xs_, 8, st2, mv2)
                normalise(v, xs_, [xs_[:, k, :] for k in range(8)], mv2, rstd2, nh2, u2)
                v.drain().then_inc(s["fin_ready"], 1)


def laid_out(inputs):
    import numpy as np

    def c(v):
        return np.ascontiguousarray(v)

    def g(name):
        return np.asarray(inputs[name])

    def stack_T(layer, names):
        return c(np.stack([g(f"{layer}_{n}").T for n in names], 1))

    r = {}
    r["x"] = c(g("L0_attn_x").reshape(TOK, D))
    r["xT"] = c(r["x"].T)
    for dst, src in (("w1T", "attn_W1"), ("w2T", "attn_W2"), ("wgT", "attn_Wg"), ("keysT", "ffn_keys"), ("rwT", "ffn_rw")):
        r[dst] = c(g("L0_" + src).T)
    bg = g("L0_attn_bg")
    hd = H * DH
    r["colsA"] = c(np.concatenate([g("L0_attn_b1")[:, None], g("L0_attn_b2")[:, None], g("L0_attn_bo")[:, None],
                                   bg[:hd].reshape(PAIRS, 128).T, bg[hd:2 * hd].reshape(PAIRS, 128).T], 1))
    r["bvB"] = c(np.broadcast_to(bg[2 * hd:], (128, hd)))
    r["woT"] = c(g("L0_attn_Wo").T.reshape(PAIRS, 128, D).transpose(1, 0, 2))
    r["rbB"] = c(np.broadcast_to(g("L0_ffn_rb"), (128, E)))
    r["ident"] = np.eye(128, dtype=np.float32)
    w1 = g("L0_ffn_w1").transpose(2, 0, 1)
    b1 = g("L0_ffn_b1").reshape(E, FC, 128).transpose(2, 0, 1)
    w2 = g("L0_ffn_w2").transpose(0, 2, 1).reshape(E, FC, 128, D).transpose(2, 0, 1, 3).reshape(128, E, FC * D)
    b2 = g("L0_ffn_b2").T[:, :, None]
    r["wall"] = c(np.concatenate([w1, b1, w2, b2], 2))
    r["cw"] = stack_T("L1_attn", ("Wq", "Wk", "Wv", "Wo"))
    r["lora_a"] = c(np.stack([g("L1_attn_" + n) for n in ("Aq", "Ak", "Av", "Ao")], 1))
    r["lora_b"] = stack_T("L1_attn", ("Bq", "Bk", "Bv", "Bo"))
    r["gw"] = stack_T("L1_ffn", ("wf", "wi", "wc", "wo"))
    r["gu"] = stack_T("L1_ffn", ("uf", "ui", "uc", "uo"))
    r["gcol"] = c(np.stack([g("L1_ffn_" + n) for n in ("bf", "bi", "bc", "in_c")], 1))
    r["bo1"] = c(np.broadcast_to(g("L1_attn_bo"), (128, D)))
    r["bo2"] = c(np.broadcast_to(g("L1_ffn_bo"), (128, D)))
    return r


def kernel(**inputs):
    import concourse.bacc as bacc
    from concourse import mybir as my
    from concourse.bass_utils import run_bass_kernel_spmd

    arrays = {"in_" + k: v for k, v in laid_out(inputs).items()}
    nc = bacc.Bacc("TRN2", target_bir_lowering=False, num_devices=1)
    t = {k[3:]: nc.dram_tensor(k, v.shape, my.dt.float32, kind="ExternalInput").ap() for k, v in arrays.items()}
    out = nc.dram_tensor("out", (TOK, D), my.dt.float32, kind="ExternalOutput").ap()
    build(nc, t, out)
    r = run_bass_kernel_spmd(nc, [arrays], core_ids=[0])
    return r.results[0]["out"].reshape(B, N, D)
```

```python
import concourse.bass as bass
from concourse import mybir
from contextlib import ExitStack

DT = mybir.dt
fp32, bf16, i32, u32 = DT.float32, DT.bfloat16, DT.int32, DT.uint32
ACT = mybir.ActivationFunctionType
ALU = mybir.AluOpType

B, N, D = 16, 256, 128
TOK = B * N
TT = N // 128
H, DH = 16, 64
PAIRS = H // 2
WINDOW = 64
SCALE0 = DH ** -0.5
E, TOPK, F = 16, 4, 512
FC = F // 128
H1, DH1 = 16, 8
SCALE1 = DH1 ** -0.5
RANK, LORA = 16, 1.0 / 16
NPART = 3
MROW = 64
BIG = 1.0e30
EPS = 1e-5
GT = 256
CAP = TOK + GT
DUMMY = E * CAP
NT = (TOK * TOPK + E * (GT - 1)) // GT
NT += NT % 2
ROWS = DUMMY + GT
WA = F + FC
WB = FC * D + 1
WCOLS = WA + WB


def batch_loop(eng, front, end, back, body):
    for b in range(front):
        body(b)
    with eng.Fori(front, end) as b:
        body(b)
    for b in range(end, end + back):
        body(b)


class Tally:

    FULL = 3

    def __init__(self, offsets):
        self.offsets = offsets

    def before(self, b, k=0):
        if not isinstance(b, int):
            n = len(self.offsets)
            return n * b + (self.before(self.FULL) - n * self.FULL + k)
        takes_place = [(c, n, any(0 <= c + o < B for o in offs)) for c in range(-3, b + 1) for n, offs in enumerate(self.offsets)]
        return sum(t for c, n, t in takes_place if (c, n) < (b, k))


def attention_loop(eng, body):
    for b in range(-3, 3):
        body(b, b % 3)
    with eng.Fori(0, 3) as i:
        for k in range(3):
            body(3 * i + (3 + k), k)
    for b in range(B - 4, B + 2):
        body(b, b % 3)


def moments(v, x, n, stat, mv, nhalf, veps):
    for k in range(n):
        v.bn_stats(stat[:, k, :], x[:, k, :])
    v.drain()
    for k in range(n):
        v.bn_aggr(mv[:, k, :], stat[:, k, :])
    v.drain()
    v.tensor_scalar(nhalf, mv[:, 0:n, 1], EPS, -0.5, ALU.add, ALU.mult)
    return v.tensor_scalar(veps, mv[:, 0:n, 1], EPS, None, ALU.add)


def refine(v, rstd, nhalf, t2):
    v.tensor_tensor(t2, rstd, rstd, ALU.mult)
    v.drain()
    v.tensor_tensor(t2, t2, nhalf, ALU.mult)
    v.drain()
    v.scalar_tensor_tensor(rstd, t2, 1.5, rstd, ALU.add, ALU.mult)
    v.drain()


def build(nc, t, out):
    ctx = ExitStack()
    with ctx:
        def sb(name, shape, dt=fp32, c=ctx):
            return c.enter_context(nc.sbuf_tensor(name, shape, dt))

        def sem(name):
            return ctx.enter_context(nc.semaphore(name))

        psum = ctx.enter_context(nc.psum_tensor("psum", [128, 8 * 512], fp32))
        bank = [psum[:, i * 512:(i + 1) * 512] for i in range(8)]

        ident = sb("ident", [128, 128])
        x_all = sb("x_all", [128, B * TT, D])
        wall = sb("wall", [128, E, WCOLS])
        posf_all = sb("posf_all", [128, B * TT * TOPK])
        pos_all = sb("pos_all", [128, B * TT * TOPK], u32)
        gate_all = sb("gate_all", [128, B, TT * TOPK])
        count = sb("count", [128, E])

        first_row = sb("first_row", [128, E])

        cnt_i = sb("cnt_i", [128, E], i32)
        ntile = sb("ntile", [128, E])
        ncum = sb("ncum", [128, E])
        delta = sb("delta", [128, E])
        tile_no = sb("tile_no", [128, 1])
        past = sb("past", [128, E])
        skip = sb("skip", [128, E])
        tile_e = sb("tile_e", [128, 1])
        tile_s = sb("tile_s", [128, 1])
        used = sb("used", [128, 1])
        plan2 = sb("plan2", [128, 2], i32)
        pad_at = sb("pad_at", [128, E], i32)
        plan = sb("plan", [1, 256], i32)
        zrow = sb("zrow", [128, 2, D])
        minus_half = sb("minus_half", [128, 8])

        a = ExitStack()
        wg = sb("wg", [128, 3 * H * DH], c=a)
        wo = sb("wo", [128, PAIRS, D], c=a)
        w1 = sb("w1", [128, D], c=a)
        w2 = sb("w2", [128, D], c=a)
        cols = sb("cols", [128, 3 + 2 * PAIRS], c=a)
        bv = sb("bv", [128, H * DH], c=a)
        hT = sb("hT", [128, TOK], c=a)
        h1 = sb("h1", [128, 2, 512], c=a)
        hV = sb("hV", [128, N], c=a)
        qT = sb("qT", [128, PAIRS, N], c=a)
        kT = sb("kT", [128, PAIRS, 2, N], c=a)
        V = sb("V", [128, TT, H * DH], c=a)
        band = sb("band", [128, TT, N], c=a)
        shifted = sb("shifted", [128, 2, TT, 2, N], c=a)
        least = sb("least", [128, 2, 4], c=a)
        P = sb("P", [128, 2, TT, 2, N], c=a)
        rowsum = sb("rowsum", [128, 2, 4], c=a)
        rinv = sb("rinv", [128, 2, 4], c=a)
        PT = sb("PT", [128, 2, 2, 2 * N], c=a)
        OT = sb("OT", [128, 2, N], c=a)
        yT = sb("yT", [128, N], c=a)
        x1T = sb("x1T", [128, N], c=a)
        x1c = sb("x1c", [128, TT, D], c=a)
        res = sb("res", [128, TT, D], c=a)
        sqj = sb("sqj", [128, D], c=a)
        xsq = sb("xsq", [128, TT], c=a)
        st = sb("st", [128, TT, 6], c=a)
        mv = sb("mv", [128, TT, 2], c=a)
        rstd = sb("rstd", [128, TT], c=a)
        nhalf = sb("nhalf", [128, TT], c=a)
        t2 = sb("t2", [128, TT], c=a)
        veps = sb("veps", [128, TT], c=a)
        keysT = sb("keysT", [128, E], c=a)
        rwT = sb("rwT", [128, E], c=a)
        rmat = sb("rmat", [128, E], c=a)
        ksq = sb("ksq", [128, E], c=a)
        rconst = sb("rconst", [128, E], c=a)
        ones = sb("ones", [128, 128], c=a)
        onesb = sb("onesb", [128, 128], bf16, c=a)
        tri = sb("tri", [128, 128], bf16, c=a)
        iota_e = sb("iota_e", [128, E], c=a)
        lg = sb("lg", [128, TT, E], c=a)
        top = sb("top", [128, TT, 8], c=a)
        topi = sb("topi", [128, TT, 8], u32, c=a)
        topif = sb("topif", [128, TT, 8], c=a)
        ntop = sb("ntop", [128, TT], c=a)
        wexp = sb("wexp", [128, TT, TOPK], c=a)
        wsum = sb("wsum", [128, TT], c=a)
        hot = sb("hot", [128, TT, TOPK, E], c=a)
        mask = sb("mask", [128, TT, E], bf16, c=a)
        chosen = sb("chosen", [128, TT, E], c=a)
        rank = sb("rank", [128, TT, E], c=a)
        junk = sb("junk", [128, TT * TOPK, E], c=a)
        posf = sb("posf", [128, TT * TOPK], c=a)
        pos = sb("pos", [128, TT * TOPK], u32, c=a)
        a.close()

        xg = sb("xg", [128, 2, 2, D])
        xgT = sb("xgT", [128, 2, GT])
        wA = sb("wA", [128, 2, WA])
        wB = sb("wB", [128, 2, WB])
        hid = sb("hid", [128, 2, FC, GT])
        yTe = sb("yTe", [128, 2, GT])
        yrow = sb("yrow", [128, 2, 2, D])

        cw = sb("cw", [128, 4, D])
        lora_a = sb("lora_a", [RANK, 4, D])
        lora_b = sb("lora_b", [RANK, 4, D])
        gw = sb("gw", [128, 4, D])
        gu = sb("gu", [128, 4, D])
        gcol = sb("gcol", [128, 4])
        bo1 = sb("bo1", [128, D])
        bo2 = sb("bo2", [128, D])
        identb = sb("identb", [128, 128], bf16)
        spare = wall[:, :, :].rearrange("q e c -> q (e c)")
        qst = [sb("qst0", [128, H, N], bf16), sb("qst1", [128, H, N], bf16),
               spare[:, 2 * B * N:2 * B * N + H * N // 2].bitcast(bf16).rearrange("q (h n) -> q h n", h=H)]
        kst = [sb("kst0", [128, H, N], bf16), sb("kst1", [128, H, N], bf16),
               spare[:, 2 * B * N + H * N // 2:2 * B * N + H * N].bitcast(bf16).rearrange("q (h n) -> q h n", h=H)]
        shift = qst[0][:, :, :].rearrange("q h n -> q (h n)").bitcast(fp32).rearrange("q (n e) -> q n e", e=E)
        zst = sb("zst", [NPART, H, N], bf16)
        v32 = sb("v32", [128, 3, TT, H, 32])
        xo_all = spare[:, 0:B * N].rearrange("q (t d) -> q t d", d=D)
        pc = spare[:, B * N:2 * B * N].rearrange("q (s h j n) -> q s h j n", s=4, h=2, j=TT)
        yk = sb("yk", [128, TT * TOPK, D])
        posc = sb("posc", [128, TT * TOPK], u32)
        gcur = sb("gcur", [128, TT * TOPK])
        sums = sb("sums", [128, 2 * TT, D])
        acc, res2 = sums[:, 0:TT, :], sums[:, TT:2 * TT, :]
        x2c = sb("x2c", [128, TT, D])
        x2T = sb("x2T", [128, 3, N])
        parts = sb("parts", [128, NPART, 2 * N], bf16)
        rest = sb("rest", [128, 2 * N])
        mx = sb("mx", [128, TT, H])
        mrest = sb("mrest", [128, TT, H // 2])
        nmx = sb("nmx", [128, TT, 2, NPART, H // 2], bf16)
        mrow = sb("mrow", [NPART * H // 2, N], bf16)
        oTc = sb("oTc", [128, N])
        dinv = sb("dinv", [128, TT, 4])
        otok = sb("otok", [128, TT, D])
        oT = sb("oT", [128, N])
        x3c = sb("x3c", [128, TT, D])
        x3T = sb("x3T", [128, N])
        c2 = sb("c2", [128, N])
        tf = sb("tf", [128, N])
        ti = sb("ti", [128, N])
        tg = sb("tg", [128, N])
        state = sb("state", [128, TT, D])
        st2 = sb("st2", [128, 8, 6])
        mv2 = sb("mv2", [128, 4, 8, 2])
        rstd2 = sb("rstd2", [128, 4, 8])
        nh2 = sb("nh2", [128, 4, 8])
        ve2 = sb("ve2", [128, 4, 8])
        shift2 = sb("shift2", [128, 4, 8])
        u2 = sb("u2", [128, 8])

        UP = [psum[:, 0:1024], psum[:, 1024:2048]]
        TI, DN, TO = bank[4], bank[5], bank[6]
        S0, S1, PTA, PTB, OTB, J, Y, M = bank

        xs = nc.dram_tensor("xs", (ROWS, D), fp32, kind="Internal").ap()
        ys = nc.dram_tensor("ys", (NT * GT, D), fp32, kind="Internal").ap()
        qkd = nc.dram_tensor("qkd", (NPART, 128, 2 * N), bf16, kind="Internal").ap()
        plan_d = nc.dram_tensor("plan_d", (128, 2), i32, kind="Internal").ap()

        names = """w_in xT_in0 xT_in1 xT_in2 xT_in3 wg_in rest_in x_in wall_in cst cst2 went_on hA_mm hA_act hB_mm h_ready
            qk_mm q_ev k_ev v_mm v_ev hv_ready
            scores shifted_ready exps pn_ready pt_mm ptA_ev ptB_ev pv_mm ot_ev wo_mm yT_ev
            m_y var_ready pow_ready x1c_ready m_x x1T_ready m_l mask_ready m_r pos_ready xsq_ready x1_kept scat exp_w top_ready
            ksq_ready rmat_ready a_done plan_ready zrow_ready plan_out plan_in pad_in
            xg_in0 xg_in1 tin_mm xgT_ready wA_ready wB_ready up_mm hid_ready dn_mm yTe_ready tout_mm yrow_ready ys_out
            cw_in lora_mm c_set cleared st_full exps1 s_full max_done pv_full o_free full0 full1 free0 free1 a1_ready parts_ready
            qkd_out stk m_in nm_ready x2_ready x2_kept x3_ready x3_kept gate_act scan_done
            yk_in comb_done var2_ready pow2_ready posc_ready state_mm state_ready h_pre h_pre_last last_sum var3_ready pow3_ready scale_ready h_act fin_ready out_done""".split()
        s = {n: sem(n) for n in names}

        def pair(b, p, off=0):
            return 8 * b + (p + off)

        def is_pair(b, p, off):
            return 0 <= 8 * b + p + off < 8 * B if isinstance(b, int) else True

        def is_batch(b, off):
            return 0 <= b + off < B if isinstance(b, int) else True

        def need(eng, name, n):
            if not isinstance(n, int) or n > 0:
                eng.wait_ge(s[name], n)

        def need_alone(eng, name, n):
            if not isinstance(n, int) or n > 0:
                eng.wait_ge(s[name], n)
                eng.sem_inc(s["went_on"], 1)

        GROUPS = B // 4

        def group(c):
            return [x[:, 8 * c:8 * c + 8, :].rearrange("q (k i) d -> q k i d", i=TT) for x in (xo_all, x_all)]

        def per_batch(v):
            return v[:, :, :].rearrange("q (o i) d -> q o i d", o=1).to_broadcast([128, 4, TT, D])

        def has(b, off):
            return 0 <= b + off < B if isinstance(b, int) else True

        PRODUCTS = [(0, 0), (0, 1), (0, 2), (1, 0), (1, 1), (2, 0)]
        NSTK = 2 * len(PRODUCTS) + 1
        TO3, TMB, QK, TOT, VP, TO0, WO = (1, 0), (0, 0), (0, 1), (1, 1), (0, 2), (1, 2), (0, 3)
        GB, TMA, TO1, TX, GA, TO2 = (1, 3), (1, 4), (0, 5), (1, 5), (0, 4), (0, 6)
        tally = [Tally([(0,), (2,), (1,), (-1,), (-2,), (0,), (0,)]), Tally([(-1,), (-1,), (0,), (-2,), (1,), (3, -1)])]
        TOS = [TO3, TO0, TO1, TO2]
        ST = psum[:, 0:1024]
        SB = [bank[2], bank[3], bank[4]]
        OB, MIS = bank[5], [bank[6], bank[7]]

        def shared(use):
            return MIS[use[0]]

        def need_full(eng, b, use):
            need(eng, f"full{use[0]}", tally[use[0]].before(b, use[1] + 1))

        def need_free(eng, b, use, done=0):
            need(eng, f"free{use[0]}", tally[use[0]].before(b, use[1] + done))

        def quad(b, p):
            return (-1, 3) if p < 2 else (0, p // 2 - 1)

        def is_tile(i, p, off):
            return 0 <= 2 * i + p + off < NT if isinstance(i, int) else True

        def pad(eng, e):
            at = eng.value_load(pad_at[0:1, e:e + 1], min_val=0, max_val=DUMMY) if e < E else DUMMY
            eng.dma_start(xs[bass.ds(at, GT), :].rearrange("(p a) d -> p a d", a=2), zrow[:, :, :]).then_inc(s["pad_in"], 16)

        block = ctx.enter_context(nc.Block())
        NCH = TOK // 512

        @block.sync
        def _(sp):
            def load(dst, src, signal):
                dst = dst[:, :, :] if len(dst.shape) == 3 else dst[:, :]
                sp.dma_start(dst, t[src]).then_inc(s[signal], 16)

            for dst, src in ((w1, "w1T"), (w2, "w2T"), (cols, "colsA")):
                load(dst, src, "w_in")
            for c in range(4):
                sp.dma_start(hT[:, c * (TOK // 4):(c + 1) * (TOK // 4)], t["xT"][:, c * (TOK // 4):(c + 1) * (TOK // 4)]).then_inc(s[f"xT_in{c}"], 16)
            load(wg, "wgT", "wg_in")
            for dst, src in ((ident, "ident"), (bv, "bvB"), (keysT, "keysT"), (rwT, "rwT"), (rconst, "rbB"), (wo, "woT")):
                load(dst, src, "rest_in")
            sp.dma_start(x_all[:, :, :], t["x"].rearrange("(n p) d -> p n d", p=128)).then_inc(s["x_in"], 16)
            load(wall, "wall", "wall_in")
            sp.wait_ge(s["plan_ready"], 1)
            sp.dma_start(plan_d, plan2[:, :]).then_inc(s["plan_out"], 16)
            sp.wait_ge(s["zrow_ready"], 1)

            for e in range(3):
                pad(sp, e)
            sp.wait_ge(s["plan_out"], 16)
            sp.dma_start(plan[:, :], plan_d.rearrange("(o t) c -> o (t c)", o=1)).then_inc(s["plan_in"], 16)
            for e in range(3, E // 2):
                pad(sp, e)
            sp.wait_ge(s["plan_in"], 16)
            sp.wait_ge(s["pad_in"], 16 * (E + 1))
            sp.wait_ge(s["a_done"], 4)

            def row_of(n):
                at = 2 * n + 1
                src = plan[0:1, at:at + 1] if isinstance(n, int) else plan[0:1, bass.ds(at, 1)]
                return sp.value_load(src, min_val=0, max_val=DUMMY)

            def load_rows(n, par):
                need_alone(sp, "tin_mm", n - 1)
                sp.dma_start(xg[:, par, :, :], xs[bass.ds(row_of(n), GT), :].rearrange("(p a) d -> p a d", a=2)).then_inc(s[f"xg_in{par}"], 16)

            load_rows(0, 0)
            load_rows(1, 1)
            def body(i):
                for p in range(2):
                    n = 2 * i + p
                    if is_tile(i, p, 2):
                        load_rows(n + 2, p)
                if isinstance(i, int) and i == 0:
                    for dst, src in ((cw, "cw"), (lora_a, "lora_a"), (lora_b, "lora_b"), (gw, "gw"), (gu, "gu"), (gcol, "gcol"),
                                     (bo1, "bo1"), (bo2, "bo2")):
                        load(dst, src, "cw_in")

            batch_loop(sp, 2, NT // 2 - 1, 2, body)
            sp.wait_ge(s["ys_out"], 16 * NT)

            def attention(b, par):
                if has(b, 0):
                    maxima(b, TMB, par, 1, 2 * b + 1, H1 * (b + 1))
                if has(b, 2):
                    load = (par + 2) % 3
                    need_alone(sp, "parts_ready", b + 3)
                    need_alone(sp, "stk", 16 * NSTK * (b + 2))
                    sp.dma_start(qkd.rearrange("a r c -> r a c"), parts[:, :, :]).then_inc(s["qkd_out"], 16)
                    need_alone(sp, "qkd_out", 16 * (b + 3))
                    need_alone(sp, "st_full", 8 * b)
                    for n, (qa, ka) in enumerate(PRODUCTS):
                        for dst, part, c0 in ((qst[load], qa, 0), (kst[load], ka, N)):
                            sp.dma_start(dst[DH1 * n:DH1 * n + DH1, :, :],
                                         qkd[part].rearrange("(h d) c -> d h c", d=DH1)[:, :, c0:c0 + N]).then_inc(s["stk"], 16)
                    sp.dma_start(qst[load][MROW:MROW + NPART, :, :], zst[:, :, :]).then_inc(s["stk"], 16)
                if has(b, 1):
                    maxima(b, TMA, (par + 1) % 3, 0, 2 * b + 2, H1 * (b + 1) + H1 // 2)

            def maxima(b, use, slot, half, before, scored):
                need_alone(sp, f"free{use[0]}", tally[use[0]].before(b, use[1] + 1))
                need_alone(sp, "s_full", scored)
                need_alone(sp, "m_in", 16 * NPART * before)
                hh = H1 // 2
                for k in range(NPART):
                    sp.dma_start(qst[slot][MROW + k:MROW + k + 1, half * hh:half * hh + hh, :], mrow[k * hh:(k + 1) * hh, :]).then_inc(s["m_in"], 16)

            sp.wait_ge(s["cleared"], 2)
            attention_loop(sp, attention)
            for c in range(B // 4):
                sp.wait_ge(s["fin_ready"], c + 1)
                sp.dma_start(out[c * 4 * N:(c + 1) * 4 * N, :].rearrange("(n p) d -> p n d", p=128), x_all[:, 8 * c:8 * c + 8, :]).then_inc(s["out_done"], 16)
            sp.wait_ge(s["out_done"], 16 * B // 4)

        @block.gpsimd
        def _(pool):
            g = nc.gpsimd
            g.memset(kT[:, :, :, :], 0.0).then_inc(s["cst2"], 1)
            g.memset(P[:, :, :, :, :], 0.0).then_inc(s["cst2"], 1)
            g.memset(band[:, :, :], 0.0).then_inc(s["cst"], 1)
            pool.wait_ge(s["cst"], 1)
            for it in range(TT):
                g.affine_select(out=band[:, it, :], in_=band[:, it, :], compare_op=ALU.is_ge, fill=-BIG,
                                base=WINDOW - 1 + 128 * it, pattern=[[-1, N]], channel_multiplier=1).then_inc(s["cst"], 1)
            g.memset(ones[:, :], 1.0).then_inc(s["cst"], 1)
            g.memset(onesb[:, :], 1.0).then_inc(s["cst"], 1)
            pool.wait_ge(s["cst"], 5)
            g.affine_select(out=tri[:, :], in_=onesb[:, :], compare_op=ALU.is_gt, fill=0.0, base=0,
                            pattern=[[1, 128]], channel_multiplier=-1).then_inc(s["cst"], 1)
            g.iota(iota_e[:, :], pattern=[[1, E]], base=0, channel_multiplier=0,
                   allow_small_or_imprecise_dtypes=True).then_inc(s["cst"], 1)
            g.iota(first_row[:, :], pattern=[[CAP // 16, E]], base=0, channel_multiplier=0,
                   allow_small_or_imprecise_dtypes=True).then_inc(s["cst"], 1)
            g.memset(count[:, :], 0.0).then_inc(s["cst"], 1)
            g.memset(minus_half[:, :], -0.5)
            g.drain()
            g.memset(zrow[:, :, :], 0.0).then_inc(s["zrow_ready"], 1)
            g.iota(tile_no[:, :], pattern=[[0, 1]], base=0, channel_multiplier=1,
                   allow_small_or_imprecise_dtypes=True).then_inc(s["zrow_ready"], 1)
            pool.wait_ge(s["h_ready"], 1)
            g.tensor_copy(hV[:, :], hT[:, 0:N]).then_inc(s["hv_ready"], 1)

            def body(b):
                for p in range(8):
                    if p == 3 and is_batch(b, 1):
                        need(pool, "v_mm", 4 * b + 4)
                        g.tensor_copy(hV[:, :], hT[:, bass.ds((b + 1) * N, N)]).then_inc(s["hv_ready"], 1)
                    if p == 4 and is_batch(b, -1):
                        need_alone(pool, "var_ready", b)
                        g.tensor_tensor(rstd[:, :], veps[:, :], minus_half[:, 0:TT], ALU.pow).then_inc(s["pow_ready"], 1)
                    if p == 5 and is_batch(b, -1):
                        need(pool, "x1c_ready", b)
                        g.tensor_copy(x_all[:, bass.ds((b - 1) * TT, TT), :], x1c[:, :, :]).then_inc(s["x1_kept"], 1)
                    if p < 4 and is_batch(b, -2):
                        if p == 0:
                            need_alone(pool, "pos_ready", b - 1)
                        for k in (2 * p, 2 * p + 1):
                            nc.gpsimd.indirect_dma_start(
                                out=xs, out_offset=bass.IndirectOffsetOnAxis(pos[:, k:k + 1], 0),
                                in_=x1c[:, k // TOPK, :], in_offset=None).then_inc(s["scat"], 16)

            batch_loop(pool, 2, B - 1, 3, body)
            pool.wait_ge(s["scat"], 16 * B * TT * TOPK)
            g.drain().then_inc(s["a_done"], 1)
            pool.wait_ge(s["a_done"], 4)
            def clear(k):
                g.memset(qst[k][:, :, :].rearrange("q h n -> q (h n)").bitcast(fp32), 0.0)
                g.memset(kst[k][:, :, :].rearrange("q h n -> q (h n)").bitcast(fp32), 0.0)
                g.drain()
                g.memset(kst[k][MROW:MROW + NPART, :, :], 1.0)
                g.drain()

            npos = B * TT * TOPK
            pool.wait_ge(s["plan_ready"], 3)

            at = posf_all[:, :].rearrange("q (n o) -> q n o", o=1)
            g.tensor_tensor(shift[:, :, :], shift[:, :, :], delta[:, :].rearrange("q (o e) -> q o e", o=1).to_broadcast([128, npos, E]), ALU.mult)
            g.drain()
            w = E // 2
            while w:
                g.tensor_tensor(shift[:, :, 0:w], shift[:, :, 0:w], shift[:, :, w:2 * w], ALU.add)
                g.drain()
                w //= 2
            g.tensor_tensor(at, at, shift[:, :, 0:1], ALU.add)
            g.drain()
            g.tensor_copy(pos_all[:, :], posf_all[:, :])
            g.drain()
            for k in range(2):
                clear(k)
            g.memset(zst[:, :, :], 0.0)
            g.drain()
            g.memset(v32[:, :, :, :, :], 0.0)
            g.drain()
            g.memset(v32[:, :, :, :, DH1:DH1 + 1], 1.0).then_inc(s["cleared"], 1)
            pool.wait_ge(s["wB_ready"], NT)
            clear(2)
            g.drain().then_inc(s["cleared"], 1)
            pool.wait_ge(s["ys_out"], 16 * NT)

            def fetch(b):
                if has(b, 4):
                    g.tensor_copy(posc[:, :], pos_all[:, bass.ds((b + 4) * TT * TOPK, TT * TOPK)]).then_inc(s["posc_ready"], 1)
                    need_alone(pool, "posc_ready", b + 5)
                    need_alone(pool, "comb_done", b + 4)
                    for n in range(TT * TOPK):
                        g.indirect_dma_start(out=yk[:, n, :], out_offset=None, in_=ys,
                                             in_offset=bass.IndirectOffsetOnAxis(posc[:, n:n + 1], 0)).then_inc(s["yk_in"], 16)

            def keep(b):
                if has(b, 3) or has(b, -1):
                    n = TT * (has(b, 3) + has(b, -1))
                    need_alone(pool, "var2_ready", b + 4)
                    g.tensor_tensor(rstd2[:, 0, 0:n], ve2[:, 0, 0:n], minus_half[:, 0:n], ALU.pow).then_inc(s["pow2_ready"], 1)
                if has(b, -1):
                    need(pool, "x3_ready", b)
                    g.tensor_copy(x_all[:, bass.ds((b - 1) * TT, TT), :], x3c[:, :, :]).then_inc(s["x3_kept"], 1)
                if has(b, 3):
                    need(pool, "x2_ready", b + 4)
                    g.tensor_tensor(x_all[:, bass.ds((b + 3) * TT, TT), :], x2c[:, :, :],
                                    bo1[:, :].rearrange("q (o d) -> q o d", o=1).to_broadcast([128, TT, D]), ALU.add).then_inc(s["x2_kept"], 1)

            def weigh(b):
                if has(b, 4):
                    need(pool, "yk_in", 16 * TT * TOPK * (b + 5))
                    g.tensor_copy(gcur[:, :], gate_all[:, bass.ds(b + 4, 1), :].rearrange("q o k -> q (o k)"))
                    g.drain()
                    g.tensor_tensor(yk[:, :, :], yk[:, :, :], gcur[:, :].rearrange("q (n o) -> q n o", o=1).to_broadcast([128, TT * TOPK, D]), ALU.mult)
                    g.drain()
                    y4 = yk[:, :, :].rearrange("q (i k) d -> q i k d", i=TT)
                    g.tensor_tensor(y4[:, :, 0:2, :], y4[:, :, 0:2, :], y4[:, :, 2:4, :], ALU.add)
                    g.drain()
                    g.tensor_tensor(acc, y4[:, :, 0, :], y4[:, :, 1, :], ALU.add)
                    g.drain()
                    g.tensor_tensor(acc, acc, x_all[:, bass.ds((b + 4) * TT, TT), :], ALU.add).then_inc(s["comb_done"], 1)

            def outputs(b):
                fetch(b)
                keep(b)
                weigh(b)

            pool.sem_inc(s["x3_kept"], 1)
            for b in range(-4, 1):
                outputs(b)
            with pool.Fori(1, B - 4) as b:
                outputs(b)
            for b in range(B - 4, B + 1):
                outputs(b)
            xo, xt = group(GROUPS - 1)
            pool.wait_ge(s["state_ready"], 1)
            g.tensor_tensor(xo, xo, per_batch(state), ALU.add).then_inc(s["h_pre_last"], 1)
            for c in range(GROUPS):
                if c == 1:
                    pool.wait_ge(s["h_act"], GROUPS)
                    g.tensor_tensor(xt, xt, xo, ALU.add).then_inc(s["last_sum"], 1)
                pool.wait_ge(s["var3_ready"], c + 1)
                g.tensor_tensor(rstd2[:, c, :], ve2[:, c, :], minus_half[:, :], ALU.pow).then_inc(s["pow3_ready"], 1)

        @block.tensor
        def _(pe):
            mm = nc.tensor.matmul
            pe.wait_ge(s["w_in"], 48)

            def qk(b, p, n):
                need(pe, "q_ev", n)
                need(pe, "k_ev", 2 * n)
                c = n // 8 if isinstance(n, int) else (b if p == 0 else b + 1)
                r = (p + 7) % 8
                tok = hT[:, bass.ds(c * N, N)] if not isinstance(c, int) else hT[:, c * N:(c + 1) * N]
                mm(J[:, 0:N], wg[:, r * 128:(r + 1) * 128], tok, start=True, stop=True)
                mm(J[:, N:2 * N], wg[:, H * DH + r * 128:H * DH + (r + 1) * 128], tok, start=True, stop=True).then_inc(s["qk_mm"], 1)

            def vproj(nv, half, jt):
                need(pe, "v_ev", nv)
                c0 = 2 * H * DH + half * 512
                mm(M[:, :], hV[:, jt * 128:(jt + 1) * 128], wg[:, c0:c0 + 512], start=True, stop=True).then_inc(s["v_mm"], 1)

            for c in range(NCH + 1):
                if c < NCH:
                    if c % 2 == 0:
                        pe.wait_ge(s[f"xT_in{c // 2}"], 16)
                    if c >= 2:
                        pe.wait_ge(s["hA_act"], c - 1)
                    mm(bank[c % 2][:, :], w1[:, :], hT[:, c * 512:(c + 1) * 512], start=True, stop=True).then_inc(s["hA_mm"], 1)
                if c >= 1:
                    pe.wait_ge(s["hA_act"], c)
                    if c >= 3:
                        pe.wait_ge(s["h_ready"], c - 2)
                    mm(bank[2 + c % 2][:, :], w2[:, :], h1[:, (c - 1) % 2, :], start=True, stop=True).then_inc(s["hB_mm"], 1)
                if c >= 2:
                    if c == 2:
                        pe.wait_ge(s["wg_in"], 16)
                        pe.wait_ge(s["h_ready"], 1)
                    qk(0, c - 1, c - 2)
            pe.wait_ge(s["cst"], 5)
            pe.wait_ge(s["rmat_ready"], 1)
            mm(M[:, 0:E], ones[:, :], ksq[:, :], start=True, stop=True).then_inc(s["ksq_ready"], 1)
            pe.wait_ge(s["rest_in"], 96)
            pe.wait_ge(s["hv_ready"], 1)
            pe.wait_ge(s["rmat_ready"], 2)
            for jt in range(TT):
                vproj(jt, 0, jt)

            def body(b):
                for p in range(8):
                    par, par1 = p % 2, (p - 1) % 2
                    if is_pair(b, p, 0):
                        need(pe, "q_ev", pair(b, p, 1))
                        need(pe, "k_ev", 2 * pair(b, p, 1))
                        for it, bk in ((0, S0), (1, S1)):
                            w = N - WINDOW if it == 0 else N
                            need(pe, "shifted_ready", 4 * pair(b, p) - 2 * (1 - it) if not isinstance(b, int) or 8 * b + p > 0 else 0)
                            mm(bk[:, 0:2 * w].rearrange("q (h j) -> q h j", h=2), qT[:, p, it * 128:(it + 1) * 128],
                               kT[:, p, :, 0:w], start=True, stop=True).then_inc(s["scores"], 1)
                    if is_pair(b, p, 7):
                        qk(b, p, pair(b, p, 7))
                    if is_batch(b, -1):
                        after_attention(b, p)
                    if is_pair(b, p, -1):
                        for h, bk, ev in ((0, PTA, "ptA_ev"), (1, PTB, "ptB_ev")):
                            need(pe, "pn_ready", 4 * pair(b, p) - 2 * (1 - h))
                            need(pe, ev, pair(b, p, -1))
                            for jt in range(TT):
                                for it in range(TT):
                                    c0 = (N if jt == 0 else 0) + it * 128
                                    last = nc.tensor.transpose(bk[:, c0:c0 + 128], P[:, par1, it, h, jt * 128:(jt + 1) * 128], ident[:, :])
                            last.then_inc(s["pt_mm"], 1)
                    if is_pair(b, p, -2):
                        r = (p - 2) % 8
                        need(pe, "ptA_ev", pair(b, p, -1))
                        need(pe, "ptB_ev", pair(b, p, -1))
                        need(pe, "ot_ev", pair(b, p, -2))
                        bb = b - 1 if p < 2 else b
                        need(pe, "v_ev", 4 * bb + (2 if r < 4 else 4))
                        for h in range(2):
                            mm(OTB[64 * h:64 * h + 64, 0:N], V[:, 0, r * 128 + 64 * h:r * 128 + 64 * h + 64], PT[:, par, h, N:2 * N], start=True, stop=False)
                        for h in range(2):
                            last = mm(OTB[64 * h:64 * h + 64, WINDOW:N], V[:, 1, r * 128 + 64 * h:r * 128 + 64 * h + 64], PT[:, par, h, WINDOW:N], start=False, stop=True)
                        last.then_inc(s["pv_mm"], 1)
                    if p == 0 and has(b, 0) and has(b, -1):
                        need(pe, "pos_ready", b - 1)
                        vproj(4 * b + 1, 0, 1)
                    if p in (1, 2) and is_batch(b, 0):
                        vproj(4 * b + (1 + p), 1, p - 1)
                    if p == 6 and is_batch(b, 1):
                        need(pe, "hv_ready", b + 2)
                        need(pe, "top_ready", b)
                        vproj(4 * b + 4, 0, 0)
                    if is_pair(b, p, -3):
                        r = (p - 3) % 8
                        need(pe, "ot_ev", pair(b, p, -2))
                        if r == 0:
                            need(pe, "yT_ev", b)
                        mm(Y[:, 0:N], wo[:, r, :], OT[:, par1, :], start=(r == 0), stop=(r == 7)).then_inc(s["wo_mm"], 1)
                    if p == 5 and is_batch(b, -1):
                        need(pe, "x1T_ready", b)
                        for it in range(TT):
                            last = mm(M[:, it * E:(it + 1) * E], x1T[:, it * 128:(it + 1) * 128], rmat[:, :], start=True, stop=True)
                        last.then_inc(s["m_l"], 1)

            def after_attention(b, p):
                if p == 3:
                    need(pe, "yT_ev", b)
                    need(pe, "pos_ready", b - 1)
                    if has(b, 0):
                        need(pe, "v_ev", 4 * b + 4)
                    for it in range(TT):
                        last = nc.tensor.transpose(M[:, it * D:(it + 1) * D], yT[:, it * 128:(it + 1) * 128], ident[:, :])
                    last.then_inc(s["m_y"], 1)
                if p == 5:
                    need(pe, "x1c_ready", b)
                    for it in range(TT):
                        last = nc.tensor.transpose(M[:, it * 128:(it + 1) * 128], x1c[:, it, :], ident[:, :])
                    last.then_inc(s["m_x"], 1)
                if p == 7:
                    need(pe, "mask_ready", b)
                    if has(b, 1):
                        need(pe, "v_ev", 4 * b + 5)
                    mm(M[:, 0:E], tri[:, :], mask[:, 0, :], start=True, stop=True)
                    mm(M[:, E:2 * E], tri[:, :], mask[:, 1, :], start=True, stop=False)
                    mm(M[:, E:2 * E], onesb[:, :], mask[:, 0, :], start=False, stop=True)
                    mm(M[:, 2 * E:3 * E], onesb[:, :], mask[:, 0, :], start=True, stop=False)
                    mm(M[:, 2 * E:3 * E], onesb[:, :], mask[:, 1, :], start=False, stop=True).then_inc(s["m_r"], 1)

            batch_loop(pe, 2, B - 1, 2, body)
            pe.drain().then_inc(s["a_done"], 1)
            pe.wait_ge(s["a_done"], 4)

            def rows_in(n, par, loads):
                need(pe, f"xg_in{par}", loads)
                need(pe, "xgT_ready", n)
                for k in range(2):
                    last = nc.tensor.transpose(TI[:, k * 128:(k + 1) * 128], xg[:, par, k, :], ident[:, :])
                last.then_inc(s["tin_mm"], 1)

            rows_in(0, 0, 16)
            def tiles(i):
                if isinstance(i, int) and i == 1:
                    pe.wait_ge(s["cw_in"], 128)
                    for k in range(4):
                        last = mm(MIS[1][:, k * D:(k + 1) * D], lora_a[:, k, :], lora_b[:, k, :], start=True, stop=True)
                    last.then_inc(s["lora_mm"], 1)
                for p in range(2):
                    n, q = 2 * i + p, 1 - p
                    if is_tile(i, p, 0):
                        need(pe, "xgT_ready", n + 1)
                        need(pe, "wA_ready", n + 1)
                        need(pe, "hid_ready", 4 * n - 4)
                        for f in range(FC):
                            mm(UP[p][:, f * GT:(f + 1) * GT], wA[:, p, f * 128:(f + 1) * 128], xgT[:, p, :], start=True, stop=True).then_inc(s["up_mm"], 1)
                    if is_tile(i, p, 1):
                        rows_in(n + 1, q, 16 * i + 16 * (p + 1))
                    if is_tile(i, p, -1):
                        need(pe, "hid_ready", 4 * n)
                        need(pe, "wB_ready", n)
                        need(pe, "yTe_ready", n - 1)
                        for f in range(FC):
                            last = mm(DN[:, 0:GT], wB[:, q, f * D:(f + 1) * D], hid[:, q, f, :], start=(f == 0), stop=(f == FC - 1))
                        last.then_inc(s["dn_mm"], 1)
                    if is_tile(i, p, -2):
                        need(pe, "yTe_ready", n - 1)
                        need(pe, "yrow_ready", n - 2)
                        for k in range(2):
                            last = nc.tensor.transpose(TO[:, k * D:(k + 1) * D], yTe[:, p, k * 128:(k + 1) * 128], ident[:, :])
                        last.then_inc(s["tout_mm"], 1)

            batch_loop(pe, 2, NT // 2 - 1, 2, tiles)

            pe.wait_ge(s["c_set"], 1)
            pe.wait_ge(s["cleared"], 2)

            def attention(b, par):
                nxt = (par + 1) % 3
                for p in range(8):
                    if has(b, 0):
                        if p % 4 == 0:
                            need(pe, "m_in", 16 * NPART * (2 * b + (p // 4 + 1)))
                        need(pe, "exps1", 8 * b + p)
                        for k in range(2):
                            for jt in range(TT):
                                last = mm(ST[:, (2 * k + jt) * N:(2 * k + jt + 1) * N], kst[par][:, 2 * p + k, jt * 128:(jt + 1) * 128],
                                          qst[par][:, 2 * p + k, :], start=True, stop=True)
                        last.then_inc(s["st_full"], 1)
                    off, j = quad(b, p)
                    if p % 2 == 0 and has(b, off):
                        need(pe, "exps1", 8 * b + p)
                        need(pe, "o_free", 4 * b + (p // 2 - 1))
                        vpar = par if off == 0 else (par + 2) % 3
                        for jt in range(TT):
                            for r in range(4):
                                hd = 4 * j + r
                                last = mm(OB[32 * r:32 * r + 32, 0:N], v32[:, vpar, jt, hd, :], pc[:, hd // 2 % 4, r % 2, jt, :],
                                          start=(jt == 0), stop=(jt == TT - 1))
                        last.then_inc(s["pv_full"], 1)
                    if p == 4 and has(b, -2):
                        need(pe, "scan_done", b - 1)
                        need_free(pe, b, TO3)
                        gates(b, GA)
                        gates(b, GB)
                    if p == 5 and has(b, 1):
                        maxima_T(b, TMA, 0, 2 * b + 3)
                    if p % 2 == 1 and has(b, off):
                        use = TOS[(p - 1) // 2]
                        need_free(pe, b, use)
                        need(pe, "o_free", 4 * b + (p - 1) // 2)
                        for it in range(TT):
                            last = nc.tensor.transpose(shared(use)[:, it * 128:(it + 1) * 128], oTc[:, it * 128:(it + 1) * 128], ident[:, :])
                        last.then_inc(s[f"full{use[0]}"], 1)
                    if p == 1 and has(b, 0):
                        maxima_T(b, TMB, 1, 2 * b + 2)
                    if p == 1 and has(b, 2):
                        need_free(pe, b, QK)
                        need_free(pe, b, TO3)
                        mm(shared(QK)[:, 0:N], cw[:, 0, :], x2T[:, (par + 2) % 3, :], start=True, stop=True)
                        mm(shared(QK)[:, N:2 * N], cw[:, 1, :], x2T[:, (par + 2) % 3, :], start=True, stop=True).then_inc(s["full0"], 1)
                    if p == 2 and has(b, -1):
                        need_free(pe, b, TOT)
                        for it in range(TT):
                            last = nc.tensor.transpose(shared(TOT)[:, it * 128:(it + 1) * 128], otok[:, it, :], ident[:, :])
                        last.then_inc(s["full1"], 1)
                    if p == 2 and has(b, 1):
                        need_free(pe, b, VP)
                        for jt in range(TT):
                            last = mm(shared(VP)[:, jt * D:(jt + 1) * D], x2T[:, nxt, jt * 128:(jt + 1) * 128], cw[:, 2, :], start=True, stop=True)
                        last.then_inc(s["full0"], 1)
                    if p == 3 and has(b, -1):
                        need_free(pe, b, WO)
                        need_free(pe, b, TOT, 1)
                        for it in range(TT):
                            last = mm(shared(WO)[:, it * D:(it + 1) * D], oT[:, it * 128:(it + 1) * 128], cw[:, 3, :], start=True, stop=True)
                        last.then_inc(s["full0"], 1)
                    if p == 5 and (has(b, 3) or has(b, -1)):
                        need_free(pe, b, TX)
                        if has(b, 3):
                            need(pe, "x2_ready", b + 4)
                            for it in range(TT):
                                last = nc.tensor.transpose(shared(TX)[:, it * 128:(it + 1) * 128], x2c[:, it, :], ident[:, :])
                        if has(b, -1):
                            need(pe, "x3_ready", b)
                            for it in range(TT):
                                last = nc.tensor.transpose(shared(TX)[:, N + it * 128:N + (it + 1) * 128], x3c[:, it, :], ident[:, :])
                        last.then_inc(s["full1"], 1)
                    scores(b, p, nxt)

            def scores(b, p, nxt):
                if not has(b, 1):
                    return
                if p == 0:
                    need(pe, "stk", 16 * NSTK * (b + 2))
                for h in (2 * p, 2 * p + 1):
                    need(pe, "max_done", H1 * (b + 1) + (h - 2))
                    for it in range(TT):
                        last = mm(SB[(nxt + h) % 3][:, it * N:(it + 1) * N], qst[nxt][:, h, it * 128:(it + 1) * 128],
                                  kst[nxt][:, h, :], start=True, stop=True)
                    last.then_inc(s["s_full"], 1)

            def maxima_T(b, use, half, n):
                need_free(pe, b, use)
                need_alone(pe, "nm_ready", n)
                for it in range(TT):
                    last = nc.tensor.transpose(shared(use).bitcast(bf16)[0:NPART * H1 // 2, it * 128:(it + 1) * 128],
                                               nmx[:, it, half, :, :].rearrange("q a h -> q (a h)"), identb[:, :])
                last.then_inc(s[f"full{use[0]}"], 1)

            def gates(b, use):
                need_free(pe, b, use)
                for n, k in enumerate((0, 1) if use == GA else (2,)):
                    mm(shared(use)[:, n * N:(n + 1) * N], gw[:, k, :], x3T[:, :], start=True, stop=False)
                    last = mm(shared(use)[:, n * N:(n + 1) * N], gu[:, k, :], c2[:, :], start=False, stop=True)
                if use == GB:
                    for it in range(TT):
                        last = mm(shared(use)[:, N + it * D:N + (it + 1) * D], x3T[:, it * 128:(it + 1) * 128], gw[:, 3, :], start=True, stop=True)
                last.then_inc(s[f"full{use[0]}"], 1)

            attention_loop(pe, attention)
            pe.wait_ge(s["scan_done"], B + 1)
            for it in range(TT):
                last = mm(SB[0][:, it * D:(it + 1) * D], c2[:, it * 128:(it + 1) * 128], gu[:, 3, :], start=True, stop=True)
            last.then_inc(s["state_mm"], 1)

        @block.scalar
        def _(act):
            sc = nc.scalar
            act.wait_ge(s["w_in"], 48)

            def qk_evac(b, p, n):
                r = (p + 7) % 8
                need(act, "qk_mm", n + 1)
                sc.activation(qT[:, r, :], J[:, 0:N], ACT.Identity, bias=cols[:, 3 + r:4 + r]).then_inc(s["q_ev"], 1)
                for h in range(2):
                    sc.activation(kT[64 * h:64 * h + 64, r, h, :], J[64 * h:64 * h + 64, N:2 * N], ACT.Identity,
                                  bias=cols[64 * h:64 * h + 64, 3 + PAIRS + r:4 + PAIRS + r]).then_inc(s["k_ev"], 1)

            for c in range(NCH + 1):
                if c < NCH:
                    act.wait_ge(s["hA_mm"], c + 1)
                    if c >= 2:
                        act.wait_ge(s["hB_mm"], c - 1)
                    sc.activation(h1[:, c % 2, :], bank[c % 2][:, :], ACT.Silu, bias=cols[:, 0:1]).then_inc(s["hA_act"], 1)
                if c >= 1:
                    act.wait_ge(s["hB_mm"], c)
                    sc.activation(hT[:, (c - 1) * 512:c * 512], bank[2 + c % 2][:, :], ACT.Identity, bias=cols[:, 1:2]).then_inc(s["h_ready"], 1)
                if c == 2:
                    act.wait_ge(s["cst2"], 2)
                if c >= 2:
                    qk_evac(0, c - 1, c - 2)

            def body(b):
                for p in range(8):
                    par, par1 = p % 2, (p - 1) % 2
                    if p == 7 and is_batch(b, -1):
                        need(act, "top_ready", b)
                        for it in range(TT):
                            last = sc.activation(wexp[:, it, :], top[:, it, 0:TOPK], ACT.Exp, bias=ntop[:, it:it + 1], accum_out=wsum[:, it:it + 1])
                        last.then_inc(s["exp_w"], 1)
                    if is_pair(b, p, 0):
                        need(act, "pt_mm", 2 * pair(b, p) - 2 if not isinstance(b, int) or 8 * b + p > 1 else 0)
                        for it in range(TT):
                            for h in range(2):
                                n = 2 * h + it
                                w = N - WINDOW if it == 0 else N
                                need(act, "shifted_ready", 4 * pair(b, p) + (2 * it + h + 1))
                                last = sc.activation(P[:, par, it, h, 0:w], shifted[:, par, it, h, 0:w], ACT.Exp, scale=-1.0,
                                                     bias=least[:, par, n:n + 1], accum_out=rowsum[:, par, n:n + 1])
                        last.then_inc(s["exps"], 1)
                    if is_pair(b, p, 7):
                        qk_evac(b, p, pair(b, p, 7))
                    if p == 5 and is_batch(b, -1):
                        need(act, "m_x", b)
                        sc.activation(x1T[:, :], M[:, 0:N], ACT.Copy).then_inc(s["x1T_ready"], 1)
                        for it in range(TT):
                            sc.activation(sqj[:, :], x1c[:, it, :], ACT.Square, accum_out=xsq[:, it:it + 1]).then_inc(s["xsq_ready"], 1)
                            need(act, "xsq_ready", 2 * b - 1 + it)
                    if is_pair(b, p, -1):
                        need(act, "pt_mm", 2 * pair(b, p))
                        need(act, "pv_mm", pair(b, p, -2))
                        sc.activation(PT[:, par1, 1, WINDOW:2 * N], PTB[:, WINDOW:2 * N], ACT.Copy).then_inc(s["ptB_ev"], 1)
                    if is_pair(b, p, -2):
                        need(act, "pv_mm", pair(b, p, -1))
                        need(act, "wo_mm", pair(b, p, -3))
                        sc.activation(OT[:, par, :], OTB[:, 0:N], ACT.Copy).then_inc(s["ot_ev"], 1)
                    if p == 2 and is_batch(b, -1):
                        need(act, "wo_mm", 8 * b)
                        need(act, "m_y", b - 1)
                        sc.activation(yT[:, :], Y[:, 0:N], ACT.Identity, bias=cols[:, 2:3]).then_inc(s["yT_ev"], 1)
            batch_loop(act, 2, B - 1, 2, body)
            act.drain().then_inc(s["a_done"], 1)
            act.wait_ge(s["plan_ready"], 1)
            act.wait_ge(s["zrow_ready"], 1)
            for e in range(E // 2, E + 1):
                pad(act, e)
            act.wait_ge(s["a_done"], 4)

            def store(m, par):
                need_alone(act, "yrow_ready", m + 1)
                need_alone(act, "ys_out", 16 * m)
                act.dma_start(ys[bass.ds(m * GT, GT), :].rearrange("(p a) d -> p a d", a=2), yrow[:, par, :, :]).then_inc(s["ys_out"], 16)

            def tiles(i):
                for p in range(2):
                    n, q = 2 * i + p, 1 - p
                    if is_tile(i, p, 0):
                        need(act, "dn_mm", n - 1)
                        for f in range(FC):
                            need(act, "up_mm", 4 * n + (2 * (f // 2) + 2))
                            sc.activation(hid[:, p, f, :], UP[p][:, f * GT:(f + 1) * GT], ACT.Gelu, bias=wA[:, p, F + f:F + f + 1]).then_inc(s["hid_ready"], 1)
                    if is_tile(i, p, -1):
                        need(act, "dn_mm", n)
                        need(act, "tout_mm", n - 2)
                        sc.activation(yTe[:, q, :], DN[:, 0:GT], ACT.Identity, bias=wB[:, q, FC * D:FC * D + 1]).then_inc(s["yTe_ready"], 1)
                    if is_tile(i, p, -3):
                        store(n - 3, q)

            batch_loop(act, 2, NT // 2 - 1, 2, tiles)
            store(NT - 1, 1)

            def attention(b, par):
                for p in range(8):
                    off, j = quad(b, p)
                    if has(b, 0):
                        need(act, "st_full", 8 * b + p + 1)
                        need(act, "pv_full", 4 * b + (p // 2 - 1))
                        sc.activation(pc[:, p % 4, :, :, :].rearrange("q h j n -> q (h j n)"), ST, ACT.Exp, scale=SCALE1).then_inc(s["exps1"], 1)
                    if p % 2 == 0 and has(b, off):
                        need(act, "pv_full", 4 * b + p // 2)
                        if p > 0 and (p > 2 or has(b, -1)):
                            need_full(act, b, TOS[p // 2 - 1])
                        if p == 0:
                            need(act, "full0", tally[0].before(b))
                        sc.activation(oTc[:, :], OB[:, 0:N], ACT.Copy).then_inc(s["o_free"], 1)
                    if p == 2 and has(b, -1):
                        need_full(act, b, TOT)
                        sc.activation(oT[:, :], shared(TOT)[:, 0:N], ACT.Copy).then_inc(s["free1"], 1)
                    if p == 2 and has(b, 1):
                        need_full(act, b, VP)
                        for jt in range(TT):
                            last = sc.activation(v32[:, (par + 1) % 3, jt, :, 0:DH1], shared(VP)[:, jt * D:(jt + 1) * D].rearrange("q (h d) -> q h d", h=H1), ACT.Copy)
                        last.then_inc(s["free0"], 1)
                    if p == 1 and has(b, 0):
                        maxima_row(b, TMB, 2 * b + 1)
                    if p == 1 and has(b, 2):
                        need_full(act, b, QK)
                        need(act, "qkd_out", 16 * (b + 2))
                        sc.activation(parts[:, 0, :], shared(QK)[:, :], ACT.Copy).then_inc(s["a1_ready"], 1)
                    if p == 4 and has(b, -2):
                        need_full(act, b, GA)
                        sc.activation(tf[:, :], shared(GA)[:, 0:N], ACT.Tanh, bias=gcol[:, 0:1], scale=0.5)
                        sc.activation(ti[:, :], shared(GA)[:, N:2 * N], ACT.Tanh, bias=gcol[:, 1:2], scale=0.5).then_inc(s["free0"], 1)
                    if p == 4 and has(b, -2):
                        need_full(act, b, GB)
                        sc.activation(tg[:, :], shared(GB)[:, 0:N], ACT.Tanh, bias=gcol[:, 2:3]).then_inc(s["gate_act"], 1)
                        sc.activation(xo_all[:, bass.ds((b - 2) * TT, TT), :].rearrange("q i d -> q (i d)"), shared(GB)[:, N:2 * N], ACT.Copy).then_inc(s["free1"], 1)
                    if p == 5 and has(b, 1):
                        maxima_row(b, TMA, 2 * b + 2)
                    if p == 5 and (has(b, 3) or has(b, -1)):
                        need_full(act, b, TX)
                        if has(b, 3):
                            last = sc.activation(x2T[:, par, :], shared(TX)[:, 0:N], ACT.Copy)
                        if has(b, -1):
                            last = sc.activation(x3T[:, :], shared(TX)[:, N:2 * N], ACT.Copy)
                        last.then_inc(s["free1"], 1)

            def maxima_row(b, use, before):
                need_full(act, b, use)
                need(act, "m_in", 16 * NPART * before)
                sc.activation(mrow[:, :], shared(use).bitcast(bf16)[0:NPART * H1 // 2, 0:N], ACT.Copy).then_inc(s[f"free{use[0]}"], 1)

            attention_loop(act, attention)
            for c in range(GROUPS):
                if c < GROUPS - 1:
                    act.wait_ge(s["h_pre"], c + 1)
                else:
                    act.wait_ge(s["h_pre_last"], 1)
                sc.activation(xo_all[:, 8 * c:8 * c + 8, :], xo_all[:, 8 * c:8 * c + 8, :], ACT.Tanh).then_inc(s["h_act"], 1)
            for c in range(GROUPS):
                act.wait_ge(s["scale_ready"], c + 1)
                for k in range(8):
                    x = x_all[:, 8 * c + k, :]
                    last = sc.activation(x, x, ACT.Identity, scale=rstd2[:, c, k:k + 1], bias=shift2[:, c, k:k + 1])
                last.then_inc(s["fin_ready"], 1)

        @block.vector
        def _(dve):
            v = nc.vector
            dve.wait_ge(s["rest_in"], 96)
            v.tensor_tensor(ksq[:, :], keysT[:, :], keysT[:, :], ALU.mult)
            v.scalar_tensor_tensor(rmat[:, :], keysT[:, :], 2.0, rwT[:, :], ALU.mult, ALU.add)
            v.drain()
            dve.wait_ge(s["cst"], 9)
            v.tensor_scalar(first_row[:, :], first_row[:, :], 16.0, None, ALU.mult).then_inc(s["rmat_ready"], 1)
            dve.wait_ge(s["ksq_ready"], 1)
            v.tensor_tensor(rconst[:, :], rconst[:, :], M[:, 0:E], ALU.subtract).then_inc(s["rmat_ready"], 1)
            v.drain()

            for jt in range(TT):
                dve.wait_ge(s["v_mm"], jt + 1)
                v.tensor_tensor(V[:, jt, 0:512], M[:, :], bv[:, 0:512], ALU.add).then_inc(s["v_ev"], 1)

            def values(n, half, jt):
                need(dve, "v_mm", n)
                cs = slice(512 * half, 512 * half + 512)
                v.tensor_tensor(V[:, jt, cs], M[:, :], bv[:, cs], ALU.add).then_inc(s["v_ev"], 1)

            def body(b):
                for p in range(8):
                    par, par1 = p % 2, (p - 1) % 2
                    if is_pair(b, p, -1):
                        need(dve, "exps", pair(b, p))
                        v.reciprocal(rinv[:, par1, :], rowsum[:, par1, :])
                        v.drain()
                        for h in range(2):
                            for it in range(TT):
                                n = 2 * h + it
                                w = N - WINDOW if it == 0 else N
                                x = P[:, par1, it, h, 0:w]
                                v.tensor_scalar(x, x, rinv[:, par1, n:n + 1], None, ALU.mult).then_inc(s["pn_ready"], 1)
                    if is_pair(b, p, 0):
                        for it, bk in ((0, S0), (1, S1)):
                            w = N - WINDOW if it == 0 else N
                            need_alone(dve, "scores", 2 * pair(b, p) + (it + 1))
                            for h in range(2):
                                n = 2 * h + it
                                v.tensor_tensor_reduce(out=shifted[:, par, it, h, 0:w], in0=bk[:, h * w:(h + 1) * w],
                                                       in1=band[:, it, 0:w], scale=-SCALE0, scalar=3.0e38, op0=ALU.add, op1=ALU.min,
                                                       accum_out=least[:, par, n:n + 1]).then_inc(s["shifted_ready"], 1)
                    if p == 6 and is_batch(b, -1):
                        need(dve, "m_l", b)
                        need(dve, "xsq_ready", 2 * b)
                        need(dve, "exp_w", b - 1)
                        for it in range(TT):
                            v.scalar_tensor_tensor(lg[:, it, :], M[:, it * E:(it + 1) * E], xsq[:, it:it + 1], rconst[:, :], ALU.subtract, ALU.add)
                        v.drain()
                        for it in range(TT):
                            v.max(top[:, it, :], lg[:, it, :])
                        v.drain()
                        for it in range(TT):
                            v.max_index(topi[:, it, :], top[:, it, :], lg[:, it, :])
                        v.tensor_scalar(ntop[:, :], top[:, :, 0], -1.0, None, ALU.mult).then_inc(s["top_ready"], 1)
                    if is_pair(b, p, -1):
                        need(dve, "pt_mm", 2 * pair(b, p) - 1)
                        need(dve, "pv_mm", pair(b, p, -2))
                        v.tensor_copy(PT[:, par1, 0, WINDOW:2 * N], PTA[:, WINDOW:2 * N]).then_inc(s["ptA_ev"], 1)
                    if p == 0 and has(b, 0) and has(b, -1):
                        values(4 * b + 2, 0, 1)
                    if p in (1, 2) and is_batch(b, 0):
                        values(4 * b + (2 + p), 1, p - 1)
                    if p == 6 and is_batch(b, 1):
                        values(4 * b + 5, 0, 0)
                    if not is_batch(b, -1):
                        continue
                    if p == 3:
                        need(dve, "m_y", b)
                        need(dve, "xsq_ready", 2 * b - 2)
                        v.tensor_tensor(res[:, :, :], M[:, 0:N].rearrange("q (i d) -> q i d", i=TT), x_all[:, bass.ds((b - 1) * TT, TT), :], ALU.add)
                        v.drain()
                        moments(v, res, TT, st, mv, nhalf[:, :], veps[:, :]).then_inc(s["var_ready"], 1)
                    if p == 4:
                        need(dve, "pow_ready", b)
                        refine(v, rstd[:, :], nhalf[:, :], t2[:, :])
                        need(dve, "scat", 16 * TT * TOPK * (b - 1))
                        need(dve, "x1_kept", b - 1)
                        for it in range(TT):
                            last = v.tensor_scalar(x1c[:, it, :], res[:, it, :], mv[:, it, 0:1], rstd[:, it:it + 1], ALU.subtract, ALU.mult)
                        last.then_inc(s["x1c_ready"], 1)
                    if p == 6:
                        v.drain()
                        v.tensor_copy(topif[:, :, :], topi[:, :, :])
                        v.drain()
                        for it in range(TT):
                            for k in range(TOPK):
                                v.tensor_scalar(hot[:, it, k, :], iota_e[:, :], topif[:, it, k:k + 1], None, ALU.is_equal)
                        v.drain()
                        v.tensor_reduce(out=chosen[:, :, :], in_=hot[:, :, :, :].rearrange("q i k e -> q i e k"), axis=mybir.AxisListType.X, op=ALU.add)
                        v.drain()
                        v.tensor_copy(mask[:, :, :], chosen[:, :, :]).then_inc(s["mask_ready"], 1)
                    if p == 7:
                        need(dve, "m_r", b)
                        v.tensor_tensor(rank[:, :, :], M[:, 0:2 * E].rearrange("q (i e) -> q i e", i=TT), count[:, :].rearrange("q (o e) -> q o e", o=1).to_broadcast([128, TT, E]), ALU.add)
                        v.drain()
                        v.tensor_tensor(rank[:, :, :], rank[:, :, :], first_row[:, :].rearrange("q (o e) -> q o e", o=1).to_broadcast([128, TT, E]), ALU.add)
                        v.tensor_tensor(count[:, :], count[:, :], M[:, 2 * E:3 * E], ALU.add)
                        v.drain()
                        need(dve, "exp_w", b)
                        v.reciprocal(wsum[:, :], wsum[:, :])
                        for it in range(TT):
                            v.tensor_tensor(junk[:, it * TOPK:(it + 1) * TOPK, :], hot[:, it, :, :],
                                            rank[:, it:it + 1, :].to_broadcast([128, TOPK, E]), ALU.mult)
                        v.drain()
                        v.tensor_reduce(out=posf[:, :], in_=junk[:, :, :], axis=mybir.AxisListType.X, op=ALU.add)
                        for it in range(TT):
                            v.tensor_scalar(gate_all[:, bass.ds(b - 1, 1), it * TOPK:(it + 1) * TOPK].rearrange("q o k -> q (o k)"), wexp[:, it, :], wsum[:, it:it + 1], None, ALU.mult)
                        v.drain()
                        v.tensor_copy(posf_all[:, bass.ds((b - 1) * TT * TOPK, TT * TOPK)], posf[:, :])
                        v.tensor_copy(pos[:, :], posf[:, :]).then_inc(s["pos_ready"], 1)

            dve.wait_ge(s["x_in"], 16)
            batch_loop(dve, 2, B - 1, 2, body)
            v.drain().then_inc(s["a_done"], 1)

            dve.wait_ge(s["zrow_ready"], 2)
            v.tensor_scalar(past[:, :], count[:, :], float(GT - 1), None, ALU.add)
            v.drain()
            v.tensor_copy(cnt_i[:, :], past[:, :])
            v.drain()
            v.tensor_scalar(cnt_i[:, :], cnt_i[:, :], GT.bit_length() - 1, None, ALU.logical_shift_right)
            v.drain()
            v.tensor_copy(ntile[:, :], cnt_i[:, :])
            v.memset(past[:, :], 1.0)
            v.drain()
            v.tensor_tensor_scan(ncum[:, :], past[:, :], ntile[:, :], 0.0, ALU.mult, ALU.add)
            v.drain()
            v.tensor_scalar(past[:, :], ncum[:, :], tile_no[:, :], None, ALU.is_le)
            v.drain()
            v.tensor_reduce(out=tile_e[:, :], in_=past[:, :], axis=mybir.AxisListType.X, op=ALU.add)
            v.tensor_tensor(skip[:, :], past[:, :], ntile[:, :], ALU.mult)
            v.drain()
            v.tensor_reduce(out=tile_s[:, :], in_=skip[:, :], axis=mybir.AxisListType.X, op=ALU.add)
            v.tensor_scalar(used[:, :], tile_e[:, :], float(E), None, ALU.is_lt)
            v.drain()
            v.tensor_tensor(tile_s[:, :], tile_no[:, :], tile_s[:, :], ALU.subtract)
            v.drain()
            v.tensor_scalar(tile_s[:, :], tile_s[:, :], float(GT), float(-DUMMY), ALU.mult, ALU.add)
            v.drain()
            v.scalar_tensor_tensor(tile_s[:, :], tile_e[:, :], float(CAP), tile_s[:, :], ALU.mult, ALU.add)
            v.tensor_scalar(plan2[:, 0:1], tile_e[:, :], float(E - 1), None, ALU.min)
            v.drain()
            v.tensor_tensor(tile_s[:, :], tile_s[:, :], used[:, :], ALU.mult)
            v.drain()
            v.tensor_scalar(plan2[:, 1:2], tile_s[:, :], float(DUMMY), None, ALU.add)
            v.tensor_tensor(skip[:, :], count[:, :], first_row[:, :], ALU.add)
            v.drain()
            v.tensor_copy(pad_at[:, :], skip[:, :])
            v.drain().then_inc(s["plan_ready"], 1)

            v.tensor_tensor(past[:, :], ncum[:, :], ntile[:, :], ALU.subtract)
            v.drain()
            v.scalar_tensor_tensor(past[:, :], past[:, :], float(GT), first_row[:, :], ALU.mult, ALU.subtract)
            v.drain()
            v.tensor_copy(delta[:, 0:1], past[:, 0:1])
            v.tensor_tensor(delta[:, 1:E], past[:, 1:E], past[:, 0:E - 1], ALU.subtract).then_inc(s["plan_ready"], 1)

            dve.wait_ge(s["wall_in"], 16)
            dve.wait_ge(s["a_done"], 4)
            dve.wait_ge(s["plan_in"], 16)

            def expert_of(n):
                src = plan[0:1, 2 * n:2 * n + 1] if isinstance(n, int) else plan[0:1, bass.ds(2 * n, 1)]
                return dve.value_load(src, min_val=0, max_val=E - 1)

            def weights_A(e, par):
                v.tensor_copy(wA[:, par, :], wall[:, bass.ds(e, 1), 0:WA].rearrange("q o c -> q (o c)")).then_inc(s["wA_ready"], 1)

            def weights_B(e, par):
                v.tensor_copy(wB[:, par, :], wall[:, bass.ds(e, 1), WA:WCOLS].rearrange("q o c -> q (o c)")).then_inc(s["wB_ready"], 1)

            def rows_T(n, par):
                need(dve, "tin_mm", n + 1)
                v.tensor_copy(xgT[:, par, :], TI[:, 0:GT]).then_inc(s["xgT_ready"], 1)

            first = expert_of(0)
            weights_A(first, 0)
            rows_T(0, 0)
            weights_B(first, 0)

            def prepare():
                v.tensor_copy(identb[:, :], ident[:, :])
                dve.wait_ge(s["cw_in"], 128)
                v.tensor_scalar(gu[:, :, :], gu[:, :, :], 0.5, None, ALU.mult)
                v.tensor_scalar(gcol[:, 0:2], gcol[:, 0:2], 0.5, None, ALU.mult)
                v.memset(c2[:, :], 0.0)
                v.drain()
                v.tensor_scalar(c2[:, :], c2[:, :], gcol[:, 3:4], 2.0, ALU.add, ALU.mult).then_inc(s["scan_done"], 1)
                dve.wait_ge(s["lora_mm"], 1)
                v.scalar_tensor_tensor(cw[:, :, :], MIS[1].rearrange("q (k d) -> q k d", k=4), LORA, cw[:, :, :], ALU.mult, ALU.add)
                v.drain().then_inc(s["c_set"], 1)
                npos = B * TT * TOPK
                v.tensor_tensor(shift[:, :, :], posf_all[:, :].rearrange("q (n o) -> q n o", o=1).to_broadcast([128, npos, E]),
                                first_row[:, :].rearrange("q (o e) -> q o e", o=1).to_broadcast([128, npos, E]), ALU.is_ge).then_inc(s["plan_ready"], 1)

            def tiles(i):
                for p in range(2):
                    n, q = 2 * i + p, 1 - p
                    if is_tile(i, p, 1):
                        e = expert_of(n + 1)
                        need(dve, "up_mm", 4 * n)
                        need(dve, "hid_ready", 4 * n)
                        weights_A(e, q)
                        rows_T(n + 1, q)
                    if is_tile(i, p, -1):
                        need(dve, "dn_mm", n)
                        need(dve, "yTe_ready", n)
                    if is_tile(i, p, 1):
                        weights_B(e, q)
                    if is_tile(i, p, -2):
                        need(dve, "tout_mm", n - 1)
                        need(dve, "ys_out", 16 * n - 48)
                        v.tensor_copy(yrow[:, p, :, :], TO[:, 0:GT].rearrange("q (a d) -> q a d", a=2)).then_inc(s["yrow_ready"], 1)
                if isinstance(i, int) and i == 1:
                    prepare()

            batch_loop(dve, 2, NT // 2 - 1, 2, tiles)

            def new_state(b):
                need(dve, "gate_act", b - 1)
                v.scalar_tensor_tensor(c2[:, :], tf[:, :], 1.0, c2[:, :], ALU.add, ALU.mult)
                v.scalar_tensor_tensor(tg[:, :], ti[:, :], 1.0, tg[:, :], ALU.add, ALU.mult)
                v.drain()
                v.scalar_tensor_tensor(c2[:, :], c2[:, :], 0.5, tg[:, :], ALU.mult, ALU.add).then_inc(s["scan_done"], 1)

            def row_maxima(b, p, par):
                if not has(b, 1):
                    return
                for h in (2 * p, 2 * p + 1):
                    need(dve, "s_full", H1 * (b + 1) + (h + 1))
                    v.tensor_reduce(out=mx[:, :, h], in_=SB[(par + 1 + h) % 3].rearrange("q (i n) -> q i n", i=TT),
                                    axis=mybir.AxisListType.X, op=ALU.max).then_inc(s["max_done"], 1)

            def minus_maxima(half):
                m = mx[:, :, half * H1 // 2:(half + 1) * H1 // 2]
                n = [nmx[:, :, half, k, :] for k in range(NPART)]
                v.drain()
                v.tensor_scalar(n[0], m, -1.0, None, ALU.mult)
                v.drain()
                v.scalar_tensor_tensor(mrest[:, :, :], m, -1.0, n[0], ALU.mult, ALU.subtract)
                v.drain()
                v.tensor_copy(n[1], mrest[:, :, :])
                v.drain()
                v.tensor_tensor(n[2], mrest[:, :, :], n[1], ALU.subtract).then_inc(s["nm_ready"], 1)

            def norm_tiles(b):
                first = 0 if has(b, 3) else TT
                outs = [x2c[:, it, :] for it in range(TT)] if has(b, 3) else []
                return sums[:, first:, :], outs + ([x3c[:, it, :] for it in range(TT)] if has(b, -1) else [])

            def norms_start(b):
                if has(b, 3):
                    need(dve, "comb_done", b + 4)
                if has(b, -1):
                    need_full(dve, b, WO)
                    need(dve, "x2_kept", b)
                    v.tensor_tensor(res2, shared(WO)[:, 0:N].rearrange("q (i d) -> q i d", i=TT), x_all[:, bass.ds((b - 1) * TT, TT), :], ALU.add).then_inc(s["free0"], 1)
                    v.drain()
                x, outs = norm_tiles(b)
                n = len(outs)
                moments(v, x, n, st2, mv2[:, 0], nh2[:, 0, 0:n], ve2[:, 0, 0:n]).then_inc(s["var2_ready"], 1)

            def norms_end(b):
                x, outs = norm_tiles(b)
                n = len(outs)
                need(dve, "pow2_ready", b + 4)
                refine(v, rstd2[:, 0, 0:n], nh2[:, 0, 0:n], u2[:, 0:n])
                if has(b, 3):
                    need(dve, "x2_kept", b + 3)
                if has(b, -1):
                    need(dve, "x3_kept", b)
                else:
                    need(dve, "full1", tally[1].before(b))
                done = [v.tensor_scalar(outs[k], x[:, k, :], mv2[:, 0, k, 0:1], rstd2[:, 0, k:k + 1], ALU.subtract, ALU.mult) for k in range(n)]
                if has(b, 3):
                    done[TT - 1].then_inc(s["x2_ready"], 1)
                if has(b, -1):
                    done[-1].then_inc(s["x3_ready"], 1)

            def attention(b, par):
                for p in range(8):
                    if p == 0 and has(b, 0):
                        minus_maxima(1)
                    if p == 4 and has(b, 1):
                        minus_maxima(0)
                    off, j = quad(b, p)
                    if p % 2 == 1 and has(b, off):
                        use = TOS[(p - 1) // 2]
                        need_full(dve, b, use)
                        o = shared(use)[:, 0:N].rearrange("q (i r c) -> q i r c", i=TT, r=4)
                        v.reciprocal(dinv[:, :, :], o[:, :, :, DH1])
                        v.drain()
                        for it in range(TT):
                            last = v.tensor_tensor(otok[:, it, 32 * j:32 * j + 32].rearrange("q (r c) -> q r c", r=4), o[:, it, :, 0:DH1],
                                                   dinv[:, it, :].rearrange("q (r o) -> q r o", o=1).to_broadcast([128, 4, DH1]), ALU.mult)
                        v.drain().then_inc(s[f"free{use[0]}"], 1)
                    if p == 3 and (has(b, 3) or has(b, -1)):
                        norms_start(b)
                    if p == 4 and (has(b, 3) or has(b, -1)):
                        norms_end(b)
                    if p == 6 and has(b, -2):
                        new_state(b)
                    row_maxima(b, p, par)
                    if p == 1 and has(b, 2):
                        need(dve, "a1_ready", b + 3)
                        v.tensor_tensor(rest[:, :], shared(QK)[:, :], parts[:, 0, :], ALU.subtract).then_inc(s["free0"], 1)
                        v.drain()
                        v.tensor_copy(parts[:, 1, :], rest[:, :])
                        v.drain()
                        v.tensor_tensor(parts[:, 2, :], rest[:, :], parts[:, 1, :], ALU.subtract).then_inc(s["parts_ready"], 1)

            attention_loop(dve, attention)
            dve.wait_ge(s["state_mm"], 1)
            need(dve, "free1", tally[1].before(B + 2))
            v.tensor_tensor(state[:, :, :], SB[0][:, 0:N].rearrange("q (i d) -> q i d", i=TT), bo2[:, :].rearrange("q (o d) -> q o d", o=1).to_broadcast([128, TT, D]), ALU.add)
            v.drain().then_inc(s["state_ready"], 1)
            for c in range(GROUPS - 1):
                xo, xt = group(c)
                v.tensor_tensor(xo, xo, per_batch(state), ALU.add).then_inc(s["h_pre"], 1)

            def squared(c):
                x, h = x_all[:, 8 * c:8 * c + 8, :], xo_all[:, 8 * c:8 * c + 8, :]
                if c < GROUPS - 1:
                    dve.wait_ge(s["h_act"], c + 1)
                    v.tensor_tensor(x, x, h, ALU.add)
                    v.drain()
                else:
                    dve.wait_ge(s["last_sum"], 1)
                moments(v, x, 8, st2, mv2[:, c], nh2[:, c, :], ve2[:, c, :]).then_inc(s["var3_ready"], 1)

            def scales(c):
                dve.wait_ge(s["pow3_ready"], c + 1)
                refine(v, rstd2[:, c, :], nh2[:, c, :], u2[:, :])
                v.scalar_tensor_tensor(shift2[:, c, :], mv2[:, c, :, 0], -1.0, rstd2[:, c, :], ALU.mult, ALU.mult).then_inc(s["scale_ready"], 1)

            dve.wait_ge(s["x3_kept"], B + 1)
            for c in range(GROUPS + 1):
                if c < GROUPS:
                    squared(c)
                if c >= 1:
                    scales(c - 1)


def laid_out(inputs):
    import numpy as np

    def c(v):
        return np.ascontiguousarray(v)

    def g(name):
        return np.asarray(inputs[name])

    def stack_T(layer, names):
        return c(np.stack([g(f"{layer}_{n}").T for n in names], 1))

    r = {}
    r["x"] = c(g("L0_attn_x").reshape(TOK, D))
    r["xT"] = c(r["x"].T)
    for dst, src in (("w1T", "attn_W1"), ("w2T", "attn_W2"), ("wgT", "attn_Wg"), ("keysT", "ffn_keys"), ("rwT", "ffn_rw")):
        r[dst] = c(g("L0_" + src).T)
    bg = g("L0_attn_bg")
    hd = H * DH
    r["colsA"] = c(np.concatenate([g("L0_attn_b1")[:, None], g("L0_attn_b2")[:, None], g("L0_attn_bo")[:, None],
                                   bg[:hd].reshape(PAIRS, 128).T, bg[hd:2 * hd].reshape(PAIRS, 128).T], 1))
    r["bvB"] = c(np.broadcast_to(bg[2 * hd:], (128, hd)))
    r["woT"] = c(g("L0_attn_Wo").T.reshape(PAIRS, 128, D).transpose(1, 0, 2))
    r["rbB"] = c(np.broadcast_to(g("L0_ffn_rb"), (128, E)))
    r["ident"] = np.eye(128, dtype=np.float32)
    w1 = g("L0_ffn_w1").transpose(2, 0, 1)
    b1 = g("L0_ffn_b1").reshape(E, FC, 128).transpose(2, 0, 1)
    w2 = g("L0_ffn_w2").transpose(0, 2, 1).reshape(E, FC, 128, D).transpose(2, 0, 1, 3).reshape(128, E, FC * D)
    b2 = g("L0_ffn_b2").T[:, :, None]
    r["wall"] = c(np.concatenate([w1, b1, w2, b2], 2))
    r["cw"] = stack_T("L1_attn", ("Wq", "Wk", "Wv", "Wo"))
    r["lora_a"] = c(np.stack([g("L1_attn_" + n) for n in ("Aq", "Ak", "Av", "Ao")], 1))
    r["lora_b"] = stack_T("L1_attn", ("Bq", "Bk", "Bv", "Bo"))
    r["gw"] = stack_T("L1_ffn", ("wf", "wi", "wc", "wo"))
    r["gu"] = stack_T("L1_ffn", ("uf", "ui", "uc", "uo"))
    r["gcol"] = c(np.stack([g("L1_ffn_" + n) for n in ("bf", "bi", "bc", "in_c")], 1))
    r["bo1"] = c(np.broadcast_to(g("L1_attn_bo"), (128, D)))
    r["bo2"] = c(np.broadcast_to(g("L1_ffn_bo"), (128, D)))
    return r


def kernel(**inputs):
    import concourse.bacc as bacc
    from concourse import mybir as my
    from concourse.bass_utils import run_bass_kernel_spmd

    arrays = {"in_" + k: v for k, v in laid_out(inputs).items()}
    nc = bacc.Bacc("TRN2", target_bir_lowering=False, num_devices=1)
    t = {k[3:]: nc.dram_tensor(k, v.shape, my.dt.float32, kind="ExternalInput").ap() for k, v in arrays.items()}
    out = nc.dram_tensor("out", (TOK, D), my.dt.float32, kind="ExternalOutput").ap()
    build(nc, t, out)
    r = run_bass_kernel_spmd(nc, [arrays], core_ids=[0])
    return r.results[0]["out"].reshape(B, N, D)
```
